# Optimizing a Trainium2 kernel written in Bass

```python
import numpy as np
import jax
import jax.numpy as jnp

def _softmax(x, axis=-1):
    return jax.nn.softmax(x, axis=axis)

def _gelu(x):
    return jax.nn.gelu(x, approximate=True)

def _silu(x):
    return jax.nn.silu(x)

def _sigmoid(x):
    return jax.nn.sigmoid(x)

def _layernorm(x, axis=-1, eps=1e-05):
    m = jnp.mean(x, axis=axis, keepdims=True)
    v = jnp.var(x, axis=axis, keepdims=True)
    return (x - m) / jnp.sqrt(v + eps)

def _scatter_add(tgt, idx, src, axis=0):
    return tgt.at[idx].add(src)

def _segment_sum(src, seg, n):
    return jax.ops.segment_sum(src, seg, n)
kernel_name = 'mk_decoder_postln_d1_seqx_r4_a7bde1'

def setup_inputs(seed: int=0):
    np.random.seed(seed)
    _w = jnp.asarray

    def _rec_inputs():
        import jax
        import jax.numpy as jnp
        _rk = jax.random.key(seed)
        x = -0.0002928 + 1 * jax.random.normal(jax.random.fold_in(_rk, 1), (16, 100, 256), jnp.float32)
        _lenS = 100 - jax.random.randint(jax.random.fold_in(_rk, 7), (16,), 0, max(1, 100 // 4) + 1, jnp.int32)
        _lenS2 = 361 - jax.random.randint(jax.random.fold_in(_rk, 8), (16,), 0, max(1, 361 // 4) + 1, jnp.int32)
        _ctx_1024P = jax.random.normal(jax.random.fold_in(_rk, 11), (16, 16, 256), jnp.float32)
        _ctx_1024c = jax.random.dirichlet(jax.random.fold_in(_rk, 511), 0.3 * jnp.ones((16,), jnp.float32), (16, 361))
        _ctx_1024t = jnp.einsum('bsk,bkd->bsd', _ctx_1024c, _ctx_1024P)
        _ctx_1024t = _ctx_1024t * jax.lax.rsqrt(jnp.mean(jnp.square(_ctx_1024t)) + 1e-12) * 0.953939
        ctx_1024 = -1.39393e-06 + 0.999914 * (_ctx_1024t + 0.3 * jax.random.normal(jax.random.fold_in(_rk, 611), (16, 361, 256), jnp.float32))
        return (x, ctx_1024)
    x, ctx_1024 = _rec_inputs()

    def _L0_attn_setup():
        import jax, jax.numpy as jnp
        import numpy as np
        H = 8
        SPARSITY = 0.1
        key = jax.random.key(seed)
        ks = jax.random.split(key, 16)
        B, S, D = (2, 512, 256)
        g2 = H * H
        std = 0.02
        inp = {'x': jax.random.normal(ks[0], (B, S, D), dtype=jnp.float32), 'Wq': jax.random.normal(ks[1], (D, D)) * std, 'bq': jnp.zeros((D,)), 'Wk': jax.random.normal(ks[2], (D, D)) * std, 'bk': jnp.zeros((D,)), 'Wv': jax.random.normal(ks[3], (D, D)) * std, 'bv': jnp.zeros((D,)), 'Wo': jax.random.normal(ks[4], (D, D)) * std, 'bo': jnp.zeros((D,)), 'Wd': jax.random.normal(ks[5], (g2, g2)) * std, 'bd': jnp.zeros((g2,)), 'Wg': jax.random.normal(ks[6], (g2, D)) * std, 'bg': jnp.zeros((g2,)), 'Wgp': jax.random.normal(ks[7], (D, g2)) * std, 'bgp': jnp.zeros((D,))}
        return inp
    _L0_attn_all = _L0_attn_setup()
    _L0_attn_in = {k: v for k, v in _L0_attn_all.items() if k in ('Wq', 'bq', 'Wk', 'bk', 'Wv', 'bv', 'Wo', 'bo', 'Wd', 'bd', 'Wg', 'bg', 'Wgp', 'bgp')}
    del _L0_attn_all

    def _L0_xattn_setup():
        import jax, jax.numpy as jnp
        import numpy as np
        MODEL_DIM = 256
        NUM_HEADS = 16
        HEAD_DIM = MODEL_DIM // NUM_HEADS
        SCALE = HEAD_DIM ** (-0.5)
        key = jax.random.key(seed)
        ks = jax.random.split(key, 8)
        B, LQ, LC = (2, 512, 512)
        std = MODEL_DIM ** (-0.5)
        return {'query': jax.random.normal(ks[0], (B, LQ, MODEL_DIM), jnp.float32), 'context': jax.random.normal(ks[1], (B, LC, MODEL_DIM), jnp.float32), 'Wq': jax.random.normal(ks[2], (MODEL_DIM, MODEL_DIM), jnp.float32) * std, 'bq': jnp.zeros((MODEL_DIM,), jnp.float32), 'Wkv': jax.random.normal(ks[3], (MODEL_DIM, 2 * MODEL_DIM), jnp.float32) * std, 'bkv': jnp.zeros((2 * MODEL_DIM,), jnp.float32), 'Wout': jax.random.normal(ks[4], (MODEL_DIM, MODEL_DIM), jnp.float32) * std, 'bout': jnp.zeros((MODEL_DIM,), jnp.float32)}
    _L0_xattn_all = _L0_xattn_setup()
    _L0_xattn_in = {k: v for k, v in _L0_xattn_all.items() if k in ('Wq', 'bq', 'Wkv', 'bkv', 'Wout', 'bout')}
    del _L0_xattn_all

    def _L0_ffn_setup():
        import jax, jax.numpy as jnp
        import numpy as np
        DIM = 256

        def _reference_tuple_inner(x, W_r, W_k, W_v, mu_r, mu_k):
            B, T, C = x.shape
            x_prev = jnp.concatenate([jnp.zeros((B, 1, C), x.dtype), x[:, :-1, :]], axis=1)
            xr = mu_r * x + (1.0 - mu_r) * x_prev
            xk = mu_k * x + (1.0 - mu_k) * x_prev
            r = jax.nn.sigmoid(jnp.einsum('btc,dc->btd', xr, W_r))
            k = jnp.einsum('btc,dc->btd', xk, W_k)
            k_act = jnp.square(jax.nn.relu(k))
            out = r * jnp.einsum('btc,dc->btd', k_act, W_v)
            new_state = x[:, -1, :]
            return (out, new_state)
        key = jax.random.key(seed)
        ks = jax.random.split(key, 6)
        B, T, C = (8, 512, DIM)
        x = jax.random.normal(ks[0], (B, T, C), dtype=jnp.float32)
        s = 1.0 / np.sqrt(C)
        W_r = jax.random.uniform(ks[1], (C, C), jnp.float32, -s, s)
        W_k = jax.random.uniform(ks[2], (C, C), jnp.float32, -s, s)
        W_v = jax.random.uniform(ks[3], (C, C), jnp.float32, -s, s)
        mu_r = jax.random.uniform(ks[4], (C,), jnp.float32)
        mu_k = jax.random.uniform(ks[5], (C,), jnp.float32)
        return {'x': x, 'W_r': W_r, 'W_k': W_k, 'W_v': W_v, 'mu_r': mu_r, 'mu_k': mu_k}
    _L0_ffn_all = _L0_ffn_setup()
    _L0_ffn_in = {k: v for k, v in _L0_ffn_all.items() if k in ('W_r', 'W_k', 'W_v', 'mu_r', 'mu_k')}
    del _L0_ffn_all
    return {'x': x, 'ctx_1024': ctx_1024, 'L0_attn_Wq': _L0_attn_in['Wq'], 'L0_attn_bq': _L0_attn_in['bq'], 'L0_attn_Wk': _L0_attn_in['Wk'], 'L0_attn_bk': _L0_attn_in['bk'], 'L0_attn_Wv': _L0_attn_in['Wv'], 'L0_attn_bv': _L0_attn_in['bv'], 'L0_attn_Wo': _L0_attn_in['Wo'], 'L0_attn_bo': _L0_attn_in['bo'], 'L0_attn_Wd': _L0_attn_in['Wd'], 'L0_attn_bd': _L0_attn_in['bd'], 'L0_attn_Wg': _L0_attn_in['Wg'], 'L0_attn_bg': _L0_attn_in['bg'], 'L0_attn_Wgp': _L0_attn_in['Wgp'], 'L0_attn_bgp': _L0_attn_in['bgp'], 'L0_xattn_Wq': _L0_xattn_in['Wq'], 'L0_xattn_bq': _L0_xattn_in['bq'], 'L0_xattn_Wkv': _L0_xattn_in['Wkv'], 'L0_xattn_bkv': _L0_xattn_in['bkv'], 'L0_xattn_Wout': _L0_xattn_in['Wout'], 'L0_xattn_bout': _L0_xattn_in['bout'], 'L0_ffn_W_r': _L0_ffn_in['W_r'], 'L0_ffn_W_k': _L0_ffn_in['W_k'], 'L0_ffn_W_v': _L0_ffn_in['W_v'], 'L0_ffn_mu_r': _L0_ffn_in['mu_r'], 'L0_ffn_mu_k': _L0_ffn_in['mu_k']}

def reference(x, ctx_1024, L0_attn_Wq, L0_attn_bq, L0_attn_Wk, L0_attn_bk, L0_attn_Wv, L0_attn_bv, L0_attn_Wo, L0_attn_bo, L0_attn_Wd, L0_attn_bd, L0_attn_Wg, L0_attn_bg, L0_attn_Wgp, L0_attn_bgp, L0_xattn_Wq, L0_xattn_bq, L0_xattn_Wkv, L0_xattn_bkv, L0_xattn_Wout, L0_xattn_bout, L0_ffn_W_r, L0_ffn_W_k, L0_ffn_W_v, L0_ffn_mu_r, L0_ffn_mu_k):
    import jax
    import jax.numpy as jnp

    def _L0_attn_ref(x, Wq, bq, Wk, bk, Wv, bv, Wo, bo, Wd, bd, Wg, bg, Wgp, bgp):
        import jax, jax.numpy as jnp
        import numpy as np
        H = 8
        SPARSITY = 0.1
        B, S, D = x.shape
        Dh = D // H
        scale = Dh ** (-0.5)
        k = max(int(S * SPARSITY), 1)

        def heads(W, b):
            return (x @ W.T + b).reshape(B, S, H, Dh).transpose(0, 2, 1, 3)
        Q, K, V = (heads(Wq, bq), heads(Wk, bk), heads(Wv, bv))
        scores = jnp.einsum('bhqd,bhkd->bhqk', Q, K) * scale
        thr = jax.lax.top_k(scores, k)[0][..., k - 1:k]
        masked = jnp.where(scores >= thr, scores, -jnp.inf)
        probs = jax.nn.softmax(masked, axis=-1)
        attn = jnp.einsum('bhqk,bhkd->bhqd', probs, V)
        attn = attn.transpose(0, 2, 1, 3).reshape(B, S, D)
        g2 = H * H
        distilled = (attn.reshape(-1, g2) @ Wd.T + bd).reshape(B, S, D)
        gate = jax.nn.sigmoid(x.mean(axis=1) @ Wg.T + bg)
        gate = (gate @ Wgp.T + bgp)[:, None, :]
        mixed = gate * distilled + (1.0 - gate) * attn
        return mixed @ Wo.T + bo

    def _L0_xattn_ref(query, context, Wq, bq, Wkv, bkv, Wout, bout):
        import jax, jax.numpy as jnp
        import numpy as np
        MODEL_DIM = 256
        NUM_HEADS = 16
        HEAD_DIM = MODEL_DIM // NUM_HEADS
        SCALE = HEAD_DIM ** (-0.5)
        B, LQ, _ = query.shape
        LC = context.shape[1]
        H, D = (NUM_HEADS, HEAD_DIM)
        q = query @ Wq + bq
        kv = context @ Wkv + bkv
        kv = kv.reshape(B, LC, H, D, 2)
        k = jnp.transpose(kv[..., 0], (0, 2, 1, 3))
        v = jnp.transpose(kv[..., 1], (0, 2, 1, 3))
        q = jnp.transpose(q.reshape(B, LQ, H, D), (0, 2, 1, 3))
        scores = jnp.einsum('bhid,bhjd->bhij', q, k) * SCALE
        attn = jax.nn.softmax(scores, axis=-1)
        out = jnp.einsum('bhij,bhjd->bhid', attn, v)
        out = jnp.transpose(out, (0, 2, 1, 3)).reshape(B, LQ, H * D)
        return out @ Wout + bout

    def _L0_ffn_ref(x, W_r, W_k, W_v, mu_r, mu_k):
        import jax, jax.numpy as jnp
        import numpy as np
        DIM = 256

        def _reference_tuple_inner(x, W_r, W_k, W_v, mu_r, mu_k):
            B, T, C = x.shape
            x_prev = jnp.concatenate([jnp.zeros((B, 1, C), x.dtype), x[:, :-1, :]], axis=1)
            xr = mu_r * x + (1.0 - mu_r) * x_prev
            xk = mu_k * x + (1.0 - mu_k) * x_prev
            r = jax.nn.sigmoid(jnp.einsum('btc,dc->btd', xr, W_r))
            k = jnp.einsum('btc,dc->btd', xk, W_k)
            k_act = jnp.square(jax.nn.relu(k))
            out = r * jnp.einsum('btc,dc->btd', k_act, W_v)
            new_state = x[:, -1, :]
            return (out, new_state)
        return _reference_tuple_inner(x, W_r, W_k, W_v, mu_r, mu_k)[0]
    x = _layernorm(x + _L0_attn_ref(x, L0_attn_Wq, L0_attn_bq, L0_attn_Wk, L0_attn_bk, L0_attn_Wv, L0_attn_bv, L0_attn_Wo, L0_attn_bo, L0_attn_Wd, L0_attn_bd, L0_attn_Wg, L0_attn_bg, L0_attn_Wgp, L0_attn_bgp), axis=-1)
    x = _layernorm(x + _L0_xattn_ref(x, ctx_1024, L0_xattn_Wq, L0_xattn_bq, L0_xattn_Wkv, L0_xattn_bkv, L0_xattn_Wout, L0_xattn_bout), axis=-1)
    x = _layernorm(x + _L0_ffn_ref(x, L0_ffn_W_r, L0_ffn_W_k, L0_ffn_W_v, L0_ffn_mu_r, L0_ffn_mu_k), axis=-1)
    return x

_drawn_inputs = setup_inputs


def setup_inputs(seed=0):
    import zlib

    import numpy as np

    out = dict(_drawn_inputs(seed))
    spreads = {'L0_attn_bq': (0.0, 0.432),
     'L0_attn_bk': (0.0, 2.0),
     'L0_attn_bv': (0.0, 0.287),
     'L0_attn_bo': (0.0, 0.1),
     'L0_attn_bd': (0.0, 0.8),
     'L0_attn_bg': (0.0, 0.8),
     'L0_attn_bgp': (0.0, 0.8),
     'L0_xattn_bq': (0.0, 0.402),
     'L0_xattn_bkv': (0.0, 0.1),
     'L0_xattn_bout': (0.0, 0.1)}
    factors = {'L0_attn_Wd': 8.0, 'L0_attn_Wg': 28.433, 'L0_attn_Wgp': 8.0, 'L0_ffn_mu_r': 6.393}
    for name, (base, spread) in spreads.items():
        noise = np.random.default_rng([zlib.crc32(name.encode()), seed]).standard_normal(out[name].shape)
        drawn = base * np.exp(spread * noise) if base else spread * noise
        out[name] = jnp.asarray(drawn.astype(out[name].dtype))
    for name, factor in factors.items():
        out[name] = (out[name] * factor).astype(out[name].dtype)
    return out
```

```python
import concourse.bass as bass
from concourse import mybir
from contextlib import ExitStack

F32 = mybir.dt.float32
F32R = mybir.dt.float32r
ACT = mybir.ActivationFunctionType
ALU = mybir.AluOpType
AX = mybir.AxisListType

B, S, D, SC = 16, 100, 256, 361
P = 128
C = D // P
SCP = SC + 1
H1, DH1 = 8, 32
HC1 = P // DH1
TOPK = max(int(S * 0.1), 1)
GATE = H1 * H1
H2, DH2 = 16, 16
NG = H2 // 2
KC = [(0, 128), (128, 128), (256, SC - 256)]
VW = 32
STACK = 3 * C
EPS = 1e-5
SCALE1 = float(DH1) ** -0.5
SCALE2 = float(DH2) ** -0.5
QSW = NG * 2 * S + 56
UNITS = 6
NPT = 3
SLOTS = 6
W_NAMES = ["q1", "k1", "v1", "o1", "q2", "k2", "v2", "o2", "r", "k", "v"]
VEC = {n: i for i, n in enumerate(
    ["bq1_0", "bq1_1", "bk1_0", "bk1_1", "bq2_0", "bq2_1", "bk2_0", "bk2_1",
     "mur_0", "mur_1", "muk_0", "muk_1", "bgp_0", "bgp_1", "bd", "bg"])}
NVEC = len(VEC)
ROWS = ["bv1", "bo1", "bv2", "bo2"]


def decoder_layer(nc, x, xT, ctxT, wpack, vecs, rows, wd, wg, wgp, consts, out):
    es = ExitStack()
    with es:
        def sb(name, shape, dt=F32):
            return es.enter_context(nc.sbuf_tensor(name, shape, dt))

        def sem(name):
            return es.enter_context(nc.semaphore(name))

        def two(make, name, *a):
            return [make(f"{name}{i}", *a) for i in range(2)]

        bank = [es.enter_context(nc.psum_tensor(f"bank{i}", [P, 512], F32)) for i in range(8)]

        w = sb("w", [P, len(W_NAMES), C, D])
        W = {n: w[:, i] for i, n in enumerate(W_NAMES)}
        vec = sb("vec", [P, NVEC])
        wd_sb = sb("wd_sb", [P, P])
        wg_sb = sb("wg_sb", [P, C, GATE])
        wgp_sb = sb("wgp_sb", [GATE, D])
        cst = sb("cst", [P, P + HC1 + 2])
        ident = cst[:, 0:P]
        quad_mask = cst[:, P:P + HC1]
        pair_mask = cst[:, P + HC1:P + HC1 + 2]
        row_sb = sb("row_sb", [1, 4 * D])
        ones_row = sb("ones_row", [1, P])
        rowb = sb("rowb", [P, 4, D])
        ROW = {n: rowb[:, i] for i, n in enumerate(ROWS)}
        mhalf = sb("mhalf", [P, 1])
        wkh, wkl, wvh, wvl = (sb(n, [P, C, D], F32R) for n in ("wkh", "wkl", "wvh", "wvl"))

        def v(name):
            return vec[:, VEC[name]:VEC[name] + 1]

        xT_all = sb("xT_all", [P, C, B * S])
        x1_all = sb("x1_all", [S, B * D])
        x1T_all = xT_all
        xsum = sb("xsum", [P, C, B])
        hbg = sb("hbg", [GATE, 1])
        g1 = sb("g1", [GATE, B])
        g1s = sb("g1s", [GATE, B])
        gate_all = sb("gate_all", [P, C, B])

        xTb = two(sb, "xTb", [P, C, S])
        xin = two(sb, "xin", [S, D])
        gb = two(sb, "gb", [P, C])
        qs = sb("qs", [P, C, S])
        kt = sb("kt", [P, C, S])
        kbd = sb("kbd", [P, C, HC1, S])
        v1 = two(sb, "v1", [S, D])
        s_sb = two(sb, "s_sb", [S, H1, S])
        rest = sb("rest", [S, H1, S])
        top1 = sb("top1", [S, H1, 8])
        top2 = sb("top2", [S, H1, 8])
        negm1 = sb("negm1", [S, H1])
        e1 = sb("e1", [S, H1, S])
        p1 = two(sb, "p1", [S, H1, S])
        den1 = sb("den1", [S, H1])
        rden1 = two(sb, "rden1", [S, H1])
        pT1 = sb("pT1", [S, H1, S])
        aT = sb("aT", [P, C, S])
        dmix = sb("dmix", [P, C, S])
        mixT = sb("mixT", [P, C, S])
        xbo = two(sb, "xbo", [S, D])
        y1 = sb("y1", [S, D])
        x1b = sb("x1b", [S, D])
        st = sb("st", [S, 6])
        mv = sb("mv", [S, 2])
        ve = sb("ve", [S, 1])
        rstd = sb("rstd", [S, 1])

        ctxf = two(sb, "ctxf", [P, C, SCP])
        ctxh = sb("ctxh", [P, C, SCP], F32R)
        ctxl = sb("ctxl", [P, C, SCP], F32R)
        kh = sb("kh", [P, C, SCP], F32R)
        kl = sb("kl", [P, C, SCP], F32R)
        ks = two(sb, "ks", [P, NG, SCP], F32R)
        qf = sb("qf", [P, C, S])
        qm = sb("qm", [P, C, 2, S])
        qh = sb("qh", [P, C, 2, S], F32R)
        ql = sb("ql", [P, C, 2, S], F32R)
        qst = two(sb, "qst", [P, QSW], F32R)
        vx = two(sb, "vx", [P, len(KC), H2, VW])
        m2 = two(sb, "m2", [S, H2])
        mrow = two(sb, "mrow", [H2 // 2, S], F32R)
        pe2 = sb("pe2", [P, SLOTS, 2, 2 * S])
        oT = sb("oT", [P, 4, S])
        rden2 = sb("rden2", [S, H2])
        att = sb("att", [S, H2, DH2])
        attT = sb("attT", [P, C, S])
        xres = sb("xres", [S, D])
        y2 = sb("y2", [S, D])
        x2 = sb("x2", [S, D])
        x2T = sb("x2T", [P, C, 1 + S])
        dx = sb("dx", [P, C, S])
        xr = sb("xr", [P, C, S])
        xk = sb("xk", [P, C, S])
        th = sb("th", [S, D])
        sg = sb("sg", [S, D])
        kr = sb("kr", [P, C, S])
        ka = sb("ka", [P, C, S])
        rv = sb("rv", [S, D])
        y3 = sb("y3", [S, D])
        x3 = two(sb, "x3", [S, D])

        carried = sem("carried")
        w_in = sem("w_in")
        xT_in = sem("xT_in")
        x_in = two(sem, "x_in")
        ones_ok = sem("ones_ok")
        rows_ps = sem("rows_ps")
        rows_ok = sem("rows_ok")
        xsum_ok = sem("xsum_ok")
        gate_ps = sem("gate_ps")
        gate_t = sem("gate_t")
        gate_u = sem("gate_u")
        gate_ps2 = sem("gate_ps2")
        gate_ok = sem("gate_ok")
        wsplit = sem("wsplit")
        hbg_ok = sem("hbg_ok")
        zeroed = sem("zeroed")
        xTb_ok = sem("xTb_ok")
        gb_ok = sem("gb_ok")
        qk_ps, v_ps = sem("qk_ps"), sem("v_ps")
        qk_sb = sem("qk_sb")
        v_sb = sem("v_sb")
        kbd_ok = sem("kbd_ok")
        s_ps = sem("s_ps")
        s_ok = sem("s_ok")
        top1_ok, negm_ok, rest_ok, top2_ok = (sem(n) for n in ("top1_ok", "negm_ok", "rest_ok", "top2_ok"))
        e1_ok, p1_ok, rden1_ok, pn_ok = (sem(n) for n in ("e1_ok", "p1_ok", "rden1_ok", "pn_ok"))
        pT_ps, pT_sb = sem("pT_ps"), sem("pT_sb")
        aT_ps, aT_sb = sem("aT_ps"), sem("aT_sb")
        d_ps, dmix_ok, mix_ok = sem("d_ps"), sem("dmix_ok"), sem("mix_ok")
        y1_ps, xbo_ok = sem("y1_ps"), sem("xbo_ok")
        ln1, ve1, rstd1 = sem("ln1"), sem("ve1"), sem("rstd1")
        x1T_ps, x1T_sb = sem("x1T_ps"), sem("x1T_sb")

        ctx_in = two(sem, "ctx_in")
        ctxh_ok, ctxl_ok = sem("ctxh_ok"), sem("ctxl_ok")
        k_ps, v2_ps = sem("k_ps"), sem("v2_ps")
        kh_ok, kl_ok, v2_sb = sem("kh_ok"), sem("kl_ok"), sem("v2_sb")
        ks_in = two(sem, "ks_in")
        q_ps, qf_ok, qm_ok, qh_ok, ql_ok = (sem(n) for n in ("q_ps", "qf_ok", "qm_ok", "qh_ok", "ql_ok"))
        qs_in = two(sem, "qs_in")
        max_ps, max_ok = sem("max_ps"), sem("max_ok")
        mT_ps, mrow_ok = sem("mT_ps"), sem("mrow_ok")
        m_in = [sem("m_in0"), sem("m_in1")]
        t_ps, exp_ok, pv_ok = sem("t_ps"), sem("exp_ok"), sem("pv_ok")
        oT_ok = sem("oT_ok")
        ot_ps, rden2_ok, att_ok = sem("ot_ps"), sem("rden2_ok"), sem("att_ok")
        at_ps, attT_ok = sem("at_ps"), sem("attT_ok")
        y2_ps, xres_ok = sem("y2_ps"), sem("xres_ok")
        ln2, ve2, rstd2 = sem("ln2"), sem("ve2"), sem("rstd2")
        x2T_ps, x2T_ok, dx_ok, xrk_ok = (sem(n) for n in ("x2T_ps", "x2T_ok", "dx_ok", "xrk_ok"))
        r_ps, th_ok, sg_ok, rv_ok = sem("r_ps"), sem("th_ok"), sem("sg_ok"), sem("rv_ok")
        kf_ps, kr_ok, ka_ok, f_ps = sem("kf_ps"), sem("kr_ok"), sem("ka_ok"), sem("f_ps")
        ln3, ve3, rstd3 = sem("ln3"), sem("ve3"), sem("rstd3")
        out_done = two(sem, "out_done")

        b_s = bank[0:2]
        b_qk, b_v, b_pT, b_aT, b_d, b_y = bank[2:8]
        b_max = bank[0:2]
        b_t = bank[2:5]
        b_o = bank[5]
        b_m = bank[6:8]

        N_W = 7

        def carry(eng):
            eng.sem_inc(carried, 1)

        block = es.enter_context(nc.Block())

        @block.sync
        def _(sp):
            sp.dma_start(xT_all[:], xT).then_inc(xT_in, 16)
            sp.dma_start(cst[:], consts).then_inc(w_in, 16)
            sp.dma_start(vec[:], vecs).then_inc(w_in, 16)
            sp.dma_start(row_sb[:], rows).then_inc(w_in, 16)
            sp.dma_start(wg_sb[:], wg).then_inc(w_in, 16)
            sp.dma_start(wgp_sb[:], wgp).then_inc(w_in, 16)
            sp.dma_start(wd_sb[:], wd).then_inc(w_in, 16)
            sp.dma_start(w[:], wpack).then_inc(w_in, 16)

            def load_x(b, par, reused):
                if reused:
                    sp.wait_ge(xbo_ok, b - 1)
                    carry(sp)
                sp.dma_start(xin[par][:], x[bass.ds(b, 1)].rearrange("a s d -> (a s) d")).then_inc(x_in[par], 16)

            load_x(0, 0, False)
            load_x(1, 1, False)
            sp.dma_start(ctxf[0][:], ctxT[0]).then_inc(ctx_in[0], 16)
            sp.dma_start(ctxf[1][:], ctxT[1]).then_inc(ctx_in[1], 16)
            with sp.Fori(0, (B - 2) // 2) as i:
                for par in range(2):
                    load_x(2 * i + 2 + par, par, True)

            def stack_k(b, par, free):
                if free:
                    sp.wait_ge(pv_ok, 2 * UNITS * (b - 1))
                    carry(sp)
                for c in range(C):
                    sp.wait_ge(kl_ok, C * b + c + 1)
                    carry(sp)
                    for copy, src in enumerate((kh, kh, kl)):
                        sp.dma_start(ks[par][32 * copy:32 * copy + 32, 4 * c:4 * c + 4, :].bitcast(F32),
                                     src[:, c, :].bitcast(F32)).then_inc(ks_in[par], 16)

            def stack_q(b, par, free):
                if free:
                    sp.wait_ge(pv_ok, 2 * UNITS * (b - 1))
                    carry(sp)
                sp.wait_ge(ql_ok, b + 1)
                carry(sp)
                qv = qst[par][:, 0:NG * 2 * S].bitcast(F32).rearrange("p (c j q) -> p c j q", c=C, j=4)
                for c in range(C):
                    for copy, src in enumerate((qh, ql, qh)):
                        sp.dma_start(qv[32 * copy:32 * copy + 32, c],
                                     src[:, c].bitcast(F32).rearrange("p t q -> p (t q)")).then_inc(qs_in[par], 16)

            def max_row(b, par, half):
                sp.wait_ge(mrow_ok, 2 * b + half + 1)
                carry(sp)
                sp.dma_start(qst[par][96:97, half * 8 * S:(half + 1) * 8 * S].bitcast(F32)
                             .rearrange("p (h q) -> p h q", h=8), mrow[half][:].bitcast(F32)).then_inc(m_in[half], 16)

            def store(b, par):
                sp.wait_ge(ln3, 4 * (b + 1))
                carry(sp)
                sp.dma_start(out[bass.ds(b, 1)].rearrange("a s d -> (a s) d"), x3[par][:]).then_inc(out_done[par], 16)

            def load_ctx(b, par):
                sp.wait_ge(ctxl_ok, b - 1)
                carry(sp)
                sp.dma_start(ctxf[par][:], ctxT[bass.ds(b, 1)].rearrange("a p c s -> (a p) c s")
                             ).then_inc(ctx_in[par], 16)

            def window(b, par, prev2=True, nxt=True, nxt3=True):
                reused = not (isinstance(b, int) and b == 0)
                max_row(b, par, 0)
                if nxt:
                    stack_k(b + 1, 1 - par, reused)
                if prev2:
                    store(b - 2, par)
                if nxt:
                    stack_q(b + 1, 1 - par, reused)
                max_row(b, par, 1)
                if nxt3:
                    load_ctx(b + 3, 1 - par)

            sp.wait_ge(zeroed, 2)
            stack_k(0, 0, False)
            stack_q(0, 0, False)
            load_ctx(2, 0)
            window(0, 0, prev2=False)
            window(1, 1, prev2=False)
            with sp.Fori(0, (B - 6) // 2) as i:
                for k in range(2):
                    window(2 * i + 2 + k, k)
            window(B - 4, 0)
            window(B - 3, 1, nxt3=False)
            window(B - 2, 0, nxt3=False)
            window(B - 1, 1, nxt=False, nxt3=False)
            store(B - 2, 0)
            store(B - 1, 1)
            sp.wait_ge(out_done[0], 16 * B // 2)
            sp.wait_ge(out_done[1], 16 * B // 2)

        @block.gpsimd
        def _(pool):
            pool.memset(ones_row[:], 1.0).then_inc(ones_ok, 1)
            pool.memset(mhalf[:], -0.5)

            def fetch_x(b, par, first):
                if first:
                    pool.wait_ge(xT_in, 16)
                else:
                    pool.wait_ge(v_ps, b - 1)
                pool.tensor_copy(xTb[par][:], xT_all[:, :, bass.ds(b * S, S)]).then_inc(xTb_ok, 1)

            def prepare_x(b, par, first):
                pool.wait_ge(x_in[par], 16 * (b // 2) + 16 if isinstance(b, int) else 8 * (b - par) + 16)
                if not first:
                    pool.wait_ge(ln1, 4 * (b - 2) + 1)
                pool.wait_ge(rows_ok, 2)
                pool.tensor_tensor(xbo[par][:], xin[par][:], ROW["bo1"][0:S], ALU.add).then_inc(xbo_ok, 1)
                if not first:
                    pool.wait_ge(mix_ok, b - 1)
                pool.wait_ge(gate_ok, C)
                pool.tensor_copy(gb[par][:], gate_all[:, :, bass.ds(b, 1)].rearrange("p c a -> p (c a)")
                                 ).then_inc(gb_ok, 1)

            def spread_keys(b, first):
                pool.wait_ge(qk_sb, 2 * C * (b + 1))
                if not first:
                    pool.wait_ge(s_ps, b)
                for c in range(C):
                    last = pool.tensor_tensor(kbd[:, c], kt[:, c:c + 1, :].broadcast_to([P, HC1, S]),
                                              quad_mask.rearrange("p (j a) -> p j a", a=1).broadcast_to([P, HC1, S]),
                                              ALU.mult)
                last.then_inc(kbd_ok, 1)

            def inv_std(n, ln, at, ve_s, rstd_s):
                pool.wait_ge(ln, at)
                carry(pool)
                pool.tensor_scalar(ve[:], mv[:, 1:2], EPS, None, ALU.add).then_inc(ve_s, 1)
                pool.wait_ge(ve_s, n + 1)
                pool.tensor_tensor(rstd[:], ve[:], mhalf[0:S], ALU.pow).then_inc(rstd_s, 1)

            def normalise(b, par):
                pool.wait_ge(rden1_ok, b + 1)
                pool.tensor_tensor(p1[par][:], p1[par][:],
                                   rden1[par][:].rearrange("p (h a) -> p h a", a=1).broadcast_to([S, H1, S]),
                                   ALU.mult).then_inc(pn_ok, 1)

            def s_window(b, par, prev=True, nxt=True):
                if nxt:
                    spread_keys(b + 1, False)
                if prev:
                    inv_std(b - 1, ln1, 4 * (b - 1) + 3, ve1, rstd1)
                normalise(b, par)
                if nxt:
                    prepare_x(b + 1, 1 - par, isinstance(b, int) and b == 0)

            fetch_x(0, 0, True)
            fetch_x(1, 1, True)
            prepare_x(0, 0, True)
            spread_keys(0, True)

            def s_full(b, par):
                s_window(b, par)
                fetch_x(b + 2, par, False)
            s_window(0, 0, prev=False)
            fetch_x(2, 0, False)
            with pool.Fori(0, (B - 4) // 2) as i:
                for k in range(2):
                    s_full(2 * i + 1 + k, (1 + k) % 2)
            s_full(B - 3, 1)
            s_window(B - 2, 0)
            s_window(B - 1, 1, nxt=False)
            inv_std(B - 1, ln1, 4 * (B - 1) + 3, ve1, rstd1)

            def ctx_low(b, par, first):
                pool.wait_ge(ctxh_ok, b + 1)
                pool.tensor_tensor(ctxl[:], ctxf[par][:], ctxh[:].bitcast(F32), ALU.subtract).then_inc(ctxl_ok, 1)

            def q_split(b, first):
                pool.wait_ge(qf_ok, b + 1)
                if not first:
                    pool.wait_ge(ql_ok, b)
                    pool.wait_ge(qh_ok, b)
                for c in range(C):
                    last = pool.tensor_tensor(qm[:, c], qf[:, c:c + 1, :].broadcast_to([P, 2, S]),
                                              pair_mask.rearrange("p (t a) -> p t a", a=1).broadcast_to([P, 2, S]),
                                              ALU.mult)
                last.then_inc(qm_ok, 1)
                pool.wait_ge(qm_ok, b + 1)
                pool.wait_ge(qh_ok, b + 1)
                pool.tensor_tensor(ql[:], qm[:], qh[:].bitcast(F32), ALU.subtract).then_inc(ql_ok, 1)

            def residual2(b, first):
                if not first:
                    pool.wait_ge(ln2, 4 * (b - 1) + 1)
                pool.tensor_tensor(xres[:], x1_all[:, bass.ds(b * D, D)], ROW["bo2"][0:S], ALU.add
                                   ).then_inc(xres_ok, 1)

            def x_window(b, par, prev=True, prev2=True, nxt=True, nxt2=True):
                if prev2:
                    n = b - 2
                    pool.wait_ge(x2T_ok, n + 1)
                    pool.wait_ge(xrk_ok, n) if not (isinstance(b, int) and b == 2) else None
                    pool.tensor_tensor(dx[:], x2T[:, :, 1:1 + S], x2T[:, :, 0:S], ALU.subtract).then_inc(dx_ok, 1)
                    pool.wait_ge(kr_ok, n + 1)
                    pool.tensor_tensor(ka[:], kr[:], kr[:], ALU.mult).then_inc(ka_ok, 1)
                    inv_std(n, ln3, 4 * n + 3, ve3, rstd3)
                if nxt:
                    q_split(b + 1, False)
                if prev:
                    residual2(b - 1, isinstance(b, int) and b == 1)
                    inv_std(b - 1, ln2, 4 * (b - 1) + 3, ve2, rstd2)
                if nxt2:
                    ctx_low(b + 2, par, False)

            def x_tail(n):
                pool.wait_ge(x2T_ok, n + 1)
                pool.wait_ge(xrk_ok, n)
                pool.tensor_tensor(dx[:], x2T[:, :, 1:1 + S], x2T[:, :, 0:S], ALU.subtract).then_inc(dx_ok, 1)
                pool.wait_ge(kr_ok, n + 1)
                pool.tensor_tensor(ka[:], kr[:], kr[:], ALU.mult).then_inc(ka_ok, 1)
                inv_std(n, ln3, 4 * n + 3, ve3, rstd3)

            pool.wait_ge(ln1, 4 * B)
            ctx_low(0, 0, True)
            q_split(0, True)
            ctx_low(1, 1, False)
            x_window(0, 0, prev=False, prev2=False)
            x_window(1, 1, prev2=False)
            x_window(2, 0)
            x_window(3, 1)
            with pool.Fori(0, (B - 6) // 2) as i:
                for k in range(2):
                    x_window(2 * i + 4 + k, k)
            x_window(B - 2, 0, nxt2=False)
            x_window(B - 1, 1, nxt=False, nxt2=False)
            residual2(B - 1, False)
            x_tail(B - 2)
            inv_std(B - 1, ln2, 4 * (B - 1) + 3, ve2, rstd2)
            x_tail(B - 1)

        @block.scalar
        def _(act):
            act.wait_ge(w_in, 16 * N_W)
            act.activation(hbg[:], vec[0:GATE, VEC["bg"]:VEC["bg"] + 1], ACT.Copy, scale=0.5).then_inc(hbg_ok, 1)
            for k in range(2):
                act.wait_ge(rows_ps, k + 1)
                act.activation(rowb[:, 2 * k:2 * k + 2].rearrange("p r d -> p (r d)"), bank[k][:, :], ACT.Copy
                               ).then_inc(rows_ok, 1)
            act.wait_ge(gate_ps, 1)
            act.wait_ge(hbg_ok, 1)
            act.activation(g1[:], bank[2][0:GATE, 0:B], ACT.Tanh, bias=hbg[:], scale=0.5 / S).then_inc(gate_t, 1)
            act.wait_ge(gate_ps2, 1)
            for c in range(C):
                act.activation(gate_all[:, c], bank[3][:, c * B:(c + 1) * B], ACT.Identity, bias=v(f"bgp_{c}")
                               ).then_inc(gate_ok, 1)

            def evac_qk(b, first):
                act.wait_ge(qk_ps, b + 1)
                if not first:
                    act.wait_ge(s_ps, b)
                    act.wait_ge(kbd_ok, b)
                for n, (dst, name) in enumerate(((qs, "bq1"), (kt, "bk1"))):
                    for c in range(C):
                        k = (n * C + c) * S
                        act.activation(dst[:, c], b_qk[:, k:k + S], ACT.Identity, bias=v(f"{name}_{c}")
                                       ).then_inc(qk_sb, 1)

            def evac_scores(b, par, first):
                for c in range(C):
                    act.wait_ge(s_ps, b + 1)
                    if not first:
                        act.wait_ge(p1_ok, b - 1)
                    act.activation(s_sb[par][:, HC1 * c:HC1 * c + HC1].rearrange("p h k -> p (h k)"),
                                   b_s[c][0:S, 0:HC1 * S], ACT.Copy).then_inc(s_ok, 1)

            def exps1(b, par, heads, first):
                act.wait_ge(negm_ok, b + 1)
                if not first:
                    act.wait_ge(p1_ok, b)
                for h in heads:
                    act.activation(e1[:, h], s_sb[par][:, h], ACT.Exp, bias=negm1[:, h:h + 1], scale=SCALE1
                                   ).then_inc(e1_ok, 1)

            def evac_pT(b, k, first):
                act.wait_ge(pT_ps, 2 * b + k + 1)
                if not first:
                    act.wait_ge(aT_ps, b)
                act.activation(pT1[:, HC1 * k:HC1 * k + HC1].rearrange("p h k -> p (h k)"),
                               b_pT[0:S, 0:HC1 * S], ACT.Copy).then_inc(pT_sb, 1)

            def evac_aT(b, first):
                act.wait_ge(aT_ps, b + 1)
                if not first:
                    act.wait_ge(mix_ok, b)
                act.activation(aT[:].rearrange("p c q -> p (c q)"), b_aT[:, 0:C * S], ACT.Copy).then_inc(aT_sb, 1)

            def evac_x1T(b):
                act.wait_ge(x1T_ps, b + 1)
                act.activation(x1T_all[:, :, bass.ds(b * S, S)], b_aT[:, 0:C * S].rearrange("p (c q) -> p c q", c=C),
                               ACT.Copy).then_inc(x1T_sb, 1)

            def s_window(b, par, prev=True, prev_first=False, nxt=True, first=False):
                if prev:
                    evac_pT(b - 1, 0, prev_first)
                    evac_pT(b - 1, 1, prev_first)
                exps1(b, par, range(H1), first)
                if nxt:
                    evac_qk(b + 1, False)
                if prev:
                    evac_aT(b - 1, prev_first)
                if nxt:
                    evac_scores(b + 1, 1 - par, isinstance(b, int) and b == 0)
                if prev:
                    evac_x1T(b - 1)

            evac_qk(0, True)
            evac_scores(0, 0, True)
            s_window(0, 0, prev=False, first=True)
            s_window(1, 1, prev_first=True)
            with act.Fori(0, (B - 4) // 2) as i:
                for k in range(2):
                    s_window(2 * i + 2 + k, k)
            s_window(B - 2, 0)
            s_window(B - 1, 1, nxt=False)
            evac_pT(B - 1, 0, False)
            evac_pT(B - 1, 1, False)
            evac_aT(B - 1, False)
            evac_x1T(B - 1)

            def k_high(b, par_prev, c, first):
                act.wait_ge(k_ps, C * b + c + 1)
                if not first and c == 0:
                    act.wait_ge(ks_in[par_prev], 16 * STACK * stacked(b - 1))
                act.activation(kh[:, c], b_m[c][:, 0:SCP], ACT.Identity, bias=v(f"bk2_{c}")).then_inc(kh_ok, 1)

            def stacked(b):
                return b // 2 + 1 if isinstance(b, int) else b // 2 + 1

            def q_full(b, first):
                act.wait_ge(q_ps, b + 1)
                if not first:
                    act.wait_ge(qm_ok, b)
                for c in range(C):
                    last = act.activation(qf[:, c], b_m[1][:, c * S:(c + 1) * S], ACT.Identity, bias=v(f"bq2_{c}"))
                last.then_inc(qf_ok, 1)

            def exp2(b, u, no_slot_wait=False):
                n = 2 * UNITS * b + u
                rows_n = KC[u % 3][1]
                act.wait_ge(t_ps, n + 1)
                if not no_slot_wait:
                    act.wait_ge(pv_ok, n - SLOTS + 1)
                act.activation(pe2[0:rows_n, u % SLOTS],
                               b_t[u % NPT][0:rows_n].rearrange("p (g q) -> p g q", g=2)[:, :, 0:2 * S],
                               ACT.Exp, scale=SCALE2).then_inc(exp_ok, 1)

            def neg_max(b, half, first):
                act.wait_ge(mT_ps, 2 * b + half + 1)
                if not first:
                    act.wait_ge(m_in[half], 16 * b)
                act.activation(mrow[half][:], b_m[0][0:8, 0:S], ACT.Copy, scale=-1.0).then_inc(mrow_ok, 1)

            def out_T(b, first):
                act.wait_ge(pv_ok, 2 * UNITS * (b + 1))
                if not first:
                    act.wait_ge(ot_ps, b)
                act.activation(oT[:].rearrange("p h q -> p (h q)"), b_o[:, 0:4 * S], ACT.Copy).then_inc(oT_ok, 1)

            def att_T(b, first):
                act.wait_ge(at_ps, b + 1)
                if not first:
                    act.wait_ge(y2_ps, b)
                act.activation(attT[:].rearrange("p c q -> p (c q)"), b_m[0][:, 0:C * S], ACT.Copy).then_inc(attT_ok, 1)

            def ffn_T(n, first):
                act.wait_ge(x2T_ps, n + 1)
                if first:
                    act.wait_ge(zeroed, 1)
                else:
                    act.wait_ge(xrk_ok, n)
                act.activation(x2T[:, :, 1:1 + S], b_m[0][:, 0:C * S].rearrange("p (c q) -> p c q", c=C),
                               ACT.Copy).then_inc(x2T_ok, 1)

            def ffn_rk(n, first):
                act.wait_ge(r_ps, n + 1)
                if not first:
                    act.wait_ge(sg_ok, n)
                act.activation(th[:], b_m[1][0:S, 0:D], ACT.Tanh, scale=0.5).then_inc(th_ok, 1)
                act.wait_ge(kf_ps, n + 1)
                if not first:
                    act.wait_ge(ka_ok, n)
                act.activation(kr[:].rearrange("p c q -> p (c q)"), b_m[0][:, 0:C * S], ACT.Relu).then_inc(kr_ok, 1)

            def x_window(b, par, prev=True, prev2=True, nxt=True):
                small = isinstance(b, int)
                if nxt:
                    k_high(b + 1, par, 0, False)
                    k_high(b + 1, par, 1, False)
                if prev:
                    ns = small and b == 1
                    exp2(b - 1, 6, False)
                    exp2(b - 1, 7)
                    exp2(b - 1, 8)
                if prev2:
                    ffn_T(b - 2, small and b == 2)
                if prev:
                    exp2(b - 1, 9)
                    exp2(b - 1, 10)
                    exp2(b - 1, 11)
                if prev2:
                    ffn_rk(b - 2, small and b == 2)
                if prev:
                    out_T(b - 1, small and b == 1)
                neg_max(b, 0, small and b == 0)
                if nxt:
                    q_full(b + 1, False)
                if prev:
                    att_T(b - 1, small and b == 1)
                for u in range(UNITS):
                    exp2(b, u, small and b == 0)
                neg_max(b, 1, small and b == 0)

            k_high(0, None, 0, True)
            k_high(0, None, 1, True)
            q_full(0, True)
            x_window(0, 0, prev=False, prev2=False)
            x_window(1, 1, prev2=False)
            x_window(2, 0)
            x_window(3, 1)
            with act.Fori(0, (B - 6) // 2) as i:
                for k in range(2):
                    x_window(2 * i + 4 + k, k)
            x_window(B - 2, 0)
            x_window(B - 1, 1, nxt=False)
            for u in range(UNITS, 2 * UNITS):
                exp2(B - 1, u)
            ffn_T(B - 2, False)
            ffn_rk(B - 2, False)
            out_T(B - 1, False)
            att_T(B - 1, False)
            ffn_T(B - 1, False)
            ffn_rk(B - 1, False)

        @block.tensor
        def _(pe):
            pe.wait_ge(ones_ok, 1)
            pe.wait_ge(w_in, 16 * N_W)
            for k in range(2):
                pe.matmul(bank[k][:, :], ones_row[:], row_sb[:, k * 512:(k + 1) * 512], start=True, stop=True
                          ).then_inc(rows_ps, 1)
            pe.wait_ge(xsum_ok, 1)
            for c in range(C):
                last = pe.matmul(bank[2][0:GATE, 0:B], wg_sb[:, c], xsum[:, c], start=(c == 0), stop=(c == C - 1))
            last.then_inc(gate_ps, 1)
            pe.wait_ge(gate_u, 1)
            for c in range(C):
                last = pe.matmul(bank[3][:, c * B:(c + 1) * B], wgp_sb[:, c * P:(c + 1) * P], g1s[:],
                                 start=True, stop=True)
            last.then_inc(gate_ps2, 1)
            pe.wait_ge(rows_ok, 2)
            pe.wait_ge(gate_ok, C)

            def project(b, par, first):
                if not first:
                    pe.wait_ge(qk_sb, 2 * C * b)
                pe.wait_ge(xTb_ok, b + 1)
                for n, name in enumerate(("q1", "k1")):
                    for c in range(C):
                        o = b_qk[:, (n * C + c) * S:(n * C + c + 1) * S]
                        for i in range(C):
                            last = pe.matmul(o, W[name][:, i, c * P:(c + 1) * P], xTb[par][:, i],
                                             start=(i == 0), stop=(i == C - 1))
                last.then_inc(qk_ps, 1)
                if not first:
                    pe.wait_ge(v_sb, b)
                for i in range(C):
                    last = pe.matmul(b_v[0:S, 0:D], xTb[par][:, i], W["v1"][:, i], start=(i == 0), stop=(i == C - 1))
                last.then_inc(v_ps, 1)

            def scores(b, par, first):
                pe.wait_ge(qk_sb, 2 * C * (b + 1))
                pe.wait_ge(kbd_ok, b + 1)
                if not first:
                    pe.wait_ge(s_ok, 2 * b)
                for c in range(C):
                    last = pe.matmul(b_s[c][0:S, 0:HC1 * S], qs[:, c], kbd[:, c].rearrange("p h k -> p (h k)"),
                                     start=True, stop=True)
                last.then_inc(s_ps, 1)

            def turn_probs(b, par, k, first):
                pe.wait_ge(pn_ok, b + 1)
                if not first:
                    pe.wait_ge(pT_sb, 2 * b + k)
                for h in range(HC1 * k, HC1 * k + HC1):
                    last = pe.transpose(b_pT[0:S, (h % HC1) * S:(h % HC1 + 1) * S], p1[par][:, h], ident[0:S, 0:S])
                last.then_inc(pT_ps, 1)

            def mix_values(b, par, first):
                pe.wait_ge(pT_sb, 2 * b + 2)
                pe.wait_ge(v_sb, b + 1)
                if not first:
                    pe.wait_ge(x1T_sb, b)
                for h in range(H1):
                    j, c = h % HC1, h // HC1
                    last = pe.matmul(b_aT[DH1 * j:DH1 * (j + 1), c * S:(c + 1) * S],
                                     v1[par][:, DH1 * h:DH1 * (h + 1)], pT1[:, h], start=True, stop=True)
                last.then_inc(aT_ps, 1)

            def distil(b, first):
                pe.wait_ge(aT_sb, b + 1)
                if not first:
                    pe.wait_ge(dmix_ok, b)
                pe.matmul(b_d[:, 0:C * S], wd_sb[:], aT[:].rearrange("p c q -> p (c q)"), start=True, stop=True
                          ).then_inc(d_ps, 1)

            def out1(b, first):
                pe.wait_ge(mix_ok, b + 1)
                if not first:
                    pe.wait_ge(ln1, 4 * (b - 1) + 1)
                for c in range(C):
                    last = pe.matmul(b_y[0:S, 0:D], mixT[:, c], W["o1"][:, c], start=(c == 0), stop=(c == C - 1))
                last.then_inc(y1_ps, 1)

            def turn_x1(b):
                pe.wait_ge(ln1, 4 * (b + 1))
                for c in range(C):
                    last = pe.transpose(b_aT[:, c * S:(c + 1) * S], x1b[:, c * P:(c + 1) * P], ident[0:S, 0:S])
                last.then_inc(x1T_ps, 1)

            def s_window(b, par, prev=True, prev_first=False, nxt=True):
                q = 1 - par
                if prev:
                    turn_probs(b - 1, q, 0, prev_first)
                if nxt:
                    project(b + 1, q, False)
                if prev:
                    turn_probs(b - 1, q, 1, False)
                    mix_values(b - 1, q, prev_first)
                if nxt:
                    scores(b + 1, q, False)
                if prev:
                    distil(b - 1, prev_first)
                    out1(b - 1, prev_first)
                    turn_x1(b - 1)

            project(0, 0, True)
            scores(0, 0, True)
            s_window(0, 0, prev=False)
            s_window(1, 1, prev_first=True)
            with pe.Fori(0, (B - 4) // 2) as i:
                for k in range(2):
                    s_window(2 * i + 2 + k, k)
            s_window(B - 2, 0)
            s_window(B - 1, 1, nxt=False)
            turn_probs(B - 1, 1, 0, False)
            turn_probs(B - 1, 1, 1, False)
            mix_values(B - 1, 1, False)
            distil(B - 1, False)
            out1(B - 1, False)
            turn_x1(B - 1)

            def split_product(o, pairs):
                todo = [(a, m) for wh, wl, xh, xl in pairs for a, m in ((wh, xh), (wh, xl), (wl, xh))]
                for n, (a, m) in enumerate(todo):
                    last = pe.matmul(o, a, m, start=(n == 0), stop=(n == len(todo) - 1))
                return last

            def proj_k(b, c, wait):
                if c == 0:
                    pe.wait_ge(ctxl_ok, b + 1)
                for s_, n_ in wait:
                    pe.wait_ge(s_, n_)
                co = slice(c * P, (c + 1) * P)
                split_product(b_m[c][:, 0:SCP], [(wkh[:, i, co], wkl[:, i, co], ctxh[:, i], ctxl[:, i])
                                                 for i in range(C)]).then_inc(k_ps, 1)

            def proj_v(b, part, wait):
                for s_, n_ in wait:
                    pe.wait_ge(s_, n_)
                for kc in ((0, 1), (2,))[part]:
                    k0, n = KC[kc]
                    o = b_m[part][0:n, (kc % 2) * D:(kc % 2 + 1) * D]
                    last = split_product(o, [(ctxh[:, i, k0:k0 + n], ctxl[:, i, k0:k0 + n], wvh[:, i], wvl[:, i])
                                             for i in range(C)])
                last.then_inc(v2_ps, 1)

            def head_max(b, par, h, first=False):
                n = H2 * b + h
                if h == 0:
                    pe.wait_ge(ks_in[par], 16 * STACK * (b // 2 + 1))
                    pe.wait_ge(qs_in[par], 16 * STACK * (b // 2 + 1))
                if not (first and h < 2):
                    pe.wait_ge(max_ok, n - 1)
                pe.matmul(b_max[h % 2][0:S, 0:SCP], qst[par][0:96, h * S:(h + 1) * S], ks[par][0:96, h // 2, :],
                          start=True, stop=True).then_inc(max_ps, 1)

            def turn_max(b, par, half, wait):
                pe.wait_ge(max_ok, H2 * b + 8 * half + 8)
                for s_, n_ in wait:
                    pe.wait_ge(s_, n_)
                pe.transpose(b_m[0][0:8, 0:S], m2[par][:, 8 * half:8 * half + 8], ident[0:S, 0:S]).then_inc(mT_ps, 1)

            def t_unit(b, par, u, first=False):
                n = 2 * UNITS * b + u
                gp, (k0, kn) = u // 3, KC[u % 3]
                if u % UNITS == 0:
                    pe.wait_ge(m_in[u // UNITS], 16 * (b + 1))
                if not (first and u < NPT):
                    pe.wait_ge(exp_ok, n - NPT + 1)
                for i in range(2):
                    g = 2 * gp + i
                    last = pe.matmul(b_t[u % NPT][0:kn, i * D:(i + 1) * D], ks[par][:, g, k0:k0 + kn],
                                     qst[par][:, g * 2 * S:g * 2 * S + D], start=True, stop=True)
                last.then_inc(t_ps, 1)

            def pv_unit(b, par, u, first=False):
                n = 2 * UNITS * b + u
                gp, kc = u // 3, u % 3
                kn = KC[kc][1]
                pe.wait_ge(exp_ok, n + 1)
                if u == 0:
                    pe.wait_ge(v2_sb, 3 * (b + 1))
                    if not first:
                        pe.wait_ge(oT_ok, b)
                for j in range(4):
                    last = pe.matmul(b_o[VW * j:VW * (j + 1), gp * S:(gp + 1) * S], vx[par][0:kn, kc, 4 * gp + j],
                                     pe2[0:kn, u % SLOTS].rearrange("p g q -> p (g q)")[:, j * S:(j + 1) * S],
                                     start=(u == 0), stop=(u == 2 * UNITS - 1), skip_group_check=True)
                last.then_inc(pv_ok, 1)

            def proj_q(b, wait):
                for s_, n_ in wait:
                    pe.wait_ge(s_, n_)
                for c in range(C):
                    for i in range(C):
                        last = pe.matmul(b_m[1][:, c * S:(c + 1) * S], W["q2"][:, i, c * P:(c + 1) * P],
                                         x1T_all[:, i, bass.ds(b * S, S)], start=(i == 0), stop=(i == C - 1))
                last.then_inc(q_ps, 1)

            def turn_out(b, wait):
                pe.wait_ge(oT_ok, b + 1)
                for s_, n_ in wait:
                    pe.wait_ge(s_, n_)
                for k in range(4):
                    last = pe.transpose(b_m[0][0:S, k * P:(k + 1) * P], oT[:, k], ident)
                last.then_inc(ot_ps, 1)

            def turn_att(b):
                pe.wait_ge(att_ok, b + 1)
                av = att[:].rearrange("p h d -> p (h d)")
                for c in range(C):
                    last = pe.transpose(b_m[0][:, c * S:(c + 1) * S], av[:, c * P:(c + 1) * P], ident[0:S, 0:S])
                last.then_inc(at_ps, 1)

            def out2(b, wait):
                pe.wait_ge(attT_ok, b + 1)
                for s_, n_ in wait:
                    pe.wait_ge(s_, n_)
                for c in range(C):
                    last = pe.matmul(b_m[1][0:S, 0:D], attT[:, c], W["o2"][:, c], start=(c == 0), stop=(c == C - 1))
                last.then_inc(y2_ps, 1)

            def turn_x2(n, wait):
                pe.wait_ge(ln2, 4 * (n + 1))
                for s_, n_ in wait:
                    pe.wait_ge(s_, n_)
                for c in range(C):
                    last = pe.transpose(b_m[0][:, c * S:(c + 1) * S], x2[:, c * P:(c + 1) * P], ident[0:S, 0:S])
                last.then_inc(x2T_ps, 1)

            def ffn_in(n, wait):
                pe.wait_ge(xrk_ok, n + 1)
                for s_, n_ in wait:
                    pe.wait_ge(s_, n_)
                for i in range(C):
                    last = pe.matmul(b_m[1][0:S, 0:D], xr[:, i], W["r"][:, i], start=(i == 0), stop=(i == C - 1))
                last.then_inc(r_ps, 1)
                for c in range(C):
                    for i in range(C):
                        last = pe.matmul(b_m[0][:, c * S:(c + 1) * S], W["k"][:, i, c * P:(c + 1) * P], xk[:, i],
                                         start=(i == 0), stop=(i == C - 1))
                last.then_inc(kf_ps, 1)

            def ffn_out(n):
                pe.wait_ge(ka_ok, n + 1)
                pe.wait_ge(th_ok, n + 1)
                for i in range(C):
                    last = pe.matmul(b_m[1][0:S, 0:D], ka[:, i], W["v"][:, i], start=(i == 0), stop=(i == C - 1))
                last.then_inc(f_ps, 1)

            def x_window(b, par, prev=True, prev2=True, nxt=True):
                first = isinstance(b, int) and b == 0
                pfirst = isinstance(b, int) and b == 1
                q = 1 - par
                head_max(b, par, 0, first)
                head_max(b, par, 1, first)
                if nxt:
                    proj_k(b + 1, 0, [(mrow_ok, 2 * b)] if not first else [(qf_ok, 1)])
                head_max(b, par, 2, first)
                if nxt:
                    proj_k(b + 1, 1, [(ln2, 4 * (b - 2) + 1)] if prev2 else [(qf_ok, b + 1)])
                head_max(b, par, 3)
                if prev:
                    t_unit(b - 1, q, 6)
                    t_unit(b - 1, q, 7)
                    pv_unit(b - 1, q, 6)
                head_max(b, par, 4)
                if prev:
                    t_unit(b - 1, q, 8)
                    pv_unit(b - 1, q, 7)
                head_max(b, par, 5)
                if prev2:
                    turn_x2(b - 2, [(kl_ok, C * (b + 1) + 1)] if nxt else [(mrow_ok, 2 * b)])
                if prev:
                    t_unit(b - 1, q, 9)
                    pv_unit(b - 1, q, 8)
                head_max(b, par, 6)
                if prev:
                    t_unit(b - 1, q, 10)
                    pv_unit(b - 1, q, 9)
                if prev2:
                    ffn_in(b - 2, [(kl_ok, C * (b + 2))] if nxt else [(ln2, 4 * (b - 2) + 1)])
                head_max(b, par, 7)
                if prev:
                    t_unit(b - 1, q, 11)
                    pv_unit(b - 1, q, 10)
                    pv_unit(b - 1, q, 11)
                if prev2:
                    ffn_out(b - 2)
                turn_max(b, par, 0, [(kr_ok, b - 1)] if prev2 else [(kl_ok, C * (b + 1) + 1)])
                head_max(b, par, 8)
                if nxt:
                    proj_v(b + 1, 0, [(mrow_ok, 2 * b + 1)])
                head_max(b, par, 9)
                if nxt:
                    proj_v(b + 1, 1, [(rv_ok, b - 1)] if prev2 else [(kl_ok, C * (b + 2))])
                if prev:
                    turn_out(b - 1, [(v2_sb, 3 * (b + 1) + 2)] if nxt else [(mrow_ok, 2 * b + 1)])
                head_max(b, par, 10)
                if nxt:
                    proj_q(b + 1, [(v2_sb, 3 * (b + 2))])
                head_max(b, par, 11)
                if prev:
                    turn_att(b - 1)
                t_unit(b, par, 0, first)
                if prev:
                    out2(b - 1, [(qf_ok, b + 2)] if nxt else [(rv_ok, b - 1)])
                t_unit(b, par, 1, first)
                pv_unit(b, par, 0, first)
                head_max(b, par, 12)
                t_unit(b, par, 2, first)
                pv_unit(b, par, 1)
                head_max(b, par, 13)
                t_unit(b, par, 3)
                pv_unit(b, par, 2)
                head_max(b, par, 14)
                t_unit(b, par, 4)
                pv_unit(b, par, 3)
                head_max(b, par, 15)
                t_unit(b, par, 5)
                pv_unit(b, par, 4)
                pv_unit(b, par, 5)
                turn_max(b, par, 1, [(attT_ok, b)] if prev else [(mrow_ok, 2 * b + 1)])

            pe.wait_ge(x1T_sb, B)
            pe.wait_ge(wsplit, 4)
            pe.wait_ge(zeroed, 2)
            pe.wait_ge(ln1, 4 * B)
            proj_k(0, 0, [])
            proj_k(0, 1, [])
            proj_v(0, 0, [(kl_ok, 1)])
            proj_v(0, 1, [(kl_ok, 2)])
            proj_q(0, [(v2_sb, 3)])
            x_window(0, 0, prev=False, prev2=False)
            x_window(1, 1, prev2=False)
            x_window(2, 0)
            x_window(3, 1)
            with pe.Fori(0, (B - 6) // 2) as i:
                for k in range(2):
                    x_window(2 * i + 4 + k, k)
            x_window(B - 2, 0)
            x_window(B - 1, 1, nxt=False)
            for u in range(UNITS, 2 * UNITS):
                t_unit(B - 1, 1, u)
                if u >= UNITS + 2:
                    pv_unit(B - 1, 1, u - 2)
            pv_unit(B - 1, 1, 2 * UNITS - 2)
            pv_unit(B - 1, 1, 2 * UNITS - 1)
            turn_x2(B - 2, [(mrow_ok, 2 * B)])
            ffn_in(B - 2, [(ln2, 4 * (B - 2) + 1)])
            ffn_out(B - 2)
            turn_out(B - 1, [(kr_ok, B - 1)])
            turn_att(B - 1)
            out2(B - 1, [(ln3, 4 * (B - 2) + 1)])
            turn_x2(B - 1, [(attT_ok, B)])
            ffn_in(B - 1, [(ln2, 4 * (B - 1) + 1)])
            ffn_out(B - 1)

        @block.vector
        def _(dve):
            for t in range(2):
                dve.memset(vx[t][:], 1.0)
                dve.memset(qst[t][:].bitcast(F32), 0.0)
                dve.memset(ks[t][96:128].bitcast(F32), 0.0)
            dve.memset(x2T[:], 0.0).then_inc(zeroed, 1)
            dve.wait_ge(zeroed, 1)
            for t in range(2):
                last = dve.memset(ks[t][96:97].bitcast(F32), 1.0)
            last.then_inc(zeroed, 1)
            dve.wait_ge(xT_in, 16)
            for c in range(C):
                last = dve.tensor_reduce(xsum[:, c], xT_all[:, c].rearrange("p (b s) -> p b s", s=S), AX.X, ALU.add)
            last.then_inc(xsum_ok, 1)
            dve.wait_ge(gate_t, 1)
            dve.tensor_scalar(g1s[:], g1[:], 0.5, 0.5, ALU.mult, ALU.add).then_inc(gate_u, 1)
            dve.wait_ge(rows_ok, 2)
            dve.wait_ge(zeroed, 2)

            def values(b, par):
                dve.wait_ge(v_ps, b + 1)
                if not (isinstance(b, int) and b < 2):
                    dve.wait_ge(aT_ps, b - 1)
                dve.tensor_tensor(v1[par][:], b_v[0:S, 0:D], ROW["bv1"][0:S], ALU.add).then_inc(v_sb, 1)

            def distilled(b, par):
                dve.wait_ge(d_ps, b + 1)
                dve.scalar_tensor_tensor(dmix[:].rearrange("p c q -> p (c q)"), b_d[:, 0:C * S], v("bd"),
                                         aT[:].rearrange("p c q -> p (c q)"), ALU.add, ALU.subtract
                                         ).then_inc(dmix_ok, 1)
                dve.wait_ge(dmix_ok, b + 1)
                dve.wait_ge(gb_ok, b + 1)
                if not (isinstance(b, int) and b == 0):
                    dve.wait_ge(y1_ps, b)
                for c in range(C):
                    last = dve.scalar_tensor_tensor(mixT[:, c], dmix[:, c], gb[par][:, c:c + 1], aT[:, c],
                                                    ALU.mult, ALU.add)
                last.then_inc(mix_ok, 1)

            def stats(n, ln, y):
                dve.wait_ge(ln, 4 * n + 1)
                dve.bn_stats(st[:], y[:]).then_inc(ln, 1)
                dve.wait_ge(ln, 4 * n + 2)
                carry(dve)
                dve.bn_aggr(mv[:], st[:]).then_inc(ln, 1)

            def norm(n, ln, rstd_s, y, dst):
                dve.wait_ge(ln, 4 * n + 3)
                dve.wait_ge(rstd_s, n + 1)
                return dve.tensor_scalar(dst, y[:], mv[:, 0:1], rstd[:], ALU.subtract, ALU.mult)

            def residual1(b, par):
                dve.wait_ge(y1_ps, b + 1)
                dve.wait_ge(xbo_ok, b + 1)
                dve.tensor_tensor(y1[:], b_y[0:S, 0:D], xbo[par][:], ALU.add).then_inc(ln1, 1)
                stats(b, ln1, y1)

            def norm1(b):
                if not (isinstance(b, int) and b == 0):
                    dve.wait_ge(x1T_ps, b)
                norm(b, ln1, rstd1, y1, x1b[:])
                norm(b, ln1, rstd1, y1, x1_all[:, bass.ds(b * D, D)]).then_inc(ln1, 1)

            def s_window(b, par, prev=True, nxt=True):
                first = isinstance(b, int) and b == 0
                q = 1 - par
                dve.wait_ge(s_ok, 2 * b + 2)
                carry(dve)
                for h in range(H1):
                    last = dve.max(top1[:, h], s_sb[par][:, h])
                last.then_inc(top1_ok, 1)
                dve.wait_ge(top1_ok, b + 1)
                if not first:
                    dve.wait_ge(e1_ok, H1 * b)
                dve.tensor_scalar(negm1[:], top1[:, :, 0], -SCALE1, None, ALU.mult).then_inc(negm_ok, 1)
                for h in range(H1):
                    last = dve.match_replace(rest[:, h], top1[:, h], s_sb[par][:, h], -3.0e38)
                last.then_inc(rest_ok, 1)
                dve.wait_ge(rest_ok, b + 1)
                carry(dve)
                for h in range(H1):
                    last = dve.max(top2[:, h], rest[:, h])
                last.then_inc(top2_ok, 1)
                if prev:
                    distilled(b - 1, q)
                if nxt:
                    values(b + 1, q)
                dve.wait_ge(top2_ok, b + 1)
                dve.wait_ge(e1_ok, H1 * (b + 1))
                if not (isinstance(b, int) and b < 2):
                    dve.wait_ge(pT_ps, 2 * (b - 1))
                for h in range(H1):
                    last = dve.scalar_tensor_tensor(p1[par][:, h], s_sb[par][:, h],
                                                    top2[:, h, TOPK - 9:TOPK - 8], e1[:, h],
                                                    ALU.is_ge, ALU.mult, accum_out=den1[:, h:h + 1])
                    if prev and h == 3:
                        residual1(b - 1, q)
                last.then_inc(p1_ok, 1)
                dve.wait_ge(p1_ok, b + 1)
                dve.reciprocal(rden1[par][:], den1[:]).then_inc(rden1_ok, 1)
                if prev:
                    norm1(b - 1)

            values(0, 0)
            s_window(0, 0, prev=False)
            s_window(1, 1)
            with dve.Fori(0, (B - 4) // 2) as i:
                for k in range(2):
                    s_window(2 * i + 2 + k, k)
            s_window(B - 2, 0)
            dve.wait_ge(w_in, 16 * N_W)
            for hi, src in ((wkh, W["k2"]), (wvh, W["v2"])):
                dve.tensor_copy(hi[:], src).then_inc(wsplit, 1)
            dve.wait_ge(wsplit, 2)
            for hi, lo, src in ((wkh, wkl, W["k2"]), (wvh, wvl, W["v2"])):
                dve.tensor_tensor(lo[:], src, hi[:].bitcast(F32), ALU.subtract).then_inc(wsplit, 1)
            s_window(B - 1, 1, nxt=False)
            distilled(B - 1, 1)
            residual1(B - 1, 1)
            norm1(B - 1)

            def ctx_high(b, par, reuse):
                dve.wait_ge(ctx_in[par], 16 * (b // 2 + 1))
                if reuse:
                    dve.wait_ge(v2_ps, 2 * b)
                dve.tensor_copy(ctxh[:], ctxf[par][:]).then_inc(ctxh_ok, 1)

            def k_low(b, c):
                dve.wait_ge(kh_ok, C * b + c + 1)
                dve.scalar_tensor_tensor(kl[:, c], b_m[c][:, 0:SCP], v(f"bk2_{c}"), kh[:, c].bitcast(F32),
                                         ALU.add, ALU.subtract).then_inc(kl_ok, 1)

            def values2(b, par, part, reuse):
                dve.wait_ge(v2_ps, 2 * b + part + 1)
                if reuse:
                    dve.wait_ge(pv_ok, 2 * UNITS * (b - 1))
                for kc in ((0, 1), (2,))[part]:
                    n = KC[kc][1]
                    dve.tensor_tensor(vx[par][0:n, kc, :, 0:DH2],
                                      b_m[part][0:n, (kc % 2) * D:(kc % 2 + 1) * D].rearrange("p (h d) -> p h d", d=DH2),
                                      ROW["bv2"][0:n].rearrange("p (h d) -> p h d", d=DH2), ALU.add
                                      ).then_inc(v2_sb, 1)

            def q_high(b, par_prev, first):
                dve.wait_ge(qm_ok, b + 1)
                if not first:
                    dve.wait_ge(qs_in[par_prev], 16 * STACK * ((b - 1) // 2 + 1))
                dve.tensor_copy(qh[:], qm[:]).then_inc(qh_ok, 1)

            def head_max(b, par, h, first):
                n = H2 * b + h
                dve.wait_ge(max_ps, n + 1)
                if h == 0 and not first:
                    dve.wait_ge(mT_ps, 2 * (b - 1))
                dve.tensor_reduce(m2[par][:, h:h + 1], b_max[h % 2][0:S, 0:SC], AX.X, ALU.max).then_inc(max_ok, 1)

            def attention(b):
                dve.wait_ge(ot_ps, b + 1)
                ov = b_m[0][0:S, :].rearrange("p (h e) -> p h e", e=VW)
                dve.reciprocal(rden2[:], ov[:, :, DH2]).then_inc(rden2_ok, 1)
                dve.wait_ge(rden2_ok, b + 1)
                if not (isinstance(b, int) and b == 0):
                    dve.wait_ge(at_ps, b)
                dve.tensor_tensor(att[:], ov[:, :, 0:DH2],
                                  rden2[:].rearrange("p (h a) -> p h a", a=1).broadcast_to([S, H2, DH2]),
                                  ALU.mult).then_inc(att_ok, 1)

            def residual2(b):
                dve.wait_ge(y2_ps, b + 1)
                dve.wait_ge(xres_ok, b + 1)
                dve.tensor_tensor(y2[:], b_m[1][0:S, 0:D], xres[:], ALU.add).then_inc(ln2, 1)
                stats(b, ln2, y2)

            def norm2(b):
                if not (isinstance(b, int) and b == 0):
                    dve.wait_ge(x2T_ps, b)
                norm(b, ln2, rstd2, y2, x2[:]).then_inc(ln2, 1)

            def shift_mix(n):
                dve.wait_ge(dx_ok, n + 1)
                if not (isinstance(n, int) and n == 0):
                    dve.wait_ge(kf_ps, n)
                for c in range(C):
                    dve.scalar_tensor_tensor(xr[:, c], dx[:, c], v(f"mur_{c}"), x2T[:, c, 0:S], ALU.mult, ALU.add)
                    last = dve.scalar_tensor_tensor(xk[:, c], dx[:, c], v(f"muk_{c}"), x2T[:, c, 0:S],
                                                    ALU.mult, ALU.add)
                last.then_inc(xrk_ok, 1)

            def sigmoid_r(n):
                dve.wait_ge(th_ok, n + 1)
                dve.tensor_scalar(sg[:], th[:], 0.5, 0.5, ALU.mult, ALU.add).then_inc(sg_ok, 1)

            def residual3(n):
                dve.wait_ge(f_ps, n + 1)
                dve.wait_ge(sg_ok, n + 1)
                dve.tensor_tensor(rv[:], b_m[1][0:S, 0:D], sg[:], ALU.mult).then_inc(rv_ok, 1)
                dve.wait_ge(rv_ok, n + 1)
                dve.tensor_tensor(y3[:], rv[:], x2[:], ALU.add).then_inc(ln3, 1)
                stats(n, ln3, y3)

            def norm3(n, par):
                if not (isinstance(n, int) and n < 2):
                    dve.wait_ge(out_done[par], 16 * (n // 2))
                norm(n, ln3, rstd3, y3, x3[par][:]).then_inc(ln3, 1)

            def x_window(b, par, prev=True, prev2=True, nxt=True, nxt2=True):
                small = isinstance(b, int)
                fm = small and b < 2
                q = 1 - par
                head_max(b, par, 0, fm)
                head_max(b, par, 1, fm)
                if nxt:
                    k_low(b + 1, 0)
                head_max(b, par, 2, fm)
                if nxt:
                    k_low(b + 1, 1)
                head_max(b, par, 3, fm)
                head_max(b, par, 4, fm)
                head_max(b, par, 5, fm)
                if prev2:
                    shift_mix(b - 2)
                head_max(b, par, 6, fm)
                head_max(b, par, 7, fm)
                if prev2:
                    sigmoid_r(b - 2)
                    residual3(b - 2)
                head_max(b, par, 8, fm)
                if nxt:
                    values2(b + 1, q, 0, not (small and b < 1))
                head_max(b, par, 9, fm)
                if nxt:
                    values2(b + 1, q, 1, not (small and b < 1))
                if prev:
                    attention(b - 1)
                if prev2:
                    norm3(b - 2, par)
                head_max(b, par, 10, fm)
                if nxt:
                    q_high(b + 1, par, False)
                head_max(b, par, 11, fm)
                if prev:
                    residual2(b - 1)
                head_max(b, par, 12, fm)
                head_max(b, par, 13, fm)
                head_max(b, par, 14, fm)
                if prev:
                    norm2(b - 1)
                head_max(b, par, 15, fm)
                if nxt2:
                    ctx_high(b + 2, par, True)

            ctx_high(0, 0, False)
            k_low(0, 0)
            k_low(0, 1)
            values2(0, 0, 0, False)
            values2(0, 0, 1, False)
            q_high(0, None, True)
            ctx_high(1, 1, True)
            x_window(0, 0, prev=False, prev2=False)
            x_window(1, 1, prev2=False)
            x_window(2, 0)
            x_window(3, 1)
            with dve.Fori(0, (B - 6) // 2) as i:
                for k in range(2):
                    x_window(2 * i + 4 + k, k)
            x_window(B - 2, 0, nxt2=False)
            x_window(B - 1, 1, nxt=False, nxt2=False)
            shift_mix(B - 2)
            sigmoid_r(B - 2)
            residual3(B - 2)
            attention(B - 1)
            norm3(B - 2, 0)
            residual2(B - 1)
            norm2(B - 1)
            shift_mix(B - 1)
            sigmoid_r(B - 1)
            residual3(B - 1)
            norm3(B - 1, 1)


def kernel(**inputs):
    import numpy as np
    import concourse.bacc as bacc
    from concourse.bass_utils import run_bass_kernel_spmd

    a = {k: np.asarray(v_) for k, v_ in inputs.items()}

    def chunks(m):
        return m.reshape(C, P, -1).transpose(1, 0, 2)

    order = np.arange(D).reshape(C, 4, 32).transpose(0, 2, 1).reshape(D)
    wkv = a["L0_xattn_Wkv"].reshape(D, D, 2)
    mats = [a["L0_attn_Wq"].T, a["L0_attn_Wk"].T, a["L0_attn_Wv"].T, a["L0_attn_Wo"].T,
            a["L0_xattn_Wq"][:, order], wkv[:, order, 0], wkv[:, :, 1], a["L0_xattn_Wout"],
            a["L0_ffn_W_r"].T, a["L0_ffn_W_k"].T, a["L0_ffn_W_v"].T]
    wpack = np.stack([chunks(m) for m in mats], axis=1)
    bkv = a["L0_xattn_bkv"].reshape(D, 2)
    cols = [a["L0_attn_bq"], a["L0_attn_bk"], a["L0_xattn_bq"][order], bkv[order, 0],
            a["L0_ffn_mu_r"], a["L0_ffn_mu_k"], a["L0_attn_bgp"]]
    vecs = np.zeros((P, NVEC), np.float32)
    for i, m in enumerate(cols):
        vecs[:, 2 * i:2 * i + 2] = m.reshape(C, P).T
    vecs[:, VEC["bd"]] = np.concatenate([a["L0_attn_bd"]] * (P // GATE))
    vecs[0:GATE, VEC["bg"]] = a["L0_attn_bg"]
    rows = np.concatenate([a["L0_attn_bv"], a["L0_attn_bo"], bkv[:, 1], a["L0_xattn_bout"]]).reshape(1, 4 * D)
    wd = np.zeros((P, P), np.float32)
    for i in range(P // GATE):
        wd[i * GATE:(i + 1) * GATE, i * GATE:(i + 1) * GATE] = a["L0_attn_Wd"].T
    part = np.arange(P)
    consts = np.concatenate([np.eye(P), part[:, None] // DH1 == np.arange(HC1),
                             part[:, None] // (P // 2) == np.arange(2)], axis=1).astype(np.float32)
    xT = a["x"].reshape(B * S, C, P).transpose(2, 1, 0)
    ctxT = np.zeros((B, P, C, SCP), np.float32)
    ctxT[:, :, :, 0:SC] = a["ctx_1024"].reshape(B, SC, C, P).transpose(0, 3, 2, 1)
    arrays = {"x": a["x"], "xT": xT, "ctxT": ctxT, "wpack": wpack, "vecs": vecs, "rows": rows, "wd": wd,
              "wg": chunks(a["L0_attn_Wg"].T), "wgp": a["L0_attn_Wgp"].T, "consts": consts}
    nc = bacc.Bacc("TRN2", target_bir_lowering=False, num_devices=1)
    arrays = {f"in_{k}": np.ascontiguousarray(m) for k, m in arrays.items()}
    args = [nc.dram_tensor(k, m.shape, mybir.dt.from_np(m.dtype), kind="ExternalInput").ap()
            for k, m in arrays.items()]
    out = nc.dram_tensor("out_0", (B, S, D), F32, kind="ExternalOutput").ap()
    decoder_layer(nc, *args, out)
    r = run_bass_kernel_spmd(nc, [arrays], core_ids=[0])
    return r.results[0]["out_0"]
```

```python
import concourse.bass as bass
from concourse import mybir
from contextlib import ExitStack

F32 = mybir.dt.float32
F32R = mybir.dt.float32r
ACT = mybir.ActivationFunctionType
ALU = mybir.AluOpType
AX = mybir.AxisListType

B, S, D, SC = 16, 100, 256, 361
P = 128
C = D // P
SCP = SC + 1
H1, DH1 = 8, 32
HC1 = P // DH1
TOPK = max(int(S * 0.1), 1)
GATE = H1 * H1
H2, DH2 = 16, 16
NG = H2 // 2
KC = [(0, 128), (128, 128), (256, SC - 256)]
VW = 32
STACK = 3 + 3
EPS = 1e-5
SCALE1 = float(DH1) ** -0.5
SCALE2 = float(DH2) ** -0.5
QSW = 8 * S + 56
UNITS = 6
NPT = 2
NMX = 3
SLOTS = 6
W_NAMES = ["q1", "k1", "v1", "o1", "q2", "k2", "v2", "o2", "r", "k", "v"]
VEC = {n: i for i, n in enumerate(
    ["bq1_0", "bq1_1", "bk1_0", "bk1_1", "bq2_0", "bq2_1", "bk2_0", "bk2_1",
     "mur_0", "mur_1", "muk_0", "muk_1", "bgp_0", "bgp_1", "bd", "bg"])}
NVEC = len(VEC)
ROWS = ["bv1", "bo1", "bv2", "bo2"]


def decoder_layer(nc, x, xT, ctxT, wpack, vecs, rows, wd, wg, wgp, consts, out):
    es = ExitStack()
    with es:
        def sb(name, shape, dt=F32):
            return es.enter_context(nc.sbuf_tensor(name, shape, dt))

        def sem(name):
            return es.enter_context(nc.semaphore(name))

        def two(make, name, *a):
            return [make(f"{name}{i}", *a) for i in range(2)]

        bank = [es.enter_context(nc.psum_tensor(f"bank{i}", [P, 512], F32)) for i in range(8)]

        w = sb("w", [P, len(W_NAMES), C, D])
        W = {n: w[:, i] for i, n in enumerate(W_NAMES)}
        vec = sb("vec", [P, NVEC])
        wd_sb = sb("wd_sb", [P, P])
        wg_sb = sb("wg_sb", [P, C, GATE])
        wgp_sb = sb("wgp_sb", [GATE, D])
        cst = sb("cst", [P, P + HC1 + 2])
        ident = cst[:, 0:P]
        quad_mask = cst[:, P:P + HC1]
        pair_mask = cst[:, P + HC1:P + HC1 + 2]
        row_sb = sb("row_sb", [1, 4 * D])
        ones_row = sb("ones_row", [1, P])
        rowb = sb("rowb", [P, 4, D])
        ROW = {n: rowb[:, i] for i, n in enumerate(ROWS)}
        mhalf = sb("mhalf", [P, 1])
        wkh, wkl, wvh, wvl = (sb(n, [P, C, D], F32R) for n in ("wkh", "wkl", "wvh", "wvl"))

        def v(name):
            return vec[:, VEC[name]:VEC[name] + 1]

        xT_all = sb("xT_all", [P, C, B * S])
        x1_all = sb("x1_all", [S, B * D])
        x1T_all = xT_all
        xsum = sb("xsum", [P, C, B])
        hbg = sb("hbg", [GATE, 1])
        g1 = sb("g1", [GATE, B])
        g1s = sb("g1s", [GATE, B])
        gate_all = sb("gate_all", [P, C, B])

        xTb = two(sb, "xTb", [P, C, S])
        xin = two(sb, "xin", [S, D])
        gb = two(sb, "gb", [P, C])
        qs = sb("qs", [P, C, S])
        kt = sb("kt", [P, C, S])
        kbd = sb("kbd", [P, C, HC1, S])
        v1 = two(sb, "v1", [S, D])
        s_sb = two(sb, "s_sb", [S, H1, S])
        rest = sb("rest", [S, H1, S])
        top1 = sb("top1", [S, H1, 8])
        top2 = sb("top2", [S, H1, 8])
        negm1 = sb("negm1", [S, H1])
        e1 = sb("e1", [S, H1, S])
        p1 = two(sb, "p1", [S, H1, S])
        den1 = sb("den1", [S, H1])
        rden1 = two(sb, "rden1", [S, H1])
        pT1 = sb("pT1", [S, H1, S])
        aT = sb("aT", [P, C, S])
        dmix = sb("dmix", [P, C, S])
        mixT = sb("mixT", [P, C, S])
        xbo = two(sb, "xbo", [S, D])
        y1 = sb("y1", [S, D])
        x1b = sb("x1b", [S, D])
        st = sb("st", [S, 6])
        mv = sb("mv", [S, 2])
        ve = sb("ve", [S, 1])
        rstd = sb("rstd", [S, 1])

        ctxf = two(sb, "ctxf", [P, C, SCP])
        ctxh = sb("ctxh", [P, C, SCP], F32R)
        ctxl = sb("ctxl", [P, C, SCP], F32R)
        kh = sb("kh", [P, C, SCP], F32R)
        kl = sb("kl", [P, C, SCP], F32R)
        ks = two(sb, "ks", [P, NG, SCP], F32R)
        qf = sb("qf", [P, C, S])
        qm = sb("qm", [P, C, 2, S])
        qh = sb("qh", [P, C, 2, S], F32R)
        ql = sb("ql", [P, C, 2, S], F32R)
        qst = two(sb, "qst", [P, C, QSW], F32R)
        vx = two(sb, "vx", [P, len(KC), H2, VW])
        m2 = two(sb, "m2", [S, H2])
        mrow = two(sb, "mrow", [H2 // 2, S], F32R)
        pe2 = sb("pe2", [P, SLOTS, 2, 2 * S])
        oT = sb("oT", [P, 4, S])
        rden2 = sb("rden2", [S, H2])
        att = sb("att", [S, H2, DH2])
        attT = sb("attT", [P, C, S])
        xres = sb("xres", [S, D])
        y2 = sb("y2", [S, D])
        x2 = sb("x2", [S, D])
        x2T = sb("x2T", [P, C, 1 + S])
        dx = sb("dx", [P, C, S])
        xr = sb("xr", [P, C, S])
        xk = sb("xk", [P, C, S])
        th = sb("th", [S, D])
        sg = sb("sg", [S, D])
        kr = sb("kr", [P, C, S])
        ka = sb("ka", [P, C, S])
        rv = sb("rv", [S, D])
        y3 = sb("y3", [S, D])
        x3 = two(sb, "x3", [S, D])

        carried = sem("carried")
        w_in = sem("w_in")
        xT_in = sem("xT_in")
        x_in = two(sem, "x_in")
        ones_ok = sem("ones_ok")
        rows_ps = sem("rows_ps")
        rows_ok = sem("rows_ok")
        xsum_ok = sem("xsum_ok")
        gate_ps = sem("gate_ps")
        gate_t = sem("gate_t")
        gate_u = sem("gate_u")
        gate_ps2 = sem("gate_ps2")
        gate_ok = sem("gate_ok")
        wsplit = sem("wsplit")
        hbg_ok = sem("hbg_ok")
        zeroed = sem("zeroed")
        xTb_ok = sem("xTb_ok")
        gb_ok = sem("gb_ok")
        qk_ps, v_ps = sem("qk_ps"), sem("v_ps")
        qk_sb = sem("qk_sb")
        v_sb = sem("v_sb")
        kbd_ok = sem("kbd_ok")
        s_ps = sem("s_ps")
        s_ok = sem("s_ok")
        top1_ok, negm_ok, rest_ok, top2_ok = (sem(n) for n in ("top1_ok", "negm_ok", "rest_ok", "top2_ok"))
        e1_ok, p1_ok, rden1_ok, pn_ok = (sem(n) for n in ("e1_ok", "p1_ok", "rden1_ok", "pn_ok"))
        pT_ps, pT_sb = sem("pT_ps"), sem("pT_sb")
        aT_ps, aT_sb = sem("aT_ps"), sem("aT_sb")
        d_ps, dmix_ok, mix_ok = sem("d_ps"), sem("dmix_ok"), sem("mix_ok")
        y1_ps, xbo_ok = sem("y1_ps"), sem("xbo_ok")
        ln1, ve1, rstd1 = sem("ln1"), sem("ve1"), sem("rstd1")
        x1T_ps, x1T_sb, x1_kept = sem("x1T_ps"), sem("x1T_sb"), sem("x1_kept")

        ctx_in = two(sem, "ctx_in")
        ctxh_ok, ctxl_ok = sem("ctxh_ok"), sem("ctxl_ok")
        k_ps, v2_ps = sem("k_ps"), sem("v2_ps")
        kh_ok, kl_ok, v2_sb = sem("kh_ok"), sem("kl_ok"), sem("v2_sb")
        st_in = [two(sem, f"st_in_{c}_") for c in range(C)]
        q_ps, qf_ok, qm_ok, qh_ok, ql_ok = (sem(n) for n in ("q_ps", "qf_ok", "qm_ok", "qh_ok", "ql_ok"))
        max_ps, max_ok = sem("max_ps"), sem("max_ok")
        mT_ps, mrow_ok = sem("mT_ps"), sem("mrow_ok")
        m_in = [sem("m_in0"), sem("m_in1")]
        t_ps, exp_ok, pv_ok = sem("t_ps"), sem("exp_ok"), sem("pv_ok")
        oT_ok = sem("oT_ok")
        ot_ps, rden2_ok, att_ok = sem("ot_ps"), sem("rden2_ok"), sem("att_ok")
        at_ps, attT_ok = sem("at_ps"), sem("attT_ok")
        y2_ps, xres_ok = sem("y2_ps"), sem("xres_ok")
        ln2, ve2, rstd2 = sem("ln2"), sem("ve2"), sem("rstd2")
        x2T_ps, x2T_ok, dx_ok, xrk_ok = (sem(n) for n in ("x2T_ps", "x2T_ok", "dx_ok", "xrk_ok"))
        th_ok, sg_ok, rv_ok = sem("th_ok"), sem("sg_ok"), sem("rv_ok")
        kf_ps, kr_ok, ka_ok, f_ps = sem("kf_ps"), sem("kr_ok"), sem("ka_ok"), sem("f_ps")
        ln3, ve3, rstd3 = sem("ln3"), sem("ve3"), sem("rstd3")
        out_done = two(sem, "out_done")

        b_s = bank[0:2]
        b_qk, b_v, b_pT, b_aT, b_d, b_y = bank[2:8]
        b_max = bank[0:NMX]
        b_t = bank[NMX:NMX + NPT]
        b_o = bank[5]
        b_m = bank[6:8]

        N_W = 7

        def carry(eng):
            eng.sem_inc(carried, 1)

        block = es.enter_context(nc.Block())

        @block.sync
        def _(sp):
            sp.dma_start(xT_all[:], xT).then_inc(xT_in, 16)
            sp.dma_start(cst[:], consts).then_inc(w_in, 16)
            sp.dma_start(vec[:], vecs).then_inc(w_in, 16)
            sp.dma_start(row_sb[:], rows).then_inc(w_in, 16)
            sp.dma_start(wg_sb[:], wg).then_inc(w_in, 16)
            sp.dma_start(wgp_sb[:], wgp).then_inc(w_in, 16)
            sp.dma_start(wd_sb[:], wd).then_inc(w_in, 16)
            sp.dma_start(w[:], wpack).then_inc(w_in, 16)

            def load_x(b, par, reused):
                if reused:
                    sp.wait_ge(xbo_ok, b - 1)
                    carry(sp)
                sp.dma_start(xin[par][:], x[bass.ds(b, 1)].rearrange("a s d -> (a s) d")).then_inc(x_in[par], 16)

            load_x(0, 0, False)
            load_x(1, 1, False)
            sp.dma_start(ctxf[0][:], ctxT[0]).then_inc(ctx_in[0], 16)
            sp.dma_start(ctxf[1][:], ctxT[1]).then_inc(ctx_in[1], 16)
            with sp.Fori(0, (B - 2) // 2) as i:
                for par in range(2):
                    load_x(2 * i + 2 + par, par, True)

            def stack(b, par, c, free):
                if free:
                    sp.wait_ge(t_ps, 2 * UNITS * (b - 2) + UNITS * (c + 1))
                    carry(sp)
                sp.wait_ge(kl_ok, C * b + c + 1)
                carry(sp)
                for copy, src in enumerate((kh, kh, kl)):
                    sp.dma_start(ks[par][32 * copy:32 * copy + 32, 4 * c:4 * c + 4, :].bitcast(F32),
                                 src[:, c, :].bitcast(F32)).then_inc(st_in[c][par], 16)
                sp.wait_ge(ql_ok, b + 1)
                carry(sp)
                for copy, src in enumerate((qh, ql, qh)):
                    sp.dma_start(qst[par][32 * copy:32 * copy + 32, c, 0:8 * S].bitcast(F32)
                                 .rearrange("p (j q) -> p j q", j=4),
                                 src[:, c].bitcast(F32).rearrange("p t q -> p (t q)")).then_inc(st_in[c][par], 16)

            def max_row(b, par, half):
                sp.wait_ge(mrow_ok, 2 * b + half + 1)
                carry(sp)
                sp.dma_start(qst[par][96:97, half, 0:8 * S].bitcast(F32)
                             .rearrange("p (h q) -> p h q", h=8), mrow[half][:].bitcast(F32)).then_inc(m_in[half], 16)

            def store(b, par):
                sp.wait_ge(ln3, 4 * (b + 1))
                carry(sp)
                sp.dma_start(out[bass.ds(b, 1)].rearrange("a s d -> (a s) d"), x3[par][:]).then_inc(out_done[par], 16)

            def load_ctx(b, par):
                sp.wait_ge(ctxl_ok, b - 1)
                carry(sp)
                sp.dma_start(ctxf[par][:], ctxT[bass.ds(b, 1)].rearrange("a p c s -> (a p) c s")
                             ).then_inc(ctx_in[par], 16)

            def window(b, par, cur=True, prev=True, prev2=True, nxt=True, nxt3=True):
                reused = not (isinstance(b, int) and b == 0)
                if prev:
                    max_row(b - 1, 1 - par, 1)
                if nxt:
                    stack(b + 1, 1 - par, 0, reused)
                if nxt3:
                    load_ctx(b + 3, 1 - par)
                if cur:
                    max_row(b, par, 0)
                if nxt:
                    stack(b + 1, 1 - par, 1, reused)
                if prev2:
                    store(b - 2, par)

            sp.wait_ge(zeroed, 2)
            for c in range(C):
                stack(0, 0, c, False)
            load_ctx(2, 0)
            window(0, 0, prev=False, prev2=False)
            window(1, 1, prev2=False)
            window(2, 0)
            window(3, 1)
            with sp.Fori(0, (B - 8) // 2) as i:
                for k in range(2):
                    window(2 * i + 4 + k, k)
            window(B - 4, 0)
            window(B - 3, 1, nxt3=False)
            window(B - 2, 0, nxt3=False)
            window(B - 1, 1, nxt=False, nxt3=False)
            window(B, 0, cur=False, nxt=False, nxt3=False)
            window(B + 1, 1, cur=False, prev=False, nxt=False, nxt3=False)
            sp.wait_ge(out_done[0], 16 * B // 2)
            sp.wait_ge(out_done[1], 16 * B // 2)

        @block.gpsimd
        def _(pool):
            pool.memset(ones_row[:], 1.0).then_inc(ones_ok, 1)
            pool.memset(mhalf[:], -0.5)

            def fetch_x(b, par, first):
                if first:
                    pool.wait_ge(xT_in, 16)
                else:
                    pool.wait_ge(v_ps, b - 1)
                pool.tensor_copy(xTb[par][:], xT_all[:, :, bass.ds(b * S, S)]).then_inc(xTb_ok, 1)

            def prepare_x(b, par, first):
                pool.wait_ge(x_in[par], 16 * (b // 2) + 16 if isinstance(b, int) else 8 * (b - par) + 16)
                if not first:
                    pool.wait_ge(ln1, 4 * (b - 2) + 1)
                pool.wait_ge(rows_ok, 2)
                pool.tensor_tensor(xbo[par][:], xin[par][:], ROW["bo1"][0:S], ALU.add).then_inc(xbo_ok, 1)
                if not first:
                    pool.wait_ge(mix_ok, b - 1)
                pool.wait_ge(gate_ok, C)
                pool.tensor_copy(gb[par][:], gate_all[:, :, bass.ds(b, 1)].rearrange("p c a -> p (c a)")
                                 ).then_inc(gb_ok, 1)

            def spread_keys(b, first):
                pool.wait_ge(qk_sb, 2 * C * (b + 1))
                if not first:
                    pool.wait_ge(s_ps, b)
                for c in range(C):
                    last = pool.tensor_tensor(kbd[:, c], kt[:, c:c + 1, :].broadcast_to([P, HC1, S]),
                                              quad_mask.rearrange("p (j a) -> p j a", a=1).broadcast_to([P, HC1, S]),
                                              ALU.mult)
                last.then_inc(kbd_ok, 1)

            def inv_std(n, ln, at, ve_s, rstd_s):
                pool.wait_ge(ln, at)
                carry(pool)
                pool.tensor_scalar(ve[:], mv[:, 1:2], EPS, None, ALU.add).then_inc(ve_s, 1)
                pool.wait_ge(ve_s, n + 1)
                pool.tensor_tensor(rstd[:], ve[:], mhalf[0:S], ALU.pow).then_inc(rstd_s, 1)

            def normalise(b, par):
                pool.wait_ge(rden1_ok, b + 1)
                for k in range(2):
                    hs = slice(HC1 * k, HC1 * (k + 1))
                    pool.tensor_tensor(p1[par][:, hs], p1[par][:, hs],
                                       rden1[par][:, hs].rearrange("p (h a) -> p h a", a=1).broadcast_to([S, HC1, S]),
                                       ALU.mult).then_inc(pn_ok, 1)

            def s_window(b, par, prev=True, prev2=True, nxt2=True, nxt3=True):
                if prev:
                    normalise(b - 1, 1 - par)
                if prev2:
                    inv_std(b - 2, ln1, 4 * (b - 2) + 3, ve1, rstd1)
                prepare_x(b, par, isinstance(b, int) and b < 2)
                if nxt2:
                    spread_keys(b + 2, False)
                if nxt3:
                    fetch_x(b + 3, 1 - par, False)

            fetch_x(0, 0, True)
            fetch_x(1, 1, True)
            spread_keys(0, True)
            fetch_x(2, 0, False)
            spread_keys(1, False)
            s_window(0, 0, prev=False, prev2=False)
            s_window(1, 1, prev2=False)
            with pool.Fori(0, (B - 6) // 2) as i:
                for k in range(2):
                    s_window(2 * i + 2 + k, k)
            s_window(B - 4, 0)
            s_window(B - 3, 1, nxt3=False)
            s_window(B - 2, 0, nxt2=False, nxt3=False)
            s_window(B - 1, 1, nxt2=False, nxt3=False)
            normalise(B - 1, 1)
            inv_std(B - 2, ln1, 4 * (B - 2) + 3, ve1, rstd1)
            inv_std(B - 1, ln1, 4 * (B - 1) + 3, ve1, rstd1)

            def ctx_low(b, par, first):
                pool.wait_ge(ctxh_ok, b + 1)
                pool.tensor_tensor(ctxl[:], ctxf[par][:], ctxh[:].bitcast(F32), ALU.subtract).then_inc(ctxl_ok, 1)

            def q_mask(b, first):
                pool.wait_ge(qf_ok, b + 1)
                if not first:
                    pool.wait_ge(ql_ok, b)
                    pool.wait_ge(qh_ok, b)
                for c in range(C):
                    last = pool.tensor_tensor(qm[:, c], qf[:, c:c + 1, :].broadcast_to([P, 2, S]),
                                              pair_mask.rearrange("p (t a) -> p t a", a=1).broadcast_to([P, 2, S]),
                                              ALU.mult)
                last.then_inc(qm_ok, 1)

            def q_low(b):
                pool.wait_ge(qm_ok, b + 1)
                pool.wait_ge(qh_ok, b + 1)
                pool.tensor_tensor(ql[:], qm[:], qh[:].bitcast(F32), ALU.subtract).then_inc(ql_ok, 1)

            def residual2(b, first):
                if not first:
                    pool.wait_ge(ln2, 4 * (b - 1) + 1)
                pool.tensor_tensor(xres[:], x1_all[:, bass.ds(b * D, D)], ROW["bo2"][0:S], ALU.add
                                   ).then_inc(xres_ok, 1)

            def shift(n, first):
                pool.wait_ge(x2T_ok, n + 1)
                if not first:
                    pool.wait_ge(xrk_ok, n)
                pool.tensor_tensor(dx[:], x2T[:, :, 1:1 + S], x2T[:, :, 0:S], ALU.subtract).then_inc(dx_ok, 1)

            def square(n):
                pool.wait_ge(kr_ok, n + 1)
                pool.tensor_tensor(ka[:], kr[:], kr[:], ALU.mult).then_inc(ka_ok, 1)

            def x_window(b, par, prev=True, prev2=True, nxt=True, nxt2=True):
                if prev2:
                    inv_std(b - 2, ln2, 4 * (b - 2) + 3, ve2, rstd2)
                if nxt:
                    q_mask(b + 1, False)
                    q_low(b + 1)
                if prev2:
                    shift(b - 2, isinstance(b, int) and b == 2)
                if prev:
                    residual2(b - 1, isinstance(b, int) and b == 1)
                if prev2:
                    square(b - 2)
                    inv_std(b - 2, ln3, 4 * (b - 2) + 3, ve3, rstd3)
                if nxt2:
                    ctx_low(b + 2, par, False)

            pool.wait_ge(x1_kept, B)
            ctx_low(0, 0, True)
            q_mask(0, True)
            q_low(0)
            ctx_low(1, 1, False)
            x_window(0, 0, prev=False, prev2=False)
            x_window(1, 1, prev2=False)
            x_window(2, 0)
            x_window(3, 1)
            with pool.Fori(0, (B - 8) // 2) as i:
                for k in range(2):
                    x_window(2 * i + 4 + k, k)
            x_window(B - 4, 0)
            x_window(B - 3, 1)
            x_window(B - 2, 0, nxt2=False)
            x_window(B - 1, 1, nxt=False, nxt2=False)
            x_window(B, 0, nxt=False, nxt2=False)
            x_window(B + 1, 1, prev=False, nxt=False, nxt2=False)

        @block.scalar
        def _(act):
            act.wait_ge(w_in, 16 * N_W)
            act.activation(hbg[:], vec[0:GATE, VEC["bg"]:VEC["bg"] + 1], ACT.Copy, scale=0.5).then_inc(hbg_ok, 1)
            for k in range(2):
                act.wait_ge(rows_ps, k + 1)
                act.activation(rowb[:, 2 * k:2 * k + 2].rearrange("p r d -> p (r d)"), bank[k][:, :], ACT.Copy
                               ).then_inc(rows_ok, 1)
            act.wait_ge(gate_ps, 1)
            act.wait_ge(hbg_ok, 1)
            act.activation(g1[:], bank[2][0:GATE, 0:B], ACT.Tanh, bias=hbg[:], scale=0.5 / S).then_inc(gate_t, 1)
            act.wait_ge(gate_ps2, 1)
            for c in range(C):
                act.activation(gate_all[:, c], bank[3][:, c * B:(c + 1) * B], ACT.Identity, bias=v(f"bgp_{c}")
                               ).then_inc(gate_ok, 1)

            def evac_qk(b, first):
                act.wait_ge(qk_ps, b + 1)
                if not first:
                    act.wait_ge(s_ps, b)
                    act.wait_ge(kbd_ok, b)
                for n, (dst, name) in enumerate(((qs, "bq1"), (kt, "bk1"))):
                    for c in range(C):
                        k = (n * C + c) * S
                        act.activation(dst[:, c], b_qk[:, k:k + S], ACT.Identity, bias=v(f"{name}_{c}")
                                       ).then_inc(qk_sb, 1)

            def evac_scores(b, par, first):
                for c in range(C):
                    act.wait_ge(s_ps, b + 1)
                    if not first:
                        act.wait_ge(p1_ok, b - 1)
                    act.activation(s_sb[par][:, HC1 * c:HC1 * c + HC1].rearrange("p h k -> p (h k)"),
                                   b_s[c][0:S, 0:HC1 * S], ACT.Copy).then_inc(s_ok, 1)

            def exps1(b, par, heads, first):
                act.wait_ge(negm_ok, b + 1)
                if not first:
                    act.wait_ge(p1_ok, b)
                for h in heads:
                    act.activation(e1[:, h], s_sb[par][:, h], ACT.Exp, bias=negm1[:, h:h + 1], scale=SCALE1
                                   ).then_inc(e1_ok, 1)

            def evac_pT(b, k, first):
                act.wait_ge(pT_ps, 2 * b + k + 1)
                if not first:
                    act.wait_ge(aT_ps, b)
                act.activation(pT1[:, HC1 * k:HC1 * k + HC1].rearrange("p h k -> p (h k)"),
                               b_pT[0:S, 0:HC1 * S], ACT.Copy).then_inc(pT_sb, 1)

            def evac_aT(b, first):
                act.wait_ge(aT_ps, b + 1)
                if not first:
                    act.wait_ge(mix_ok, b)
                act.activation(aT[:].rearrange("p c q -> p (c q)"), b_aT[:, 0:C * S], ACT.Copy).then_inc(aT_sb, 1)

            def evac_x1T(b):
                act.wait_ge(x1T_ps, b + 1)
                act.activation(x1T_all[:, :, bass.ds(b * S, S)], b_aT[:, 0:C * S].rearrange("p (c q) -> p c q", c=C),
                               ACT.Copy).then_inc(x1T_sb, 1)
                act.activation(x1_all[:, bass.ds(b * D, D)], x1b[:], ACT.Copy).then_inc(x1_kept, 1)

            def s_window(b, par, prev=True, prev2=True, nxt=True, nxt2=True):
                first, prev_first = (isinstance(b, int) and b == n for n in range(2))
                if nxt:
                    evac_scores(b + 1, 1 - par, first)
                if prev:
                    evac_pT(b - 1, 0, prev_first)
                exps1(b, par, range(0, HC1), first)
                if prev:
                    evac_pT(b - 1, 1, prev_first)
                exps1(b, par, range(HC1, H1), first)
                if prev:
                    evac_aT(b - 1, prev_first)
                if nxt2:
                    evac_qk(b + 2, False)
                if prev2:
                    evac_x1T(b - 2)

            evac_qk(0, True)
            evac_scores(0, 0, True)
            evac_qk(1, False)
            s_window(0, 0, prev=False, prev2=False)
            s_window(1, 1, prev2=False)
            with act.Fori(0, (B - 4) // 2) as i:
                for k in range(2):
                    s_window(2 * i + 2 + k, k)
            s_window(B - 2, 0, nxt2=False)
            s_window(B - 1, 1, nxt=False, nxt2=False)
            evac_pT(B - 1, 0, False)
            evac_pT(B - 1, 1, False)
            evac_aT(B - 1, False)
            evac_x1T(B - 2)
            evac_x1T(B - 1)

            def k_high(b, par_prev, c, first):
                act.wait_ge(k_ps, C * b + c + 1)
                if not first:
                    act.wait_ge(st_in[c][par_prev], 16 * STACK * stacked(b - 1))
                act.activation(kh[:, c], b_m[1][:, 0:SCP], ACT.Identity, bias=v(f"bk2_{c}")).then_inc(kh_ok, 1)

            def stacked(b):
                return b // 2 + 1

            def q_full(b, first):
                act.wait_ge(q_ps, b + 1)
                if not first:
                    act.wait_ge(qm_ok, b)
                for c in range(C):
                    last = act.activation(qf[:, c], b_m[1][:, c * S:(c + 1) * S], ACT.Identity, bias=v(f"bq2_{c}"))
                last.then_inc(qf_ok, 1)

            def exp2(b, u, no_slot_wait=False):
                n = 2 * UNITS * b + u
                rows_n = KC[u % 3][1]
                act.wait_ge(t_ps, n + 1)
                if not no_slot_wait:
                    act.wait_ge(pv_ok, n - SLOTS + 1)
                act.activation(pe2[0:rows_n, u % SLOTS],
                               b_t[u % NPT][0:rows_n].rearrange("p (g q) -> p g q", g=2)[:, :, 0:2 * S],
                               ACT.Exp, scale=SCALE2).then_inc(exp_ok, 1)

            def neg_max(b, half, first):
                act.wait_ge(mT_ps, 2 * b + half + 1)
                if not first:
                    act.wait_ge(m_in[half], 16 * b)
                act.activation(mrow[half][:], b_m[1][0:8, 0:S], ACT.Copy, scale=-1.0).then_inc(mrow_ok, 1)

            def out_T(b, first):
                act.wait_ge(pv_ok, 2 * UNITS * (b + 1))
                if not first:
                    act.wait_ge(ot_ps, b)
                act.activation(oT[:].rearrange("p h q -> p (h q)"), b_o[:, 0:4 * S], ACT.Copy).then_inc(oT_ok, 1)

            def att_T(b, first):
                act.wait_ge(at_ps, b + 1)
                if not first:
                    act.wait_ge(y2_ps, b)
                act.activation(attT[:].rearrange("p c q -> p (c q)"), b_m[0][:, 0:C * S], ACT.Copy).then_inc(attT_ok, 1)

            def ffn_T(n, first):
                act.wait_ge(x2T_ps, n + 1)
                if first:
                    act.wait_ge(zeroed, 1)
                else:
                    act.wait_ge(xrk_ok, n)
                act.activation(x2T[:, :, 1:1 + S], b_m[0][:, 0:C * S].rearrange("p (c q) -> p c q", c=C),
                               ACT.Copy).then_inc(x2T_ok, 1)

            def ffn_rk(n, first):
                act.wait_ge(kf_ps, n + 1)
                if not first:
                    act.wait_ge(sg_ok, n)
                act.activation(th[:], b_m[0][0:S, 0:D], ACT.Tanh, scale=0.5).then_inc(th_ok, 1)
                if not first:
                    act.wait_ge(ka_ok, n)
                act.activation(kr[:].rearrange("p c q -> p (c q)"), b_m[0][:, D:D + C * S], ACT.Relu
                               ).then_inc(kr_ok, 1)

            def x_window(b, par, cur=True, prev=True, prev2=True, nxt=True):
                cur_first, prev_first, prev2_first = (isinstance(b, int) and b == n for n in range(3))
                if prev:
                    exp2(b - 1, 3, prev_first)
                    neg_max(b - 1, 1, prev_first)
                    exp2(b - 1, 4, prev_first)
                if nxt:
                    q_full(b + 1, False)
                if prev:
                    exp2(b - 1, 5, prev_first)
                if nxt:
                    k_high(b + 1, par, 0, False)
                if prev:
                    exp2(b - 1, 6)
                if prev2:
                    ffn_T(b - 2, prev2_first)
                if prev:
                    exp2(b - 1, 7)
                    exp2(b - 1, 8)
                if nxt:
                    k_high(b + 1, par, 1, False)
                if prev2:
                    ffn_rk(b - 2, prev2_first)
                if prev:
                    exp2(b - 1, 9)
                if cur:
                    neg_max(b, 0, cur_first)
                if prev:
                    exp2(b - 1, 10)
                    exp2(b - 1, 11)
                    out_T(b - 1, prev_first)
                if cur:
                    exp2(b, 0, cur_first)
                    exp2(b, 1, cur_first)
                    exp2(b, 2, cur_first)
                if prev:
                    att_T(b - 1, prev_first)

            k_high(0, None, 0, True)
            k_high(0, None, 1, True)
            q_full(0, True)
            x_window(0, 0, prev=False, prev2=False)
            x_window(1, 1, prev2=False)
            x_window(2, 0)
            x_window(3, 1)
            with act.Fori(0, (B - 8) // 2) as i:
                for k in range(2):
                    x_window(2 * i + 4 + k, k)
            x_window(B - 4, 0)
            x_window(B - 3, 1)
            x_window(B - 2, 0)
            x_window(B - 1, 1, nxt=False)
            x_window(B, 0, cur=False, nxt=False)
            x_window(B + 1, 1, cur=False, prev=False, nxt=False)

        @block.tensor
        def _(pe):
            pe.wait_ge(ones_ok, 1)
            pe.wait_ge(w_in, 16 * N_W)
            for k in range(2):
                pe.matmul(bank[k][:, :], ones_row[:], row_sb[:, k * 512:(k + 1) * 512], start=True, stop=True
                          ).then_inc(rows_ps, 1)
            pe.wait_ge(xsum_ok, 1)
            for c in range(C):
                last = pe.matmul(bank[2][0:GATE, 0:B], wg_sb[:, c], xsum[:, c], start=(c == 0), stop=(c == C - 1))
            last.then_inc(gate_ps, 1)
            pe.wait_ge(gate_u, 1)
            for c in range(C):
                last = pe.matmul(bank[3][:, c * B:(c + 1) * B], wgp_sb[:, c * P:(c + 1) * P], g1s[:],
                                 start=True, stop=True)
            last.then_inc(gate_ps2, 1)
            pe.wait_ge(rows_ok, 2)
            pe.wait_ge(gate_ok, C)

            def project_qk(b, par, n, first):
                if not first:
                    pe.wait_ge(qk_sb, 2 * C * b)
                pe.wait_ge(xTb_ok, b + 1)
                for c in range(C):
                    o = b_qk[:, (n * C + c) * S:(n * C + c + 1) * S]
                    for i in range(C):
                        last = pe.matmul(o, W[("q1", "k1")[n]][:, i, c * P:(c + 1) * P], xTb[par][:, i],
                                         start=(i == 0), stop=(i == C - 1))
                if n == 1:
                    last.then_inc(qk_ps, 1)

            def project_v(b, par, first):
                if not first:
                    pe.wait_ge(v_sb, b)
                for i in range(C):
                    last = pe.matmul(b_v[0:S, 0:D], xTb[par][:, i], W["v1"][:, i], start=(i == 0), stop=(i == C - 1))
                last.then_inc(v_ps, 1)

            def scores(b, first):
                pe.wait_ge(qk_sb, 2 * C * (b + 1))
                pe.wait_ge(kbd_ok, b + 1)
                if not first:
                    pe.wait_ge(s_ok, 2 * b)
                for c in range(C):
                    last = pe.matmul(b_s[c][0:S, 0:HC1 * S], qs[:, c], kbd[:, c].rearrange("p h k -> p (h k)"),
                                     start=True, stop=True)
                last.then_inc(s_ps, 1)

            def turn_probs(b, par, k, first):
                pe.wait_ge(pn_ok, 2 * b + k + 1)
                if not first:
                    pe.wait_ge(pT_sb, 2 * b + k)
                for h in range(HC1 * k, HC1 * k + HC1):
                    last = pe.transpose(b_pT[0:S, (h % HC1) * S:(h % HC1 + 1) * S], p1[par][:, h], ident[0:S, 0:S])
                last.then_inc(pT_ps, 1)

            def mix_values(b, par):
                pe.wait_ge(pT_sb, 2 * b + 2)
                pe.wait_ge(v_sb, b + 1)
                if not (isinstance(b, int) and b < 2):
                    pe.wait_ge(x1T_sb, b - 1)
                for h in range(H1):
                    j, c = h % HC1, h // HC1
                    last = pe.matmul(b_aT[DH1 * j:DH1 * (j + 1), c * S:(c + 1) * S],
                                     v1[par][:, DH1 * h:DH1 * (h + 1)], pT1[:, h], start=True, stop=True)
                last.then_inc(aT_ps, 1)

            def distil(b, first):
                pe.wait_ge(aT_sb, b + 1)
                if not first:
                    pe.wait_ge(dmix_ok, b)
                pe.matmul(b_d[:, 0:C * S], wd_sb[:], aT[:].rearrange("p c q -> p (c q)"), start=True, stop=True
                          ).then_inc(d_ps, 1)

            def out1(b, first):
                pe.wait_ge(mix_ok, b + 1)
                if not first:
                    pe.wait_ge(ln1, 4 * (b - 1) + 1)
                for c in range(C):
                    last = pe.matmul(b_y[0:S, 0:D], mixT[:, c], W["o1"][:, c], start=(c == 0), stop=(c == C - 1))
                last.then_inc(y1_ps, 1)

            def turn_x1(b, at):
                pe.wait_ge(ln1, 4 * (b + 1))
                pe.wait_ge(aT_sb, at)
                for c in range(C):
                    last = pe.transpose(b_aT[:, c * S:(c + 1) * S], x1b[:, c * P:(c + 1) * P], ident[0:S, 0:S])
                last.then_inc(x1T_ps, 1)

            def s_window(b, par, prev=True, prev2=True, nxt=True, nxt2=True):
                q = 1 - par
                prev_first = isinstance(b, int) and b == 1
                if nxt:
                    scores(b + 1, False)
                if prev:
                    turn_probs(b - 1, q, 0, prev_first)
                if nxt2:
                    project_qk(b + 2, par, 0, False)
                if prev:
                    turn_probs(b - 1, q, 1, False)
                if nxt2:
                    project_qk(b + 2, par, 1, False)
                if prev:
                    mix_values(b - 1, q)
                    distil(b - 1, prev_first)
                if nxt2:
                    project_v(b + 2, par, False)
                if prev:
                    out1(b - 1, prev_first)
                if prev2:
                    turn_x1(b - 2, b)

            project_qk(0, 0, 0, True)
            project_qk(0, 0, 1, True)
            project_v(0, 0, True)
            scores(0, True)
            project_qk(1, 1, 0, False)
            project_qk(1, 1, 1, False)
            project_v(1, 1, False)
            s_window(0, 0, prev=False, prev2=False)
            s_window(1, 1, prev2=False)
            with pe.Fori(0, (B - 4) // 2) as i:
                for k in range(2):
                    s_window(2 * i + 2 + k, k)
            s_window(B - 2, 0, nxt2=False)
            s_window(B - 1, 1, nxt=False, nxt2=False)
            turn_probs(B - 1, 1, 0, False)
            turn_probs(B - 1, 1, 1, False)
            mix_values(B - 1, 1)
            distil(B - 1, False)
            out1(B - 1, False)
            turn_x1(B - 2, B)
            pe.wait_ge(x1T_sb, B - 1)
            turn_x1(B - 1, B)

            def split_product(o, pairs):
                todo = [(a, m) for wh, wl, xh, xl in pairs for a, m in ((wh, xh), (wh, xl), (wl, xh))]
                for n, (a, m) in enumerate(todo):
                    last = pe.matmul(o, a, m, start=(n == 0), stop=(n == len(todo) - 1))
                return last

            def proj_k(b, c, wait):
                if c == 0:
                    pe.wait_ge(ctxl_ok, b + 1)
                for s_, n_ in wait:
                    pe.wait_ge(s_, n_)
                co = slice(c * P, (c + 1) * P)
                split_product(b_m[1][:, 0:SCP], [(wkh[:, i, co], wkl[:, i, co], ctxh[:, i], ctxl[:, i])
                                                 for i in range(C)]).then_inc(k_ps, 1)

            def proj_v(b, part, wait):
                for s_, n_ in wait:
                    pe.wait_ge(s_, n_)
                for kc in ((0, 1), (2,))[part]:
                    k0, n = KC[kc]
                    o = b_m[1][0:n, (kc % 2) * D:(kc % 2 + 1) * D]
                    last = split_product(o, [(ctxh[:, i, k0:k0 + n], ctxl[:, i, k0:k0 + n], wvh[:, i], wvl[:, i])
                                             for i in range(C)])
                last.then_inc(v2_ps, 1)

            def head_max(b, par, h, first=False):
                n = H2 * b + h
                if h % 8 == 0:
                    pe.wait_ge(st_in[h // 8][par], 16 * STACK * (b // 2 + 1))
                at = (h + par) % NMX
                if h >= NMX:
                    pe.wait_ge(max_ok, n - NMX + 1)
                elif not first:
                    before = max(g for g in range(H2) if (g + 1 - par) % NMX == at)
                    pe.wait_ge(max_ok, H2 * (b - 1) + before + 1)
                pe.matmul(b_max[at][0:S, 0:SCP], qst[par][0:96, h // 8, (h % 8) * S:(h % 8 + 1) * S],
                          ks[par][0:96, h // 2, :], start=True, stop=True).then_inc(max_ps, 1)

            def turn_max(b, par, half, wait):
                pe.wait_ge(max_ok, H2 * b + 8 * half + 8)
                for s_, n_ in wait:
                    pe.wait_ge(s_, n_)
                pe.transpose(b_m[1][0:8, 0:S], m2[par][:, 8 * half:8 * half + 8], ident[0:S, 0:S]).then_inc(mT_ps, 1)

            def t_unit(b, par, u, first=False):
                n = 2 * UNITS * b + u
                gp, (k0, kn) = u // 3, KC[u % 3]
                if u % UNITS == 0:
                    pe.wait_ge(m_in[u // UNITS], 16 * (b + 1))
                if not (first and u < NPT):
                    pe.wait_ge(exp_ok, n - NPT + 1)
                for i in range(2):
                    g = 2 * gp + i
                    last = pe.matmul(b_t[u % NPT][0:kn, i * D:(i + 1) * D], ks[par][:, g, k0:k0 + kn],
                                     qst[par][:, g // 4, (g % 4) * 2 * S:(g % 4) * 2 * S + D],
                                     start=True, stop=True)
                last.then_inc(t_ps, 1)

            def pv_unit(b, par, u, first=False):
                n = 2 * UNITS * b + u
                gp, kc = u // 3, u % 3
                kn = KC[kc][1]
                pe.wait_ge(exp_ok, n + 1)
                if u == 0:
                    pe.wait_ge(v2_sb, 3 * (b + 1))
                    if not first:
                        pe.wait_ge(oT_ok, b)
                for j in range(4):
                    last = pe.matmul(b_o[VW * j:VW * (j + 1), gp * S:(gp + 1) * S], vx[par][0:kn, kc, 4 * gp + j],
                                     pe2[0:kn, u % SLOTS].rearrange("p g q -> p (g q)")[:, j * S:(j + 1) * S],
                                     start=(u == 0), stop=(u == 2 * UNITS - 1), skip_group_check=True)
                last.then_inc(pv_ok, 1)

            def proj_q(b, wait):
                for s_, n_ in wait:
                    pe.wait_ge(s_, n_)
                for c in range(C):
                    for i in range(C):
                        last = pe.matmul(b_m[1][:, c * S:(c + 1) * S], W["q2"][:, i, c * P:(c + 1) * P],
                                         x1T_all[:, i, bass.ds(b * S, S)], start=(i == 0), stop=(i == C - 1))
                last.then_inc(q_ps, 1)

            def turn_out(b, wait):
                pe.wait_ge(oT_ok, b + 1)
                for s_, n_ in wait:
                    pe.wait_ge(s_, n_)
                for k in range(4):
                    last = pe.transpose(b_m[0][0:S, k * P:(k + 1) * P], oT[:, k], ident)
                last.then_inc(ot_ps, 1)

            def turn_att(b):
                pe.wait_ge(att_ok, b + 1)
                av = att[:].rearrange("p h d -> p (h d)")
                for c in range(C):
                    last = pe.transpose(b_m[0][:, c * S:(c + 1) * S], av[:, c * P:(c + 1) * P], ident[0:S, 0:S])
                last.then_inc(at_ps, 1)

            def out2(b, wait):
                pe.wait_ge(attT_ok, b + 1)
                for s_, n_ in wait:
                    pe.wait_ge(s_, n_)
                for c in range(C):
                    last = pe.matmul(b_m[0][0:S, 0:D], attT[:, c], W["o2"][:, c], start=(c == 0), stop=(c == C - 1))
                last.then_inc(y2_ps, 1)

            def turn_x2(n, wait):
                pe.wait_ge(ln2, 4 * (n + 1))
                for s_, n_ in wait:
                    pe.wait_ge(s_, n_)
                for c in range(C):
                    last = pe.transpose(b_m[0][:, c * S:(c + 1) * S], x2[:, c * P:(c + 1) * P], ident[0:S, 0:S])
                last.then_inc(x2T_ps, 1)

            def ffn_in(n, wait):
                pe.wait_ge(xrk_ok, n + 1)
                for s_, n_ in wait:
                    pe.wait_ge(s_, n_)
                for i in range(C):
                    pe.matmul(b_m[0][0:S, 0:D], xr[:, i], W["r"][:, i], start=(i == 0), stop=(i == C - 1))
                for c in range(C):
                    for i in range(C):
                        last = pe.matmul(b_m[0][:, D + c * S:D + (c + 1) * S], W["k"][:, i, c * P:(c + 1) * P],
                                         xk[:, i], start=(i == 0), stop=(i == C - 1))
                last.then_inc(kf_ps, 1)

            def ffn_out(n):
                pe.wait_ge(ka_ok, n + 1)
                for i in range(C):
                    last = pe.matmul(b_m[0][0:S, 0:D], ka[:, i], W["v"][:, i], start=(i == 0), stop=(i == C - 1))
                last.then_inc(f_ps, 1)

            def x_window(b, par, cur=True, prev=True, prev2=True, nxt=True):
                first, prev_first = (isinstance(b, int) and b == n for n in range(2))
                q = 1 - par
                if cur:
                    head_max(b, par, 0, first)
                if prev:
                    turn_max(b - 1, q, 1, [(v2_sb, 3 * (b + 1))] if cur else [(mrow_ok, 2 * b - 1)])
                    pv_unit(b - 1, q, 3)
                if cur:
                    head_max(b, par, 1, first)
                if prev:
                    t_unit(b - 1, q, 4)
                if nxt:
                    proj_q(b + 1, [(mrow_ok, 2 * b)] if not first else [(qf_ok, 1)])
                if cur:
                    head_max(b, par, 2, first)
                if prev:
                    t_unit(b - 1, q, 5)
                    pv_unit(b - 1, q, 4)
                if cur:
                    head_max(b, par, 3, first)
                if nxt:
                    proj_k(b + 1, 0, [(qf_ok, b + 2)])
                if prev:
                    pv_unit(b - 1, q, 5)
                if cur:
                    head_max(b, par, 4)
                if prev:
                    t_unit(b - 1, q, 6)
                if prev2:
                    turn_x2(b - 2, [])
                if cur:
                    head_max(b, par, 5)
                if prev:
                    t_unit(b - 1, q, 7)
                    pv_unit(b - 1, q, 6)
                if cur:
                    head_max(b, par, 6)
                if prev:
                    t_unit(b - 1, q, 8)
                    pv_unit(b - 1, q, 7)
                if nxt:
                    proj_k(b + 1, 1, [(kl_ok, C * (b + 1) + 1)])
                if cur:
                    head_max(b, par, 7)
                if prev:
                    pv_unit(b - 1, q, 8)
                if prev2:
                    ffn_in(b - 2, [])
                if cur:
                    head_max(b, par, 8)
                if prev:
                    t_unit(b - 1, q, 9)
                if cur:
                    turn_max(b, par, 0, [(kl_ok, C * (b + 2))] if nxt else [(mrow_ok, 2 * b)])
                    head_max(b, par, 9)
                if prev:
                    t_unit(b - 1, q, 10)
                    pv_unit(b - 1, q, 9)
                if cur:
                    head_max(b, par, 10)
                if prev2:
                    ffn_out(b - 2)
                if prev:
                    t_unit(b - 1, q, 11)
                    pv_unit(b - 1, q, 10)
                if cur:
                    head_max(b, par, 11)
                if prev:
                    pv_unit(b - 1, q, 11)
                if nxt:
                    proj_v(b + 1, 0, [(mrow_ok, 2 * b + 1)])
                if cur:
                    head_max(b, par, 12)
                    t_unit(b, par, 0, first)
                if prev:
                    turn_out(b - 1, [(rv_ok, b - 1)] if prev2 else [])
                if cur:
                    head_max(b, par, 13)
                    t_unit(b, par, 1, first)
                    pv_unit(b, par, 0, first)
                if nxt:
                    proj_v(b + 1, 1, [(v2_sb, 3 * (b + 1) + 2)])
                if cur:
                    head_max(b, par, 14)
                    t_unit(b, par, 2)
                if prev:
                    turn_att(b - 1)
                if cur:
                    pv_unit(b, par, 1)
                    head_max(b, par, 15)
                    t_unit(b, par, 3)
                    pv_unit(b, par, 2)
                if prev:
                    out2(b - 1, [])

            pe.wait_ge(x1T_sb, B)
            pe.wait_ge(wsplit, 4)
            pe.wait_ge(zeroed, 2)
            pe.wait_ge(ln1, 4 * B)
            proj_k(0, 0, [])
            proj_k(0, 1, [(kl_ok, 1)])
            proj_v(0, 0, [(kl_ok, 2)])
            proj_v(0, 1, [(v2_sb, 2)])
            proj_q(0, [(v2_sb, 3)])
            x_window(0, 0, prev=False, prev2=False)
            x_window(1, 1, prev2=False)
            x_window(2, 0)
            x_window(3, 1)
            with pe.Fori(0, (B - 8) // 2) as i:
                for k in range(2):
                    x_window(2 * i + 4 + k, k)
            x_window(B - 4, 0)
            x_window(B - 3, 1)
            x_window(B - 2, 0)
            x_window(B - 1, 1, nxt=False)
            x_window(B, 0, cur=False, nxt=False)
            x_window(B + 1, 1, cur=False, prev=False, nxt=False)

        @block.vector
        def _(dve):
            for t in range(2):
                dve.memset(vx[t][:], 1.0)
                dve.memset(qst[t][:].bitcast(F32), 0.0)
                dve.memset(ks[t][96:128].bitcast(F32), 0.0)
            dve.memset(x2T[:], 0.0).then_inc(zeroed, 1)
            dve.wait_ge(zeroed, 1)
            for t in range(2):
                last = dve.memset(ks[t][96:97].bitcast(F32), 1.0)
            last.then_inc(zeroed, 1)
            dve.wait_ge(xT_in, 16)
            for c in range(C):
                last = dve.tensor_reduce(xsum[:, c], xT_all[:, c].rearrange("p (b s) -> p b s", s=S), AX.X, ALU.add)
            last.then_inc(xsum_ok, 1)
            dve.wait_ge(gate_t, 1)
            dve.tensor_scalar(g1s[:], g1[:], 0.5, 0.5, ALU.mult, ALU.add).then_inc(gate_u, 1)
            dve.wait_ge(rows_ok, 2)
            dve.wait_ge(zeroed, 2)

            def values(b, par):
                dve.wait_ge(v_ps, b + 1)
                if not (isinstance(b, int) and b < 2):
                    dve.wait_ge(aT_ps, b - 1)
                dve.tensor_tensor(v1[par][:], b_v[0:S, 0:D], ROW["bv1"][0:S], ALU.add).then_inc(v_sb, 1)

            def distilled(b, par):
                dve.wait_ge(d_ps, b + 1)
                dve.scalar_tensor_tensor(dmix[:].rearrange("p c q -> p (c q)"), b_d[:, 0:C * S], v("bd"),
                                         aT[:].rearrange("p c q -> p (c q)"), ALU.add, ALU.subtract
                                         ).then_inc(dmix_ok, 1)
                dve.wait_ge(dmix_ok, b + 1)
                dve.wait_ge(gb_ok, b + 1)
                if not (isinstance(b, int) and b == 0):
                    dve.wait_ge(y1_ps, b)
                for c in range(C):
                    last = dve.scalar_tensor_tensor(mixT[:, c], dmix[:, c], gb[par][:, c:c + 1], aT[:, c],
                                                    ALU.mult, ALU.add)
                last.then_inc(mix_ok, 1)

            def stats(n, ln, y):
                dve.wait_ge(ln, 4 * n + 1)
                dve.bn_stats(st[:], y[:]).then_inc(ln, 1)
                dve.wait_ge(ln, 4 * n + 2)
                carry(dve)
                dve.bn_aggr(mv[:], st[:]).then_inc(ln, 1)

            def norm(n, ln, rstd_s, y, dst):
                dve.wait_ge(ln, 4 * n + 3)
                dve.wait_ge(rstd_s, n + 1)
                return dve.tensor_scalar(dst, y[:], mv[:, 0:1], rstd[:], ALU.subtract, ALU.mult)

            def residual1(b, par):
                dve.wait_ge(y1_ps, b + 1)
                dve.wait_ge(xbo_ok, b + 1)
                dve.tensor_tensor(y1[:], b_y[0:S, 0:D], xbo[par][:], ALU.add).then_inc(ln1, 1)
                stats(b, ln1, y1)

            def norm1(b):
                if not (isinstance(b, int) and b == 0):
                    dve.wait_ge(x1T_ps, b)
                    dve.wait_ge(x1_kept, b)
                norm(b, ln1, rstd1, y1, x1b[:]).then_inc(ln1, 1)

            def s_window(b, par, prev=True, prev2=True, nxt=True):
                first = isinstance(b, int) and b == 0
                q = 1 - par
                dve.wait_ge(s_ok, 2 * b + 2)
                carry(dve)
                for h in range(H1):
                    last = dve.max(top1[:, h], s_sb[par][:, h])
                last.then_inc(top1_ok, 1)
                dve.wait_ge(top1_ok, b + 1)
                if not first:
                    dve.wait_ge(e1_ok, H1 * b)
                dve.tensor_scalar(negm1[:], top1[:, :, 0], -SCALE1, None, ALU.mult).then_inc(negm_ok, 1)
                for h in range(H1):
                    last = dve.match_replace(rest[:, h], top1[:, h], s_sb[par][:, h], -3.0e38)
                last.then_inc(rest_ok, 1)
                dve.wait_ge(rest_ok, b + 1)
                carry(dve)
                for h in range(H1):
                    last = dve.max(top2[:, h], rest[:, h])
                last.then_inc(top2_ok, 1)
                if prev2:
                    norm1(b - 2)
                if nxt:
                    values(b + 1, q)
                if prev:
                    distilled(b - 1, q)
                dve.wait_ge(top2_ok, b + 1)
                dve.wait_ge(e1_ok, H1 * (b + 1))
                if not (isinstance(b, int) and b < 2):
                    dve.wait_ge(pT_ps, 2 * (b - 1))
                for h in range(H1):
                    last = dve.scalar_tensor_tensor(p1[par][:, h], s_sb[par][:, h],
                                                    top2[:, h, TOPK - 9:TOPK - 8], e1[:, h],
                                                    ALU.is_ge, ALU.mult, accum_out=den1[:, h:h + 1])
                last.then_inc(p1_ok, 1)
                dve.wait_ge(p1_ok, b + 1)
                dve.reciprocal(rden1[par][:], den1[:]).then_inc(rden1_ok, 1)
                if prev:
                    residual1(b - 1, q)

            values(0, 0)
            s_window(0, 0, prev=False, prev2=False)
            s_window(1, 1, prev2=False)
            with dve.Fori(0, (B - 4) // 2) as i:
                for k in range(2):
                    s_window(2 * i + 2 + k, k)
            s_window(B - 2, 0)
            dve.wait_ge(w_in, 16 * N_W)
            for hi, src in ((wkh, W["k2"]), (wvh, W["v2"])):
                dve.tensor_copy(hi[:], src).then_inc(wsplit, 1)
            dve.wait_ge(wsplit, 2)
            for hi, lo, src in ((wkh, wkl, W["k2"]), (wvh, wvl, W["v2"])):
                dve.tensor_tensor(lo[:], src, hi[:].bitcast(F32), ALU.subtract).then_inc(wsplit, 1)
            s_window(B - 1, 1, nxt=False)
            norm1(B - 2)
            distilled(B - 1, 1)
            residual1(B - 1, 1)
            norm1(B - 1)

            def ctx_high(b, par, reuse):
                dve.wait_ge(ctx_in[par], 16 * (b // 2 + 1))
                if reuse:
                    dve.wait_ge(v2_ps, 2 * b)
                dve.tensor_copy(ctxh[:], ctxf[par][:]).then_inc(ctxh_ok, 1)

            def k_low(b, c):
                dve.wait_ge(kh_ok, C * b + c + 1)
                dve.scalar_tensor_tensor(kl[:, c], b_m[1][:, 0:SCP], v(f"bk2_{c}"), kh[:, c].bitcast(F32),
                                         ALU.add, ALU.subtract).then_inc(kl_ok, 1)

            def values2(b, par, part, reuse):
                dve.wait_ge(v2_ps, 2 * b + part + 1)
                if reuse:
                    dve.wait_ge(pv_ok, 2 * UNITS * (b - 1))
                for kc in ((0, 1), (2,))[part]:
                    n = KC[kc][1]
                    dve.tensor_tensor(vx[par][0:n, kc, :, 0:DH2],
                                      b_m[1][0:n, (kc % 2) * D:(kc % 2 + 1) * D].rearrange("p (h d) -> p h d", d=DH2),
                                      ROW["bv2"][0:n].rearrange("p (h d) -> p h d", d=DH2), ALU.add
                                      ).then_inc(v2_sb, 1)

            def q_high(b, par_prev, first):
                dve.wait_ge(qm_ok, b + 1)
                if not first:
                    for c in range(C):
                        dve.wait_ge(st_in[c][par_prev], 16 * STACK * ((b - 1) // 2 + 1))
                dve.tensor_copy(qh[:], qm[:]).then_inc(qh_ok, 1)

            def head_max(b, par, h, first):
                n = H2 * b + h
                dve.wait_ge(max_ps, n + 1)
                if h == 0 and not first:
                    dve.wait_ge(mT_ps, 2 * (b - 1))
                dve.tensor_reduce(m2[par][:, h:h + 1], b_max[(h + par) % NMX][0:S, 0:SC], AX.X, ALU.max).then_inc(max_ok, 1)

            def attention(b):
                dve.wait_ge(ot_ps, b + 1)
                ov = b_m[0][0:S, :].rearrange("p (h e) -> p h e", e=VW)
                dve.reciprocal(rden2[:], ov[:, :, DH2]).then_inc(rden2_ok, 1)
                dve.wait_ge(rden2_ok, b + 1)
                if not (isinstance(b, int) and b == 0):
                    dve.wait_ge(at_ps, b)
                dve.tensor_tensor(att[:], ov[:, :, 0:DH2],
                                  rden2[:].rearrange("p (h a) -> p h a", a=1).broadcast_to([S, H2, DH2]),
                                  ALU.mult).then_inc(att_ok, 1)

            def residual2(b):
                dve.wait_ge(y2_ps, b + 1)
                dve.wait_ge(xres_ok, b + 1)
                dve.tensor_tensor(y2[:], b_m[0][0:S, 0:D], xres[:], ALU.add).then_inc(ln2, 1)
                stats(b, ln2, y2)

            def norm2(b):
                if not (isinstance(b, int) and b == 0):
                    dve.wait_ge(x2T_ps, b)
                norm(b, ln2, rstd2, y2, x2[:]).then_inc(ln2, 1)

            def shift_mix(n):
                dve.wait_ge(dx_ok, n + 1)
                if not (isinstance(n, int) and n == 0):
                    dve.wait_ge(kf_ps, n)
                for c in range(C):
                    dve.scalar_tensor_tensor(xr[:, c], dx[:, c], v(f"mur_{c}"), x2T[:, c, 0:S], ALU.mult, ALU.add)
                    last = dve.scalar_tensor_tensor(xk[:, c], dx[:, c], v(f"muk_{c}"), x2T[:, c, 0:S],
                                                    ALU.mult, ALU.add)
                last.then_inc(xrk_ok, 1)

            def sigmoid_r(n):
                dve.wait_ge(th_ok, n + 1)
                dve.tensor_scalar(sg[:], th[:], 0.5, 0.5, ALU.mult, ALU.add).then_inc(sg_ok, 1)

            def residual3(n):
                dve.wait_ge(f_ps, n + 1)
                dve.wait_ge(sg_ok, n + 1)
                dve.tensor_tensor(rv[:], b_m[0][0:S, 0:D], sg[:], ALU.mult).then_inc(rv_ok, 1)
                dve.wait_ge(rv_ok, n + 1)
                dve.tensor_tensor(y3[:], rv[:], x2[:], ALU.add).then_inc(ln3, 1)
                stats(n, ln3, y3)

            def norm3(n, par):
                if not (isinstance(n, int) and n < 2):
                    dve.wait_ge(out_done[par], 16 * (n // 2))
                norm(n, ln3, rstd3, y3, x3[par][:]).then_inc(ln3, 1)

            def x_window(b, par, cur=True, prev=True, prev2=True, nxt=True, nxt2=True):
                fm = isinstance(b, int) and b < 2
                q = 1 - par

                def heads(*hs):
                    if cur:
                        for h in hs:
                            head_max(b, par, h, fm)
                heads(0)
                if prev2:
                    residual2(b - 2)
                heads(1, 2)
                if prev2:
                    norm2(b - 2)
                heads(3, 4)
                if nxt:
                    q_high(b + 1, par, False)
                heads(5)
                if nxt:
                    k_low(b + 1, 0)
                heads(6)
                if prev2:
                    shift_mix(b - 2)
                heads(7, 8)
                if nxt:
                    k_low(b + 1, 1)
                heads(9, 10)
                if prev2:
                    sigmoid_r(b - 2)
                heads(11)
                if prev2:
                    residual3(b - 2)
                heads(12)
                if nxt:
                    values2(b + 1, q, 0, not (isinstance(b, int) and b < 1))
                if prev:
                    attention(b - 1)
                heads(13)
                if prev2:
                    norm3(b - 2, par)
                heads(14)
                if nxt:
                    values2(b + 1, q, 1, not (isinstance(b, int) and b < 1))
                if nxt2:
                    ctx_high(b + 2, par, True)
                heads(15)

            ctx_high(0, 0, False)
            k_low(0, 0)
            k_low(0, 1)
            values2(0, 0, 0, False)
            values2(0, 0, 1, False)
            q_high(0, None, True)
            ctx_high(1, 1, True)
            x_window(0, 0, prev=False, prev2=False)
            x_window(1, 1, prev2=False)
            x_window(2, 0)
            x_window(3, 1)
            with dve.Fori(0, (B - 8) // 2) as i:
                for k in range(2):
                    x_window(2 * i + 4 + k, k)
            x_window(B - 4, 0)
            x_window(B - 3, 1)
            x_window(B - 2, 0, nxt2=False)
            x_window(B - 1, 1, nxt=False, nxt2=False)
            x_window(B, 0, cur=False, nxt=False, nxt2=False)
            x_window(B + 1, 1, cur=False, prev=False, nxt=False, nxt2=False)


def kernel(**inputs):
    import numpy as np
    import concourse.bacc as bacc
    from concourse.bass_utils import run_bass_kernel_spmd

    a = {k: np.asarray(v_) for k, v_ in inputs.items()}

    def chunks(m):
        return m.reshape(C, P, -1).transpose(1, 0, 2)

    order = np.arange(D).reshape(C, 4, 32).transpose(0, 2, 1).reshape(D)
    wkv = a["L0_xattn_Wkv"].reshape(D, D, 2)
    mats = [a["L0_attn_Wq"].T, a["L0_attn_Wk"].T, a["L0_attn_Wv"].T, a["L0_attn_Wo"].T,
            a["L0_xattn_Wq"][:, order], wkv[:, order, 0], wkv[:, :, 1], a["L0_xattn_Wout"],
            a["L0_ffn_W_r"].T, a["L0_ffn_W_k"].T, a["L0_ffn_W_v"].T]
    wpack = np.stack([chunks(m) for m in mats], axis=1)
    bkv = a["L0_xattn_bkv"].reshape(D, 2)
    cols = [a["L0_attn_bq"], a["L0_attn_bk"], a["L0_xattn_bq"][order], bkv[order, 0],
            a["L0_ffn_mu_r"], a["L0_ffn_mu_k"], a["L0_attn_bgp"]]
    vecs = np.zeros((P, NVEC), np.float32)
    for i, m in enumerate(cols):
        vecs[:, 2 * i:2 * i + 2] = m.reshape(C, P).T
    vecs[:, VEC["bd"]] = np.concatenate([a["L0_attn_bd"]] * (P // GATE))
    vecs[0:GATE, VEC["bg"]] = a["L0_attn_bg"]
    rows = np.concatenate([a["L0_attn_bv"], a["L0_attn_bo"], bkv[:, 1], a["L0_xattn_bout"]]).reshape(1, 4 * D)
    wd = np.zeros((P, P), np.float32)
    for i in range(P // GATE):
        wd[i * GATE:(i + 1) * GATE, i * GATE:(i + 1) * GATE] = a["L0_attn_Wd"].T
    part = np.arange(P)
    consts = np.concatenate([np.eye(P), part[:, None] // DH1 == np.arange(HC1),
                             part[:, None] // (P // 2) == np.arange(2)], axis=1).astype(np.float32)
    xT = a["x"].reshape(B * S, C, P).transpose(2, 1, 0)
    ctxT = np.zeros((B, P, C, SCP), np.float32)
    ctxT[:, :, :, 0:SC] = a["ctx_1024"].reshape(B, SC, C, P).transpose(0, 3, 2, 1)
    arrays = {"x": a["x"], "xT": xT, "ctxT": ctxT, "wpack": wpack, "vecs": vecs, "rows": rows, "wd": wd,
              "wg": chunks(a["L0_attn_Wg"].T), "wgp": a["L0_attn_Wgp"].T, "consts": consts}
    nc = bacc.Bacc("TRN2", target_bir_lowering=False, num_devices=1)
    arrays = {f"in_{k}": np.ascontiguousarray(m) for k, m in arrays.items()}
    args = [nc.dram_tensor(k, m.shape, mybir.dt.from_np(m.dtype), kind="ExternalInput").ap()
            for k, m in arrays.items()]
    out = nc.dram_tensor("out_0", (B, S, D), F32, kind="ExternalOutput").ap()
    decoder_layer(nc, *args, out)
    r = run_bass_kernel_spmd(nc, [arrays], core_ids=[0])
    return r.results[0]["out_0"]
```

```python
import concourse.bass as bass
from concourse import mybir
from contextlib import ExitStack

F32 = mybir.dt.float32
F32R = mybir.dt.float32r
ACT = mybir.ActivationFunctionType
ALU = mybir.AluOpType
AX = mybir.AxisListType

B, S, D, SC = 16, 100, 256, 361
P = 128
C = D // P
SCP = SC + 1
H1, DH1 = 8, 32
HC1 = P // DH1
TOPK = max(int(S * 0.1), 1)
GATE = H1 * H1
H2, DH2 = 16, 16
NG = H2 // 2
KC = [(0, 128), (128, 128), (256, SC - 256)]
VW = 32
STACK = 3 + 3
EPS = 1e-5
SCALE1 = float(DH1) ** -0.5
SCALE2 = float(DH2) ** -0.5
QSW = 8 * S + 56
UNITS = 6
NPT = 2
NMX = 3
SLOTS = 6
W_NAMES = ["q1", "k1", "v1", "o1", "q2", "k2", "v2", "o2", "r", "k", "v"]
VEC = {n: i for i, n in enumerate(
    ["bq1_0", "bq1_1", "bk1_0", "bk1_1", "bq2_0", "bq2_1", "bk2_0", "bk2_1",
     "mur_0", "mur_1", "muk_0", "muk_1", "bgp_0", "bgp_1", "bv1_0", "bv1_1", "bd", "bg"])}
NVEC = len(VEC)
ROWS = ["bo1", "bv2", "bo2"]


def decoder_layer(nc, x, xT, ctxT, wpack, vecs, rows, wd, wg, wgp, consts, out):
    es = ExitStack()
    with es:
        def sb(name, shape, dt=F32):
            return es.enter_context(nc.sbuf_tensor(name, shape, dt))

        def sem(name):
            return es.enter_context(nc.semaphore(name))

        def two(make, name, *a):
            return [make(f"{name}{i}", *a) for i in range(2)]

        bank = [es.enter_context(nc.psum_tensor(f"bank{i}", [P, 512], F32)) for i in range(8)]

        w = sb("w", [P, len(W_NAMES), C, D])
        W = {n: w[:, i] for i, n in enumerate(W_NAMES)}
        vec = sb("vec", [P, NVEC])
        wd_sb = sb("wd_sb", [P, P])
        wg_sb = sb("wg_sb", [P, C, GATE])
        wgp_sb = sb("wgp_sb", [GATE, D])
        cst = sb("cst", [P, P + HC1 + 2])
        ident = cst[:, 0:P]
        quad_mask = cst[:, P:P + HC1]
        pair_mask = cst[:, P + HC1:P + HC1 + 2]
        row_sb = sb("row_sb", [1, len(ROWS) * D])
        ones_row = sb("ones_row", [1, P])
        rowb = sb("rowb", [P, len(ROWS), D])
        ROW = {n: rowb[:, i] for i, n in enumerate(ROWS)}
        mhalf = sb("mhalf", [P, 1])
        wkh, wkl, wvh, wvl = (sb(n, [P, C, D], F32R) for n in ("wkh", "wkl", "wvh", "wvl"))

        def v(name):
            return vec[:, VEC[name]:VEC[name] + 1]

        xT_all = sb("xT_all", [P, C, B * S])
        x1_all = sb("x1_all", [S, B * D])
        x1T_all = q2_all = xT_all
        xsum = sb("xsum", [P, C, B])
        hbg = sb("hbg", [GATE, 1])
        g1 = sb("g1", [GATE, B])
        g1s = sb("g1s", [GATE, B])
        gate_all = sb("gate_all", [P, 2 * C, B])

        xTb = two(sb, "xTb", [P, C, S])
        xin = two(sb, "xin", [S, D])
        gb = two(sb, "gb", [P, 2 * C])
        qs = sb("qs", [P, C, S])
        kt = sb("kt", [P, C, S])
        kbd = sb("kbd", [P, C, HC1, S])
        v1 = two(sb, "v1", [S, D])
        s_sb = two(sb, "s_sb", [S, H1, S])
        rest = sb("rest", [S, H1, S])
        top1 = sb("top1", [S, H1, 8])
        top2 = sb("top2", [S, H1, 8])
        negm1 = sb("negm1", [S, H1])
        e1 = sb("e1", [S, H1, S])
        p1 = two(sb, "p1", [S, H1, S])
        den1 = sb("den1", [S, H1])
        rden1 = two(sb, "rden1", [S, H1])
        pT1 = sb("pT1", [S, H1, S])
        aT = sb("aT", [P, C, S])
        aTb = sb("aTb", [P, C, S])
        mixT = sb("mixT", [P, C, S])
        xbo = two(sb, "xbo", [S, D])
        y1 = sb("y1", [S, D])
        x1b = sb("x1b", [S, D])
        st = sb("st", [S, 6])
        mv = [sb(f"mv{i}", [S, 2]) for i in (1, 2, 3)]
        ve = [sb(f"ve_{i}", [S, 1]) for i in (1, 2, 3)]
        rstd = [sb(f"rstd_{i}", [S, 1]) for i in (1, 2, 3)]

        ctxf = two(sb, "ctxf", [P, C, SCP])
        ctxh = sb("ctxh", [P, C, SCP], F32R)
        ctxl = sb("ctxl", [P, C, SCP], F32R)
        kh = sb("kh", [P, C, SCP], F32R)
        kl = sb("kl", [P, C, SCP], F32R)
        ones_k = sb("ones_k", [NG, SCP], F32R)
        ks = two(sb, "ks", [P, NG, SCP], F32R)
        qm = sb("qm", [P, C, 2, S])
        qh = sb("qh", [P, C, 2, S], F32R)
        ql = sb("ql", [P, C, 2, S], F32R)
        qst = two(sb, "qst", [P, C, QSW], F32R)
        vx = two(sb, "vx", [P, len(KC), H2, VW])
        m2 = two(sb, "m2", [S, H2])
        mrow = two(sb, "mrow", [H2 // 2, S], F32R)
        pe2 = sb("pe2", [P, SLOTS, 2, 2 * S])
        oT = sb("oT", [P, 4, S])
        rden2 = sb("rden2", [S, H2])
        att = sb("att", [S, H2, DH2])
        attT = sb("attT", [P, C, S])
        xres = sb("xres", [S, D])
        y2 = sb("y2", [S, D])
        x2 = sb("x2", [S, D])
        x2T = sb("x2T", [P, C, 1 + S])
        dx = sb("dx", [P, C, S])
        xr = sb("xr", [P, C, S])
        xk = sb("xk", [P, C, S])
        th = sb("th", [S, D])
        sg = sb("sg", [S, D])
        kr = sb("kr", [P, C, S])
        ka = sb("ka", [P, C, S])
        y3 = sb("y3", [S, D])
        x3 = two(sb, "x3", [S, D])

        carried = sem("carried")
        row_in = sem("row_in")
        qk_in = sem("qk_in")
        vo_in = sem("vo_in")
        gate_in = sem("gate_in")
        w_in = sem("w_in")
        x01_in = sem("x01_in")
        xT_in = sem("xT_in")
        x_in = two(sem, "x_in")
        ones_ok = sem("ones_ok")
        rows_ps = sem("rows_ps")
        rows_ok = sem("rows_ok")
        xsum_ok = sem("xsum_ok")
        gate_ps = sem("gate_ps")
        gate_t = sem("gate_t")
        gate_u = sem("gate_u")
        gate_ps2 = sem("gate_ps2")
        gate_ok = sem("gate_ok")
        wsplit = sem("wsplit")
        hbg_ok = sem("hbg_ok")
        zeroed = sem("zeroed")
        ones_k_ok = sem("ones_k_ok")
        ones_in = sem("ones_in")
        xTb_ok = sem("xTb_ok")
        gb_ok = sem("gb_ok")
        qk_ps, v_ps = sem("qk_ps"), sem("v_ps")
        qk_sb = sem("qk_sb")
        v_sb = sem("v_sb")
        kbd_ok = sem("kbd_ok")
        s_ps = sem("s_ps")
        s_ok = sem("s_ok")
        top1_ok, negm_ok, rest_ok, top2_ok = (sem(n) for n in ("top1_ok", "negm_ok", "rest_ok", "top2_ok"))
        e1_ok, p1_ok, rden1_ok, pn_ok = (sem(n) for n in ("e1_ok", "p1_ok", "rden1_ok", "pn_ok"))
        pT_ps, pT_sb = sem("pT_ps"), sem("pT_sb")
        aT_ps, aT_sb = sem("aT_ps"), sem("aT_sb")
        aTb_ok, wdm_ok, gates_ok = sem("aTb_ok"), sem("wdm_ok"), sem("gates_ok")
        d_ps, mix_ok = sem("d_ps"), sem("mix_ok")
        y1_ps, xbo_ok = sem("y1_ps"), sem("xbo_ok")
        ln1, ve1, rstd1 = sem("ln1"), sem("ve1"), sem("rstd1")
        x1T_ps, x1T_sb, x1_kept = sem("x1T_ps"), sem("x1T_sb"), sem("x1_kept")

        ctx_in = two(sem, "ctx_in")
        ctxh_ok, ctxl_ok = sem("ctxh_ok"), sem("ctxl_ok")
        k_ps, v2_ps = sem("k_ps"), sem("v2_ps")
        kh_ok, kl_ok, v2_sb = sem("kh_ok"), sem("kl_ok"), sem("v2_sb")
        st_in = [two(sem, f"st_in_{c}_") for c in range(C)]
        q2_ps, q2_sb, qm_ok, qh_ok, ql_ok = (sem(n) for n in ("q2_ps", "q2_sb", "qm_ok", "qh_ok", "ql_ok"))
        max_ps, max_ok = sem("max_ps"), sem("max_ok")
        mT_ps, mrow_ok = sem("mT_ps"), sem("mrow_ok")
        m_in = [sem("m_in0"), sem("m_in1")]
        t_ps, exp_ok, pv_ok = sem("t_ps"), sem("exp_ok"), sem("pv_ok")
        oT_ok = sem("oT_ok")
        ot_ps, rden2_ok, att_ok = sem("ot_ps"), sem("rden2_ok"), sem("att_ok")
        at_ps, attT_ok = sem("at_ps"), sem("attT_ok")
        y2_ps, xres_ok = sem("y2_ps"), sem("xres_ok")
        ln2, ve2, rstd2 = sem("ln2"), sem("ve2"), sem("rstd2")
        x2T_ps, x2T_ok, dx_ok, xrk_ok = (sem(n) for n in ("x2T_ps", "x2T_ok", "dx_ok", "xrk_ok"))
        th_ok, sg_ok, rv_ok = sem("th_ok"), sem("sg_ok"), sem("rv_ok")
        kf_ps, kr_ok, ka_ok, f_ps = sem("kf_ps"), sem("kr_ok"), sem("ka_ok"), sem("f_ps")
        ln3, ve3, rstd3 = sem("ln3"), sem("ve3"), sem("rstd3")
        out_done = two(sem, "out_done")

        b_s = bank[0:2]
        b_qk, b_v, b_pT, b_aT, b_d, b_y = bank[2:8]
        b_row = bank[6:8]
        b_max = bank[0:NMX]
        b_t = bank[NMX:NMX + NPT]
        b_o = bank[5]
        b_m = bank[6:8]

        def carry(eng):
            eng.sem_inc(carried, 1)

        N_CLEAR = 7

        block = es.enter_context(nc.Block())

        @block.sync
        def _(sp):
            sp.dma_start(row_sb[:], rows).then_inc(row_in, 16)
            sp.dma_start(w[:, 0:2], wpack[:, 0:2]).then_inc(qk_in, 16)
            sp.dma_start(xT_all[:, :, 0:2 * S], xT[:, :, 0:2 * S]).then_inc(x01_in, 16)
            sp.dma_start(vec[:], vecs).then_inc(qk_in, 16)
            sp.dma_start(cst[:], consts).then_inc(qk_in, 16)
            sp.dma_start(w[:, 2:4], wpack[:, 2:4]).then_inc(vo_in, 16)
            sp.dma_start(xT_all[:, :, 2 * S:], xT[:, :, 2 * S:]).then_inc(xT_in, 16)
            sp.dma_start(wd_sb[:], wd).then_inc(gate_in, 16)
            sp.dma_start(wg_sb[:], wg).then_inc(gate_in, 16)
            sp.dma_start(wgp_sb[:], wgp).then_inc(gate_in, 16)

            def load_x(b, par, reused):
                if reused:
                    sp.wait_ge(xbo_ok, b - 1)
                    carry(sp)
                sp.dma_start(xin[par][:], x[bass.ds(b, 1)].rearrange("a s d -> (a s) d")).then_inc(x_in[par], 16)

            load_x(0, 0, False)
            load_x(1, 1, False)
            sp.dma_start(w[:, 4:], wpack[:, 4:]).then_inc(w_in, 16)
            sp.dma_start(ctxf[0][:], ctxT[0]).then_inc(ctx_in[0], 16)
            sp.dma_start(ctxf[1][:], ctxT[1]).then_inc(ctx_in[1], 16)
            with sp.Fori(0, (B - 2) // 2) as i:
                for par in range(2):
                    load_x(2 * i + 2 + par, par, True)

            def stack(b, par, c, free):
                if free:
                    sp.wait_ge(t_ps, 2 * UNITS * (b - 2) + UNITS * (c + 1))
                    carry(sp)
                sp.wait_ge(kl_ok, C * b + c + 1)
                carry(sp)
                for copy, src in enumerate((kh, kh, kl)):
                    sp.dma_start(ks[par][32 * copy:32 * copy + 32, 4 * c:4 * c + 4, :].bitcast(F32),
                                 src[:, c, :].bitcast(F32)).then_inc(st_in[c][par], 16)
                sp.wait_ge(ql_ok, b + 1)
                carry(sp)
                for copy, src in enumerate((qh, ql, qh)):
                    sp.dma_start(qst[par][32 * copy:32 * copy + 32, c, 0:8 * S].bitcast(F32)
                                 .rearrange("p (j q) -> p j q", j=4),
                                 src[:, c].bitcast(F32).rearrange("p t q -> p (t q)")).then_inc(st_in[c][par], 16)

            def max_row(b, par, half):
                sp.wait_ge(mrow_ok, 2 * b + half + 1)
                carry(sp)
                sp.dma_start(qst[par][96:97, half, 0:8 * S].bitcast(F32)
                             .rearrange("p (h q) -> p h q", h=8), mrow[half][:].bitcast(F32)).then_inc(m_in[half], 16)

            def store(b, par):
                sp.wait_ge(ln3, 4 * (b + 1))
                carry(sp)
                sp.dma_start(out[bass.ds(b, 1)].rearrange("a s d -> (a s) d"), x3[par][:]).then_inc(out_done[par], 16)

            def load_ctx(b, par):
                sp.wait_ge(ctxl_ok, b - 1)
                carry(sp)
                sp.dma_start(ctxf[par][:], ctxT[bass.ds(b, 1)].rearrange("a p c s -> (a p) c s")
                             ).then_inc(ctx_in[par], 16)

            def window(b, par, cur=True, prev=True, prev2=True, nxt=True, nxt3=True):
                reused = not (isinstance(b, int) and b == 0)
                if prev:
                    max_row(b - 1, 1 - par, 1)
                if nxt:
                    stack(b + 1, 1 - par, 0, reused)
                if nxt3:
                    load_ctx(b + 3, 1 - par)
                if cur:
                    max_row(b, par, 0)
                if nxt:
                    stack(b + 1, 1 - par, 1, reused)
                if prev2:
                    store(b - 2, par)

            sp.wait_ge(zeroed, N_CLEAR)
            sp.wait_ge(ones_k_ok, 1)
            for t in range(2):
                sp.dma_start(ks[t][96:97].bitcast(F32), ones_k[:].bitcast(F32)).then_inc(ones_in, 16)
            for c in range(C):
                stack(0, 0, c, False)
            load_ctx(2, 0)
            window(0, 0, prev=False, prev2=False)
            window(1, 1, prev2=False)
            window(2, 0)
            window(3, 1)
            with sp.Fori(0, (B - 8) // 2) as i:
                for k in range(2):
                    window(2 * i + 4 + k, k)
            window(B - 4, 0)
            window(B - 3, 1, nxt3=False)
            window(B - 2, 0, nxt3=False)
            window(B - 1, 1, nxt=False, nxt3=False)
            window(B, 0, cur=False, nxt=False, nxt3=False)
            window(B + 1, 1, cur=False, prev=False, nxt=False, nxt3=False)
            sp.wait_ge(out_done[0], 16 * B // 2)
            sp.wait_ge(out_done[1], 16 * B // 2)

        @block.gpsimd
        def _(pool):
            pool.memset(ones_row[:], 1.0).then_inc(ones_ok, 1)
            pool.memset(mhalf[:], -0.5)

            def fetch_x(b, par, first):
                if first:
                    pool.wait_ge(x01_in, 16)
                else:
                    pool.wait_ge(v_ps, b - 1)
                pool.tensor_copy(xTb[par][:], xT_all[:, :, bass.ds(b * S, S)]).then_inc(xTb_ok, 1)

            def prepare_x(b, par, first):
                pool.wait_ge(x_in[par], 16 * (b // 2) + 16 if isinstance(b, int) else 8 * (b - par) + 16)
                if not first:
                    pool.wait_ge(ln1, 4 * (b - 2) + 1)
                pool.wait_ge(rows_ok, 2)
                pool.tensor_tensor(xbo[par][:], xin[par][:], ROW["bo1"][0:S], ALU.add).then_inc(xbo_ok, 1)
                if not first:
                    pool.wait_ge(mix_ok, b - 1)
                pool.wait_ge(gates_ok, 1)
                pool.tensor_copy(gb[par][:], gate_all[:, :, bass.ds(b, 1)].rearrange("p c a -> p (c a)")
                                 ).then_inc(gb_ok, 1)

            def spread_keys(b, first):
                if not first:
                    pool.wait_ge(s_ps, C * b)
                for c in range(C):
                    pool.wait_ge(qk_sb, 2 * C * b + c + 1)
                    pool.tensor_tensor(kbd[:, c], kt[:, c:c + 1, :].broadcast_to([P, HC1, S]),
                                       quad_mask.rearrange("p (j a) -> p j a", a=1).broadcast_to([P, HC1, S]),
                                       ALU.mult).then_inc(kbd_ok, 1)

            def inv_std(n, k, ln, at, ve_s, rstd_s):
                pool.wait_ge(ln, at)
                carry(pool)
                pool.tensor_scalar(ve[k][:], mv[k][:, 1:2], EPS, None, ALU.add).then_inc(ve_s, 1)
                pool.wait_ge(ve_s, n + 1)
                pool.tensor_tensor(rstd[k][:], ve[k][:], mhalf[0:S], ALU.pow).then_inc(rstd_s, 1)

            def normalise(b, par):
                pool.wait_ge(rden1_ok, b + 1)
                for k in range(2):
                    hs = slice(HC1 * k, HC1 * (k + 1))
                    pool.tensor_tensor(p1[par][:, hs], p1[par][:, hs],
                                       rden1[par][:, hs].rearrange("p (h a) -> p h a", a=1).broadcast_to([S, HC1, S]),
                                       ALU.mult).then_inc(pn_ok, 1)

            clears = [0]

            def s_window(b, par, prev=True, prev2=True, nxt2=True, nxt3=True, clear=(), low=False, std_first=False):
                if prev:
                    normalise(b - 1, 1 - par)
                    prepare_x(b, par, isinstance(b, int) and b < 2)
                if std_first:
                    inv_std(b - 2, 0, ln1, 4 * (b - 2) + 3, ve1, rstd1)
                for k, (part, value) in enumerate(clear):
                    if k == 0:
                        pool.wait_ge(*((rstd1, b - 1) if std_first else (gb_ok, b + 1)))
                    pool.memset(part, value).then_inc(zeroed, 1)
                    clears[0] += 1
                    pool.wait_ge(zeroed, clears[0])
                if low:
                    ctx_low(0, 0, True)
                if prev2 and not std_first:
                    inv_std(b - 2, 0, ln1, 4 * (b - 2) + 3, ve1, rstd1)
                if nxt3:
                    fetch_x(b + 3, 1 - par, False)
                if nxt2:
                    spread_keys(b + 2, False)

            def ctx_low(b, par, first):
                pool.wait_ge(ctxh_ok, b + 1)
                pool.tensor_tensor(ctxl[:], ctxf[par][:], ctxh[:].bitcast(F32), ALU.subtract).then_inc(ctxl_ok, 1)

            def q_mask(b, first):
                if not first:
                    pool.wait_ge(ql_ok, b)
                    pool.wait_ge(qh_ok, b)
                for c in range(C):
                    last = pool.tensor_tensor(qm[:, c], q2_all[:, c:c + 1, bass.ds(b * S, S)].broadcast_to([P, 2, S]),
                                              pair_mask.rearrange("p (t a) -> p t a", a=1).broadcast_to([P, 2, S]),
                                              ALU.mult)
                last.then_inc(qm_ok, 1)

            def q_low(b):
                pool.wait_ge(qm_ok, b + 1)
                pool.wait_ge(qh_ok, b + 1)
                pool.tensor_tensor(ql[:], qm[:], qh[:].bitcast(F32), ALU.subtract).then_inc(ql_ok, 1)

            fetch_x(0, 0, True)
            fetch_x(1, 1, True)
            pool.wait_ge(qk_in, 48)
            spread_keys(0, True)
            pool.wait_ge(xT_in, 16)
            fetch_x(2, 0, False)
            spread_keys(1, False)
            s_window(0, 0, prev=False, prev2=False)
            prepare_x(0, 0, True)
            s_window(1, 1, prev2=False, clear=[(vx[0][:], 1.0)])
            s_window(2, 0, clear=[(vx[1][:], 1.0), (x2T[:], 0.0), (qst[0][:].bitcast(F32), 0.0)])
            s_window(3, 1, low=True)
            with pool.Fori(0, (B - 8) // 2) as i:
                for k in range(2):
                    s_window(2 * i + 4 + k, k)
            pool.wait_ge(q2_sb, 2)
            q_mask(0, True)
            s_window(B - 4, 0, clear=[(ks[0][96:128].bitcast(F32), 0.0)], std_first=True)
            s_window(B - 3, 1, nxt3=False, clear=[(ks[1][96:128].bitcast(F32), 0.0)],
                     std_first=True)
            s_window(B - 2, 0, nxt2=False, nxt3=False,
                     clear=[(qst[1][:].bitcast(F32), 0.0)])
            q_low(0)
            q_mask(1, False)
            s_window(B - 1, 1, nxt2=False, nxt3=False)

            def residual2(b, first):
                if not first:
                    pool.wait_ge(ln2, 4 * (b - 1) + 1)
                pool.tensor_tensor(xres[:], x1_all[:, bass.ds(b * D, D)], ROW["bo2"][0:S], ALU.add
                                   ).then_inc(xres_ok, 1)

            def shift(n, first):
                pool.wait_ge(x2T_ok, n + 1)
                if not first:
                    pool.wait_ge(xrk_ok, n)
                pool.tensor_tensor(dx[:], x2T[:, :, 1:1 + S], x2T[:, :, 0:S], ALU.subtract).then_inc(dx_ok, 1)

            def square(n):
                pool.wait_ge(kr_ok, n + 1)
                pool.tensor_tensor(ka[:], kr[:], kr[:], ALU.mult).then_inc(ka_ok, 1)

            def x_window(b, par, prev=True, prev2=True, nxt=True, nxt2=True):
                if prev2:
                    inv_std(b - 2, 1, ln2, 4 * (b - 2) + 3, ve2, rstd2)
                if nxt:
                    q_low(b + 1)
                if prev2:
                    shift(b - 2, isinstance(b, int) and b == 2)
                if prev:
                    residual2(b - 1, isinstance(b, int) and b == 1)
                if prev2:
                    square(b - 2)
                    inv_std(b - 2, 2, ln3, 4 * (b - 2) + 3, ve3, rstd3)
                if nxt2:
                    q_mask(b + 2, False)
                    ctx_low(b + 2, par, False)

            normalise(B - 1, 1)
            ctx_low(1, 1, False)
            inv_std(B - 2, 0, ln1, 4 * (B - 2) + 3, ve1, rstd1)
            inv_std(B - 1, 0, ln1, 4 * (B - 1) + 3, ve1, rstd1)
            x_window(0, 0, prev=False, prev2=False)
            pool.wait_ge(x1_kept, B)
            pool.wait_ge(q2_sb, B)
            x_window(1, 1, prev2=False)
            x_window(2, 0)
            x_window(3, 1)
            with pool.Fori(0, (B - 8) // 2) as i:
                for k in range(2):
                    x_window(2 * i + 4 + k, k)
            x_window(B - 4, 0)
            x_window(B - 3, 1)
            x_window(B - 2, 0, nxt2=False)
            x_window(B - 1, 1, nxt=False, nxt2=False)
            x_window(B, 0, nxt=False, nxt2=False)
            x_window(B + 1, 1, prev=False, nxt=False, nxt2=False)

        @block.scalar
        def _(act):
            act.wait_ge(qk_in, 48)
            act.activation(hbg[:], vec[0:GATE, VEC["bg"]:VEC["bg"] + 1], ACT.Copy, scale=0.5).then_inc(hbg_ok, 1)

            def row_biases():
                for k in range(2):
                    act.wait_ge(rows_ps, k + 1)
                    part = rowb[:, 2 * k:min(2 * k + 2, len(ROWS))].rearrange("p r d -> p (r d)")
                    act.activation(part, b_row[k][:, 0:part.shape[1]], ACT.Copy).then_inc(rows_ok, 1)

            def gate_tanh():
                act.wait_ge(gate_ps, 1)
                act.wait_ge(hbg_ok, 1)
                act.activation(g1[:], b_pT[0:GATE, 0:B], ACT.Tanh, bias=hbg[:], scale=0.5 / S).then_inc(gate_t, 1)

            def gate_values():
                act.wait_ge(gate_ps2, 1)
                for c in range(C):
                    act.activation(gate_all[:, c], b_aT[:, c * B:(c + 1) * B], ACT.Identity, bias=v(f"bgp_{c}")
                                   ).then_inc(gate_ok, 1)

            def evac_k(b, first):
                act.wait_ge(qk_ps, b + 1)
                if not first:
                    act.wait_ge(kbd_ok, C * b)
                for c in range(C):
                    act.activation(kt[:, c], b_qk[:, (C + c) * S:(C + c + 1) * S], ACT.Identity, bias=v(f"bk1_{c}")
                                   ).then_inc(qk_sb, 1)

            def evac_q(b, first):
                if not first:
                    act.wait_ge(s_ps, C * b)
                for c in range(C):
                    act.activation(qs[:, c], b_qk[:, c * S:(c + 1) * S], ACT.Identity, bias=v(f"bq1_{c}")
                                   ).then_inc(qk_sb, 1)

            def evac_scores(b, par, first):
                for c in range(C):
                    act.wait_ge(s_ps, C * b + c + 1)
                    if not first:
                        act.wait_ge(p1_ok, b - 1)
                    act.activation(s_sb[par][:, HC1 * c:HC1 * c + HC1].rearrange("p h k -> p (h k)"),
                                   b_s[c][0:S, 0:HC1 * S], ACT.Copy).then_inc(s_ok, 1)

            def exps1(b, par, heads, first):
                act.wait_ge(negm_ok, b + 1)
                if not first:
                    act.wait_ge(p1_ok, b)
                for h in heads:
                    act.activation(e1[:, h], s_sb[par][:, h], ACT.Exp, bias=negm1[:, h:h + 1], scale=SCALE1
                                   ).then_inc(e1_ok, 1)

            def evac_pT(b, k, first):
                act.wait_ge(pT_ps, 2 * b + k + 1)
                if not first:
                    act.wait_ge(aT_ps, b)
                act.activation(pT1[:, HC1 * k:HC1 * k + HC1].rearrange("p h k -> p (h k)"),
                               b_pT[0:S, 0:HC1 * S], ACT.Copy).then_inc(pT_sb, 1)

            def evac_aT(b, par, first):
                act.wait_ge(aT_ps, b + 1)
                if not first:
                    act.wait_ge(mix_ok, b)
                for c in range(C):
                    last = act.activation(aT[:, c], b_aT[:, c * S:(c + 1) * S], ACT.Identity, bias=v(f"bv1_{c}"))
                last.then_inc(aT_sb, 1)
                act.wait_ge(gb_ok, b + 1)
                for c in range(C):
                    last = act.activation(aTb[:, c], b_aT[:, c * S:(c + 1) * S], ACT.Identity,
                                          bias=gb[par][:, C + c:C + c + 1])
                last.then_inc(aTb_ok, 1)

            def evac_v(b, par):
                act.wait_ge(v_ps, b + 1)
                if not (isinstance(b, int) and b < 2):
                    act.wait_ge(aT_ps, b - 1)
                act.activation(v1[par][:], b_v[0:S, 0:D], ACT.Copy).then_inc(v_sb, 1)

            def evac_q2(b, o):
                act.wait_ge(q2_ps, b + 1)
                carry(act)
                for c in range(C):
                    last = act.activation(q2_all[:, c, bass.ds(b * S, S)], o[:, c * S:(c + 1) * S],
                                          ACT.Identity, bias=v(f"bq2_{c}"))
                last.then_inc(q2_sb, 1)

            def evac_x1T(b):
                act.wait_ge(x1T_ps, b + 1)
                act.activation(x1T_all[:, :, bass.ds(b * S, S)], b_aT[:, 0:C * S].rearrange("p (c q) -> p c q", c=C),
                               ACT.Copy).then_inc(x1T_sb, 1)
                act.activation(x1_all[:, bass.ds(b * D, D)], x1b[:], ACT.Copy).then_inc(x1_kept, 1)

            def k_high(b, par_prev, c, first, o=b_m[1]):
                act.wait_ge(k_ps, C * b + c + 1)
                if not first:
                    act.wait_ge(st_in[c][par_prev], 16 * STACK * stacked(b - 1))
                act.activation(kh[:, c], o[:, 0:SCP], ACT.Identity, bias=v(f"bk2_{c}")).then_inc(kh_ok, 1)

            def stacked(b):
                return b // 2 + 1

            def s_window(b, par, prev=True, prev2=True, prev3=True, nxt=True, nxt2=True):
                first, prev_first = (isinstance(b, int) and b == n for n in range(2))
                if prev_first:
                    exps1(b, par, range(0, HC1), first)
                if prev3:
                    evac_x1T(b - 3)
                if prev:
                    evac_pT(b - 1, 0, prev_first)
                if nxt2:
                    evac_k(b + 2, False)
                if prev:
                    evac_pT(b - 1, 1, prev_first)
                if not prev_first:
                    exps1(b, par, range(0, HC1), first)
                if prev:
                    evac_aT(b - 1, 1 - par, prev_first)
                exps1(b, par, range(HC1, H1), first)
                if nxt2:
                    evac_q(b + 2, False)
                elif nxt:
                    k_high(0, None, 0, True, b_qk)
                else:
                    k_high(0, None, 1, True, b_v)
                if nxt:
                    evac_scores(b + 1, 1 - par, first)
                if prev3:
                    evac_q2(b - 3, (b_v if nxt else b_y)[:, D:512])
                if nxt:
                    evac_v(b + 1, 1 - par)

            row_biases()
            evac_k(0, True)
            evac_q(0, True)
            evac_v(0, 0)
            evac_scores(0, 0, True)
            evac_k(1, False)
            evac_q(1, False)
            gate_tanh()
            s_window(0, 0, prev=False, prev2=False, prev3=False)
            gate_values()
            s_window(1, 1, prev2=False, prev3=False)
            s_window(2, 0, prev3=False)
            s_window(3, 1)
            with act.Fori(0, (B - 6) // 2) as i:
                for k in range(2):
                    s_window(2 * i + 4 + k, k)
            s_window(B - 2, 0, nxt2=False)
            s_window(B - 1, 1, nxt=False, nxt2=False)
            def exp2(b, u, no_slot_wait=False):
                n = 2 * UNITS * b + u
                rows_n = KC[u % 3][1]
                act.wait_ge(t_ps, n + 1)
                if not no_slot_wait:
                    act.wait_ge(pv_ok, n - SLOTS + 1)
                act.activation(pe2[0:rows_n, u % SLOTS],
                               b_t[u % NPT][0:rows_n].rearrange("p (g q) -> p g q", g=2)[:, :, 0:2 * S],
                               ACT.Exp, scale=SCALE2).then_inc(exp_ok, 1)

            def neg_max(b, half, first):
                act.wait_ge(mT_ps, 2 * b + half + 1)
                if not first:
                    act.wait_ge(m_in[half], 16 * b)
                act.activation(mrow[half][:], b_m[1][0:8, 0:S], ACT.Copy, scale=-1.0).then_inc(mrow_ok, 1)

            def out_T(b, first):
                act.wait_ge(pv_ok, 2 * UNITS * (b + 1))
                if not first:
                    act.wait_ge(ot_ps, b)
                act.activation(oT[:].rearrange("p h q -> p (h q)"), b_o[:, 0:4 * S], ACT.Copy).then_inc(oT_ok, 1)

            def att_T(b, first, o=b_m[0]):
                act.wait_ge(at_ps, b + 1)
                if not first:
                    act.wait_ge(y2_ps, b)
                act.activation(attT[:].rearrange("p c q -> p (c q)"), o[:, 0:C * S], ACT.Copy).then_inc(attT_ok, 1)

            def ffn_T(n, first):
                act.wait_ge(x2T_ps, n + 1)
                if first:
                    act.wait_ge(zeroed, N_CLEAR)
                else:
                    act.wait_ge(xrk_ok, n)
                act.activation(x2T[:, :, 1:1 + S], b_m[0][:, 0:C * S].rearrange("p (c q) -> p c q", c=C),
                               ACT.Copy).then_inc(x2T_ok, 1)

            def ffn_rk(n, first):
                act.wait_ge(kf_ps, n + 1)
                if not first:
                    act.wait_ge(sg_ok, n)
                act.activation(th[:], b_m[0][0:S, 0:D], ACT.Tanh, scale=0.5).then_inc(th_ok, 1)
                if not first:
                    act.wait_ge(ka_ok, n)
                act.activation(kr[:].rearrange("p c q -> p (c q)"), b_m[0][:, D:D + C * S], ACT.Relu
                               ).then_inc(kr_ok, 1)

            def x_window(b, par, prev=True, prev2=True, nxt=True):
                prev_first, prev2_first = (isinstance(b, int) and b == n for n in (1, 2))
                if prev:
                    exp2(b - 1, 1, prev_first)
                    exp2(b - 1, 2, prev_first)
                    neg_max(b - 1, 1, prev_first)
                    exp2(b - 1, 3, prev_first)
                    exp2(b - 1, 4, prev_first)
                    exp2(b - 1, 5, prev_first)
                if nxt:
                    k_high(b + 1, par, 0, False)
                if prev2:
                    ffn_T(b - 2, prev2_first)
                if prev:
                    exp2(b - 1, 6)
                    exp2(b - 1, 7)
                if nxt:
                    k_high(b + 1, par, 1, False)
                if prev:
                    exp2(b - 1, 8)
                    exp2(b - 1, 9)
                if prev2:
                    ffn_rk(b - 2, prev2_first)
                if prev:
                    exp2(b - 1, 10)
                    exp2(b - 1, 11)
                neg_max(b, 0, False)
                if prev:
                    out_T(b - 1, prev_first)
                exp2(b, 0)
                if prev:
                    att_T(b - 1, prev_first)

            evac_x1T(B - 3)
            evac_pT(B - 1, 0, False)
            evac_pT(B - 1, 1, False)
            evac_q2(B - 3, b_y[:, D:512])
            evac_aT(B - 1, 1, False)
            k_high(1, 0, 0, False)
            evac_x1T(B - 2)
            k_high(1, 0, 1, False)
            evac_q2(B - 2, b_m[0])
            evac_x1T(B - 1)
            neg_max(0, 0, True)
            evac_q2(B - 1, b_m[0])
            exp2(0, 0, True)
            x_window(1, 1, prev2=False)
            x_window(2, 0)
            x_window(3, 1)
            with act.Fori(0, (B - 8) // 2) as i:
                for k in range(2):
                    x_window(2 * i + 4 + k, k)
            x_window(B - 4, 0)
            x_window(B - 3, 1)
            x_window(B - 2, 0)
            x_window(B - 1, 1, nxt=False)
            exp2(B - 1, 1)
            exp2(B - 1, 2)
            neg_max(B - 1, 1, False)
            for u in range(3, 6):
                exp2(B - 1, u)
            ffn_T(B - 2, False)
            for u in range(6, 12):
                exp2(B - 1, u)
            out_T(B - 1, False)
            ffn_rk(B - 2, False)
            att_T(B - 1, False, b_m[1])
            ffn_T(B - 1, False)
            ffn_rk(B - 1, False)

        @block.tensor
        def _(pe):
            pe.wait_ge(ones_ok, 1)
            pe.wait_ge(row_in, 16)
            for k in range(2):
                n = min(512, len(ROWS) * D - 512 * k)
                pe.matmul(b_row[k][:, 0:n], ones_row[:], row_sb[:, k * 512:k * 512 + n], start=True, stop=True
                          ).then_inc(rows_ps, 1)

            def gate_hidden():
                pe.wait_ge(gate_in, 48)
                pe.wait_ge(xsum_ok, 1)
                for c in range(C):
                    last = pe.matmul(b_pT[0:GATE, 0:B], wg_sb[:, c], xsum[:, c], start=(c == 0), stop=(c == C - 1))
                last.then_inc(gate_ps, 1)

            def gate_out():
                pe.wait_ge(gate_u, 1)
                for c in range(C):
                    last = pe.matmul(b_aT[:, c * B:(c + 1) * B], wgp_sb[:, c * P:(c + 1) * P], g1s[:],
                                     start=True, stop=True)
                last.then_inc(gate_ps2, 1)

            def project_qk(b, par, n, first):
                if not first:
                    pe.wait_ge(qk_sb, 2 * C * b)
                pe.wait_ge(xTb_ok, b + 1)
                for c in range(C):
                    o = b_qk[:, (n * C + c) * S:(n * C + c + 1) * S]
                    for i in range(C):
                        last = pe.matmul(o, W[("q1", "k1")[n]][:, i, c * P:(c + 1) * P], xTb[par][:, i],
                                         start=(i == 0), stop=(i == C - 1))
                if n == 1:
                    last.then_inc(qk_ps, 1)

            def project_v(b, par, first):
                if not first:
                    pe.wait_ge(v_sb, b)
                for i in range(C):
                    last = pe.matmul(b_v[0:S, 0:D], xTb[par][:, i], W["v1"][:, i], start=(i == 0), stop=(i == C - 1))
                last.then_inc(v_ps, 1)

            def scores(b, first):
                pe.wait_ge(qk_sb, 2 * C * (b + 1))
                if not first:
                    pe.wait_ge(s_ok, 2 * b)
                for c in range(C):
                    pe.wait_ge(kbd_ok, C * b + c + 1)
                    pe.matmul(b_s[c][0:S, 0:HC1 * S], qs[:, c], kbd[:, c].rearrange("p h k -> p (h k)"),
                              start=True, stop=True).then_inc(s_ps, 1)

            def turn_probs(b, par, k, first):
                pe.wait_ge(pn_ok, 2 * b + k + 1)
                if not first:
                    pe.wait_ge(pT_sb, 2 * b + k)
                for h in range(HC1 * k, HC1 * k + HC1):
                    last = pe.transpose(b_pT[0:S, (h % HC1) * S:(h % HC1 + 1) * S], p1[par][:, h], ident[0:S, 0:S])
                last.then_inc(pT_ps, 1)

            def mix_values(b, par):
                pe.wait_ge(pT_sb, 2 * b + 2)
                pe.wait_ge(v_sb, b + 1)
                if not (isinstance(b, int) and b < 3):
                    pe.wait_ge(x1T_sb, b - 2)
                for h in range(H1):
                    j, c = h % HC1, h // HC1
                    last = pe.matmul(b_aT[DH1 * j:DH1 * (j + 1), c * S:(c + 1) * S],
                                     v1[par][:, DH1 * h:DH1 * (h + 1)], pT1[:, h], start=True, stop=True)
                last.then_inc(aT_ps, 1)

            def distil(b, first):
                pe.wait_ge(aT_sb, b + 1)
                if not first:
                    pe.wait_ge(mix_ok, b)
                pe.matmul(b_d[:, 0:C * S], wd_sb[:], aT[:].rearrange("p c q -> p (c q)"), start=True, stop=True
                          ).then_inc(d_ps, 1)

            def out1(b, first, o=b_y[:, 0:D]):
                pe.wait_ge(mix_ok, b + 1)
                if not first:
                    pe.wait_ge(ln1, 4 * (b - 1) + 1)
                for c in range(C):
                    last = pe.matmul(o[0:S], mixT[:, c], W["o1"][:, c], start=(c == 0), stop=(c == C - 1))
                last.then_inc(y1_ps, 1)

            def turn_x1(b, at):
                pe.wait_ge(ln1, 4 * (b + 1))
                pe.wait_ge(aTb_ok, at)
                for c in range(C):
                    last = pe.transpose(b_aT[:, c * S:(c + 1) * S], x1b[:, c * P:(c + 1) * P], ident[0:S, 0:S])
                last.then_inc(x1T_ps, 1)

            def project_q2(b, o, wait):
                pe.wait_ge(x1T_sb, b + 1)
                for s_, n_ in wait:
                    pe.wait_ge(s_, n_)
                for c in range(C):
                    for i in range(C):
                        last = pe.matmul(o[:, c * S:(c + 1) * S], W["q2"][:, i, c * P:(c + 1) * P],
                                         x1T_all[:, i, bass.ds(b * S, S)], start=(i == 0), stop=(i == C - 1))
                last.then_inc(q2_ps, 1)

            def split_product(o, pairs):
                todo = [(a, m) for wh, wl, xh, xl in pairs for a, m in ((wh, xh), (wh, xl), (wl, xh))]
                for n, (a, m) in enumerate(todo):
                    last = pe.matmul(o, a, m, start=(n == 0), stop=(n == len(todo) - 1))
                return last

            def proj_k(b, c, wait, bank_k=b_m[1]):
                if c == 0:
                    pe.wait_ge(ctxl_ok, b + 1)
                for s_, n_ in wait:
                    pe.wait_ge(s_, n_)
                co = slice(c * P, (c + 1) * P)
                split_product(bank_k[:, 0:SCP], [(wkh[:, i, co], wkl[:, i, co], ctxh[:, i], ctxl[:, i])
                                                 for i in range(C)]).then_inc(k_ps, 1)

            def proj_v(b, part, wait, bank_v=b_m[1]):
                for s_, n_ in wait:
                    pe.wait_ge(s_, n_)
                for kc in ((0, 1), (2,))[part]:
                    k0, n = KC[kc]
                    o = bank_v[0:n, (kc % 2) * D:(kc % 2 + 1) * D]
                    last = split_product(o, [(ctxh[:, i, k0:k0 + n], ctxl[:, i, k0:k0 + n], wvh[:, i], wvl[:, i])
                                             for i in range(C)])
                last.then_inc(v2_ps, 1)

            def s_window(b, par, prev=True, prev2=True, prev3=True, nxt=True, nxt2=True):
                q = 1 - par
                prev_first = isinstance(b, int) and b == 1
                if prev3:
                    turn_x1(b - 3, b - 1)
                if nxt2:
                    project_qk(b + 2, par, 0, False)
                if prev:
                    turn_probs(b - 1, q, 0, prev_first)
                if nxt2:
                    project_qk(b + 2, par, 1, False)
                if prev:
                    turn_probs(b - 1, q, 1, False)
                if nxt:
                    if not (isinstance(b, int) and b < 4):
                        pe.wait_ge(q2_sb, b - 3)
                    project_v(b + 1, q, False)
                if not nxt:
                    pe.wait_ge(q2_sb, B - 4)
                    proj_k(0, 1, [(v_sb, B)], b_v)
                if prev3 and not nxt:
                    project_q2(b - 3, b_y[:, D:512], [(ln1, 4 * (b - 2) + 1)])
                if prev_first:
                    pe.wait_ge(gate_ok, C)
                if prev:
                    mix_values(b - 1, q)
                if nxt:
                    scores(b + 1, False)
                if nxt and not nxt2:
                    pe.wait_ge(wsplit, 4)
                    proj_k(0, 0, [(qk_sb, 2 * C * B)], b_qk)
                if prev:
                    distil(b - 1, prev_first)
                if prev3 and nxt:
                    project_q2(b - 3, b_v[:, D:512], [])
                if not nxt:
                    proj_v(0, 0, [(kl_ok, 1)], b_qk)
                    proj_v(0, 1, [(s_ok, C * B - 1)], b_s[0])
                    pe.wait_ge(q2_sb, B - 3)
                if prev:
                    out1(b - 1, prev_first)

            pe.wait_ge(qk_in, 48)
            project_qk(0, 0, 0, True)
            project_qk(0, 0, 1, True)
            pe.wait_ge(vo_in, 16)
            project_v(0, 0, True)
            scores(0, True)
            project_qk(1, 1, 0, False)
            project_qk(1, 1, 1, False)
            gate_hidden()
            s_window(0, 0, prev=False, prev2=False, prev3=False)
            gate_out()
            pe.wait_ge(wdm_ok, 1)
            pe.wait_ge(rows_ok, 2)
            s_window(1, 1, prev2=False, prev3=False)
            s_window(2, 0, prev3=False)
            pe.wait_ge(w_in, 16)
            s_window(3, 1)
            with pe.Fori(0, (B - 6) // 2) as i:
                for k in range(2):
                    s_window(2 * i + 4 + k, k)
            s_window(B - 2, 0, nxt2=False)
            s_window(B - 1, 1, nxt=False, nxt2=False)
            def head_max(b, par, h, first=False):
                n = H2 * b + h
                if h % 8 == 0:
                    pe.wait_ge(st_in[h // 8][par], 16 * STACK * (b // 2 + 1))
                at = (h + par) % NMX
                if h >= NMX:
                    pe.wait_ge(max_ok, n - NMX + 1)
                elif not first:
                    before = max(g for g in range(H2) if (g + 1 - par) % NMX == at)
                    pe.wait_ge(max_ok, H2 * (b - 1) + before + 1)
                pe.matmul(b_max[at][0:S, 0:SCP], qst[par][0:96, h // 8, (h % 8) * S:(h % 8 + 1) * S],
                          ks[par][0:96, h // 2, :], start=True, stop=True).then_inc(max_ps, 1)

            def turn_max(b, par, half, wait):
                pe.wait_ge(max_ok, H2 * b + 8 * half + 8)
                for s_, n_ in wait:
                    pe.wait_ge(s_, n_)
                pe.transpose(b_m[1][0:8, 0:S], m2[par][:, 8 * half:8 * half + 8], ident[0:S, 0:S]).then_inc(mT_ps, 1)

            def t_unit(b, par, u, first=False):
                n = 2 * UNITS * b + u
                gp, (k0, kn) = u // 3, KC[u % 3]
                if u % UNITS == 0:
                    pe.wait_ge(m_in[u // UNITS], 16 * (b + 1))
                if not (first and u < NPT):
                    pe.wait_ge(exp_ok, n - NPT + 1)
                for i in range(2):
                    g = 2 * gp + i
                    last = pe.matmul(b_t[u % NPT][0:kn, i * D:(i + 1) * D], ks[par][:, g, k0:k0 + kn],
                                     qst[par][:, g // 4, (g % 4) * 2 * S:(g % 4) * 2 * S + D],
                                     start=True, stop=True)
                last.then_inc(t_ps, 1)

            def pv_unit(b, par, u, first=False):
                n = 2 * UNITS * b + u
                gp, kc = u // 3, u % 3
                kn = KC[kc][1]
                pe.wait_ge(exp_ok, n + 1)
                if u == 0:
                    pe.wait_ge(v2_sb, 3 * (b + 1))
                    pe.wait_ge(oT_ok, b) if not first else pe.wait_ge(x1T_sb, B)
                for j in range(4):
                    last = pe.matmul(b_o[VW * j:VW * (j + 1), gp * S:(gp + 1) * S], vx[par][0:kn, kc, 4 * gp + j],
                                     pe2[0:kn, u % SLOTS].rearrange("p g q -> p (g q)")[:, j * S:(j + 1) * S],
                                     start=(u == 0), stop=(u == 2 * UNITS - 1), skip_group_check=True)
                last.then_inc(pv_ok, 1)

            def turn_out(b, wait, o=b_m[0]):
                pe.wait_ge(oT_ok, b + 1)
                for s_, n_ in wait:
                    pe.wait_ge(s_, n_)
                for k in range(4):
                    last = pe.transpose(o[0:S, k * P:(k + 1) * P], oT[:, k], ident)
                last.then_inc(ot_ps, 1)

            def turn_att(b, o=b_m[0]):
                pe.wait_ge(att_ok, b + 1)
                av = att[:].rearrange("p h d -> p (h d)")
                for c in range(C):
                    last = pe.transpose(o[:, c * S:(c + 1) * S], av[:, c * P:(c + 1) * P], ident[0:S, 0:S])
                last.then_inc(at_ps, 1)

            def out2(b, wait, o=b_m[0]):
                pe.wait_ge(attT_ok, b + 1)
                for s_, n_ in wait:
                    pe.wait_ge(s_, n_)
                for c in range(C):
                    last = pe.matmul(o[0:S, 0:D], attT[:, c], W["o2"][:, c], start=(c == 0), stop=(c == C - 1))
                last.then_inc(y2_ps, 1)

            def turn_x2(n, wait):
                pe.wait_ge(ln2, 4 * (n + 1))
                for s_, n_ in wait:
                    pe.wait_ge(s_, n_)
                for c in range(C):
                    last = pe.transpose(b_m[0][:, c * S:(c + 1) * S], x2[:, c * P:(c + 1) * P], ident[0:S, 0:S])
                last.then_inc(x2T_ps, 1)

            def ffn_in(n, wait):
                pe.wait_ge(xrk_ok, n + 1)
                for s_, n_ in wait:
                    pe.wait_ge(s_, n_)
                for i in range(C):
                    pe.matmul(b_m[0][0:S, 0:D], xr[:, i], W["r"][:, i], start=(i == 0), stop=(i == C - 1))
                for c in range(C):
                    for i in range(C):
                        last = pe.matmul(b_m[0][:, D + c * S:D + (c + 1) * S], W["k"][:, i, c * P:(c + 1) * P],
                                         xk[:, i], start=(i == 0), stop=(i == C - 1))
                last.then_inc(kf_ps, 1)

            def ffn_out(n):
                pe.wait_ge(ka_ok, n + 1)
                for i in range(C):
                    last = pe.matmul(b_m[0][0:S, 0:D], ka[:, i], W["v"][:, i], start=(i == 0), stop=(i == C - 1))
                last.then_inc(f_ps, 1)

            def x_window(b, par, prev=True, prev2=True, nxt=True):
                first, prev_first = (isinstance(b, int) and b == n for n in range(2))
                q = 1 - par
                if first:
                    turn_x1(B - 3, B - 1)
                    pe.wait_ge(v2_sb, 3)
                    pe.wait_ge(s_ok, C * B)
                head_max(b, par, 0, first)
                if first:
                    head_max(b, par, 1, first)
                    turn_probs(B - 1, 1, 0, False)
                    head_max(b, par, 2, first)
                    turn_probs(B - 1, 1, 1, False)
                    project_q2(B - 3, b_y[:, D:512], [(ln1, 4 * (B - 2) + 1)])
                    mix_values(B - 1, 1)
                    head_max(b, par, 3)
                    proj_k(b + 1, 0, [(q2_sb, B - 2)])
                    distil(B - 1, False)
                    head_max(b, par, 4)
                    turn_x1(B - 2, B)
                    head_max(b, par, 5)
                    out1(B - 1, False, b_d[:, D:512])
                    proj_k(b + 1, 1, [(kl_ok, C * (b + 1) + 1)])
                    head_max(b, par, 6)
                    project_q2(B - 2, b_m[0], [(ln1, 4 * (B - 1) + 1)])
                    head_max(b, par, 7)
                    head_max(b, par, 8)
                    head_max(b, par, 9)
                    pe.wait_ge(x1T_sb, B - 1)
                    turn_x1(B - 1, B)
                    head_max(b, par, 10)
                    turn_max(b, par, 0, [(kl_ok, C * (b + 2))])
                    head_max(b, par, 11)
                    head_max(b, par, 12)
                    project_q2(B - 1, b_m[0], [(q2_sb, B - 1)])
                    head_max(b, par, 13)
                    proj_v(b + 1, 0, [(mrow_ok, 2 * b + 1)])
                    head_max(b, par, 14)
                    head_max(b, par, 15)
                    proj_v(b + 1, 1, [(v2_sb, 3 * (b + 1) + 2)])
                    pe.wait_ge(zeroed, N_CLEAR)
                    pe.wait_ge(ones_in, 32)
                    pe.wait_ge(kl_ok, C)
                    pe.wait_ge(pT_sb, 2 * B)
                    t_unit(b, par, 0, first)
                    t_unit(b, par, 1, first)
                    t_unit(b, par, 2)
                    return
                if prev2:
                    out2(b - 2, [])
                if prev:
                    turn_max(b - 1, q, 1, [(v2_sb, 3 * (b + 1))])
                    pv_unit(b - 1, q, 0, prev_first)
                    t_unit(b - 1, q, 3)
                head_max(b, par, 1)
                if prev:
                    t_unit(b - 1, q, 4)
                    pv_unit(b - 1, q, 1)
                    pv_unit(b - 1, q, 2)
                head_max(b, par, 2)
                if prev:
                    pv_unit(b - 1, q, 3)
                    t_unit(b - 1, q, 5)
                if nxt:
                    proj_k(b + 1, 0, [(mrow_ok, 2 * b)])
                head_max(b, par, 3)
                if prev:
                    pv_unit(b - 1, q, 4)
                if prev2:
                    turn_x2(b - 2, [])
                if prev:
                    t_unit(b - 1, q, 6)
                head_max(b, par, 4)
                if prev:
                    pv_unit(b - 1, q, 5)
                head_max(b, par, 5)
                if prev:
                    t_unit(b - 1, q, 7)
                head_max(b, par, 6)
                if prev:
                    pv_unit(b - 1, q, 6)
                    t_unit(b - 1, q, 8)
                if nxt:
                    proj_k(b + 1, 1, [(kl_ok, C * (b + 1) + 1)])
                head_max(b, par, 7)
                if prev:
                    t_unit(b - 1, q, 9)
                if prev2:
                    ffn_in(b - 2, [])
                head_max(b, par, 8)
                head_max(b, par, 9)
                if prev:
                    t_unit(b - 1, q, 10)
                    pv_unit(b - 1, q, 7)
                    pv_unit(b - 1, q, 8)
                head_max(b, par, 10)
                turn_max(b, par, 0, [(kl_ok, C * (b + 2))] if nxt else [(mrow_ok, 2 * b)])
                head_max(b, par, 11)
                if prev:
                    t_unit(b - 1, q, 11)
                head_max(b, par, 12)
                if prev2:
                    ffn_out(b - 2)
                if prev:
                    pv_unit(b - 1, q, 9)
                    pv_unit(b - 1, q, 10)
                    pv_unit(b - 1, q, 11)
                head_max(b, par, 13)
                if nxt:
                    proj_v(b + 1, 0, [(mrow_ok, 2 * b + 1)])
                if prev:
                    turn_out(b - 1, [(rv_ok, b - 1)] if prev2 else [(q2_sb, B)])
                head_max(b, par, 14)
                t_unit(b, par, 0)
                head_max(b, par, 15)
                if nxt:
                    proj_v(b + 1, 1, [(v2_sb, 3 * (b + 1) + 2)])
                if prev:
                    turn_att(b - 1)
                t_unit(b, par, 1)
                t_unit(b, par, 2)

            x_window(0, 0, prev=False, prev2=False)
            x_window(1, 1, prev2=False)
            x_window(2, 0)
            x_window(3, 1)
            with pe.Fori(0, (B - 8) // 2) as i:
                for k in range(2):
                    x_window(2 * i + 4 + k, k)
            x_window(B - 4, 0)
            x_window(B - 3, 1)
            x_window(B - 2, 0)
            x_window(B - 1, 1, nxt=False)
            turn_max(B - 1, 1, 1, [(mrow_ok, 2 * B - 1)])
            out2(B - 2, [])
            pv_unit(B - 1, 1, 0)
            t_unit(B - 1, 1, 3)
            t_unit(B - 1, 1, 4)
            pv_unit(B - 1, 1, 1)
            pv_unit(B - 1, 1, 2)
            t_unit(B - 1, 1, 5)
            for u in range(3, 6):
                pv_unit(B - 1, 1, u)
            turn_x2(B - 2, [])
            t_unit(B - 1, 1, 6)
            for u in range(7, 12):
                t_unit(B - 1, 1, u)
                pv_unit(B - 1, 1, u - 1)
            pv_unit(B - 1, 1, 11)
            ffn_in(B - 2, [])
            turn_out(B - 1, [(mrow_ok, 2 * B)], b_m[1])
            ffn_out(B - 2)
            turn_att(B - 1, b_m[1])
            out2(B - 1, [], b_m[1])
            turn_x2(B - 1, [(rv_ok, B - 1)])
            ffn_in(B - 1, [])
            ffn_out(B - 1)

        @block.vector
        def _(dve):
            def mixed(b, par):
                dve.wait_ge(d_ps, b + 1)
                dve.wait_ge(aTb_ok, b + 1)
                if not (isinstance(b, int) and b == 0):
                    dve.wait_ge(y1_ps, b)
                for c in range(C):
                    last = dve.scalar_tensor_tensor(mixT[:, c], b_d[:, c * S:(c + 1) * S], gb[par][:, c:c + 1],
                                                    aTb[:, c], ALU.mult, ALU.add)
                last.then_inc(mix_ok, 1)

            def moments(n, ln, y):
                dve.wait_ge(ln, 4 * n + 1)
                dve.bn_stats(st[:], y[:]).then_inc(ln, 1)

            def mean_var(n, k, ln):
                dve.wait_ge(ln, 4 * n + 2)
                carry(dve)
                dve.bn_aggr(mv[k][:], st[:]).then_inc(ln, 1)

            def stats(n, k, ln, y):
                moments(n, ln, y)
                mean_var(n, k, ln)

            def norm(n, k, ln, rstd_s, y, dst):
                dve.wait_ge(ln, 4 * n + 3)
                dve.wait_ge(rstd_s, n + 1)
                return dve.tensor_scalar(dst, y[:], mv[k][:, 0:1], rstd[k][:], ALU.subtract, ALU.mult)

            def residual1(b, par, o=b_y[:, 0:D]):
                dve.wait_ge(y1_ps, b + 1)
                dve.wait_ge(xbo_ok, b + 1)
                dve.tensor_tensor(y1[:], o[0:S], xbo[par][:], ALU.add).then_inc(ln1, 1)

            def norm1(b):
                if not (isinstance(b, int) and b == 0):
                    dve.wait_ge(x1T_ps, b)
                    dve.wait_ge(x1_kept, b)
                norm(b, 0, ln1, rstd1, y1, x1b[:]).then_inc(ln1, 1)

            def ctx_high(b, par, reuse):
                dve.wait_ge(ctx_in[par], 16 * (b // 2 + 1))
                if reuse:
                    dve.wait_ge(v2_ps, 2 * b)
                dve.tensor_copy(ctxh[:], ctxf[par][:]).then_inc(ctxh_ok, 1)

            def k_low(b, c, o=b_m[1]):
                dve.wait_ge(kh_ok, C * b + c + 1)
                dve.scalar_tensor_tensor(kl[:, c], o[:, 0:SCP], v(f"bk2_{c}"), kh[:, c].bitcast(F32),
                                         ALU.add, ALU.subtract).then_inc(kl_ok, 1)

            def values2(b, par, part, reuse, o=b_m[1]):
                dve.wait_ge(v2_ps, 2 * b + part + 1)
                if reuse:
                    dve.wait_ge(pv_ok, 2 * UNITS * (b - 1))
                for kc in ((0, 1), (2,))[part]:
                    n = KC[kc][1]
                    dve.tensor_tensor(vx[par][0:n, kc, :, 0:DH2],
                                      o[0:n, (kc % 2) * D:(kc % 2 + 1) * D].rearrange("p (h d) -> p h d", d=DH2),
                                      ROW["bv2"][0:n].rearrange("p (h d) -> p h d", d=DH2), ALU.add
                                      ).then_inc(v2_sb, 1)

            def q_high(b, par_prev, first):
                dve.wait_ge(qm_ok, b + 1)
                if not first:
                    for c in range(C):
                        dve.wait_ge(st_in[c][par_prev], 16 * STACK * ((b - 1) // 2 + 1))
                dve.tensor_copy(qh[:], qm[:]).then_inc(qh_ok, 1)

            def split_weights():
                dve.wait_ge(w_in, 16)
                for hi, src in ((wkh, W["k2"]), (wvh, W["v2"])):
                    dve.tensor_copy(hi[:], src).then_inc(wsplit, 1)
                dve.wait_ge(wsplit, 2)
                for hi, lo, src in ((wkh, wkl, W["k2"]), (wvh, wvl, W["v2"])):
                    dve.tensor_tensor(lo[:], src, hi[:].bitcast(F32), ALU.subtract).then_inc(wsplit, 1)

            def s_window(b, par, prev=True, prev2=True, nxt=True):
                first, prev_first = (isinstance(b, int) and b == n for n in range(2))
                q = 1 - par
                for h in range(H1):
                    if h % HC1 == 0:
                        dve.wait_ge(s_ok, C * b + h // HC1 + 1)
                        carry(dve)
                    last = dve.max(top1[:, h], s_sb[par][:, h])
                last.then_inc(top1_ok, 1)
                if prev2:
                    moments(b - 2, ln1, y1)
                dve.wait_ge(top1_ok, b + 1)
                if not first:
                    dve.wait_ge(e1_ok, H1 * b)
                dve.tensor_scalar(negm1[:], top1[:, :, 0], -SCALE1, None, ALU.mult).then_inc(negm_ok, 1)
                for h in range(H1):
                    last = dve.match_replace(rest[:, h], top1[:, h], s_sb[par][:, h], -3.0e38)
                last.then_inc(rest_ok, 1)
                if prev2:
                    mean_var(b - 2, 0, ln1)
                dve.wait_ge(rest_ok, b + 1)
                carry(dve)
                for h in range(H1):
                    last = dve.max(top2[:, h], rest[:, h])
                last.then_inc(top2_ok, 1)
                if first:
                    dve.wait_ge(gate_t, 1)
                    dve.tensor_scalar(g1s[:], g1[:], 0.5, 0.5, ALU.mult, ALU.add).then_inc(gate_u, 1)
                if prev2:
                    norm1(b - 2)
                dve.wait_ge(top2_ok, b + 1)
                if not (isinstance(b, int) and b < 2):
                    dve.wait_ge(pT_ps, 2 * (b - 1))
                for h in range(H1):
                    if h % HC1 == 0:
                        dve.wait_ge(e1_ok, H1 * b + h + HC1)
                    last = dve.scalar_tensor_tensor(p1[par][:, h], s_sb[par][:, h],
                                                    top2[:, h, TOPK - 9:TOPK - 8], e1[:, h],
                                                    ALU.is_ge, ALU.mult, accum_out=den1[:, h:h + 1])
                    if prev_first and h == HC1 - 1:
                        split_weights()
                    if prev and h == HC1 - 1:
                        mixed(b - 1, q)
                last.then_inc(p1_ok, 1)
                dve.wait_ge(p1_ok, b + 1)
                dve.reciprocal(rden1[par][:], den1[:]).then_inc(rden1_ok, 1)
                if not nxt:
                    k_low(0, 1, b_v)
                    dve.wait_ge(zeroed, N_CLEAR)
                    values2(0, 0, 0, False, b_qk)
                    values2(0, 0, 1, False, b_s[0])
                if prev:
                    residual1(b - 1, q)

            dve.memset(ones_k[:].bitcast(F32), 1.0).then_inc(ones_k_ok, 1)
            dve.wait_ge(qk_in, 48)
            dve.wait_ge(gate_in, 48)
            dve.tensor_tensor(wd_sb[:], wd_sb[:], ident, ALU.subtract).then_inc(wdm_ok, 1)
            dve.wait_ge(x01_in, 16)
            dve.wait_ge(xT_in, 16)
            for c in range(C):
                last = dve.tensor_reduce(xsum[:, c], xT_all[:, c].rearrange("p (b s) -> p b s", s=S), AX.X, ALU.add)
            last.then_inc(xsum_ok, 1)
            s_window(0, 0, prev=False, prev2=False)
            dve.wait_ge(gate_ok, C)
            for c in range(C):
                last = dve.tensor_scalar(gate_all[:, C + c], gate_all[:, c], v("bd"), v(f"bv1_{c}"),
                                         ALU.mult, ALU.add)
            last.then_inc(gates_ok, 1)
            dve.wait_ge(rows_ok, 2)
            s_window(1, 1, prev2=False)
            ctx_high(0, 0, False)
            with dve.Fori(0, (B - 4) // 2) as i:
                for k in range(2):
                    s_window(2 * i + 2 + k, k)
            q_high(0, None, True)
            s_window(B - 2, 0)
            k_low(0, 0, b_qk)
            s_window(B - 1, 1, nxt=False)

            def head_max(b, par, h, first):
                n = H2 * b + h
                dve.wait_ge(max_ps, n + 1)
                if h == 0 and not first:
                    dve.wait_ge(mT_ps, 2 * (b - 1))
                dve.tensor_reduce(m2[par][:, h:h + 1], b_max[(h + par) % NMX][0:S, 0:SC], AX.X, ALU.max).then_inc(max_ok, 1)

            def attention(b, o=b_m[0]):
                dve.wait_ge(ot_ps, b + 1)
                ov = o[0:S, :].rearrange("p (h e) -> p h e", e=VW)
                dve.reciprocal(rden2[:], ov[:, :, DH2]).then_inc(rden2_ok, 1)
                dve.wait_ge(rden2_ok, b + 1)
                if not (isinstance(b, int) and b == 0):
                    dve.wait_ge(at_ps, b)
                dve.tensor_tensor(att[:], ov[:, :, 0:DH2],
                                  rden2[:].rearrange("p (h a) -> p h a", a=1).broadcast_to([S, H2, DH2]),
                                  ALU.mult).then_inc(att_ok, 1)

            def residual2(b, o=b_m[0]):
                dve.wait_ge(y2_ps, b + 1)
                dve.wait_ge(xres_ok, b + 1)
                dve.tensor_tensor(y2[:], o[0:S, 0:D], xres[:], ALU.add).then_inc(ln2, 1)
                stats(b, 1, ln2, y2)

            def norm2(b):
                if not (isinstance(b, int) and b == 0):
                    dve.wait_ge(x2T_ps, b)
                norm(b, 1, ln2, rstd2, y2, x2[:]).then_inc(ln2, 1)

            def shift_mix(n):
                dve.wait_ge(dx_ok, n + 1)
                if not (isinstance(n, int) and n == 0):
                    dve.wait_ge(kf_ps, n)
                for c in range(C):
                    dve.scalar_tensor_tensor(xr[:, c], dx[:, c], v(f"mur_{c}"), x2T[:, c, 0:S], ALU.mult, ALU.add)
                    last = dve.scalar_tensor_tensor(xk[:, c], dx[:, c], v(f"muk_{c}"), x2T[:, c, 0:S],
                                                    ALU.mult, ALU.add)
                last.then_inc(xrk_ok, 1)

            def sigmoid_r(n):
                dve.wait_ge(th_ok, n + 1)
                dve.tensor_scalar(sg[:], th[:], 0.5, 0.5, ALU.mult, ALU.add).then_inc(sg_ok, 1)

            def residual3(n):
                dve.wait_ge(f_ps, n + 1)
                dve.wait_ge(sg_ok, n + 1)
                dve.tensor_tensor(y3[:], b_m[0][0:S, 0:D], sg[:], ALU.mult).then_inc(rv_ok, 1)
                dve.wait_ge(rv_ok, n + 1)
                dve.tensor_tensor(y3[:], y3[:], x2[:], ALU.add).then_inc(ln3, 1)
                stats(n, 2, ln3, y3)

            def norm3(n, par):
                if not (isinstance(n, int) and n < 2):
                    dve.wait_ge(out_done[par], 16 * (n // 2))
                norm(n, 2, ln3, rstd3, y3, x3[par][:]).then_inc(ln3, 1)

            def x_window(b, par, prev=True, prev2=True, nxt=True, nxt2=True):
                fm = isinstance(b, int) and b < 2
                q = 1 - par

                def heads(*hs):
                    for h in hs:
                        head_max(b, par, h, fm)
                if prev2:
                    residual2(b - 2)
                heads(0, 1)
                if nxt:
                    q_high(b + 1, par, False)
                if prev2:
                    norm2(b - 2)
                heads(2, 3)
                if nxt:
                    k_low(b + 1, 0)
                heads(4)
                if prev2:
                    shift_mix(b - 2)
                heads(5, 6)
                if nxt:
                    k_low(b + 1, 1)
                heads(7, 8, 9)
                if prev2:
                    sigmoid_r(b - 2)
                heads(10, 11, 12)
                if prev2:
                    residual3(b - 2)
                heads(13)
                if nxt:
                    values2(b + 1, q, 0, not (isinstance(b, int) and b < 1))
                if prev:
                    attention(b - 1)
                heads(14)
                if nxt:
                    values2(b + 1, q, 1, not (isinstance(b, int) and b < 1))
                if nxt2:
                    ctx_high(b + 2, par, True)
                heads(15)
                if prev2:
                    norm3(b - 2, par)

            moments(B - 2, ln1, y1)
            ctx_high(1, 1, True)
            mean_var(B - 2, 0, ln1)
            for h in range(4):
                head_max(0, 0, h, True)
            norm1(B - 2)
            mixed(B - 1, 1)
            k_low(1, 0)
            q_high(1, 0, False)
            for h in range(4, 6):
                head_max(0, 0, h, True)
            residual1(B - 1, 1, b_d[:, D:512])
            moments(B - 1, ln1, y1)
            mean_var(B - 1, 0, ln1)
            k_low(1, 1)
            for h in range(6, 10):
                head_max(0, 0, h, True)
                if h == 6:
                    norm1(B - 1)
            for h in range(10, 14):
                head_max(0, 0, h, True)
            values2(1, 1, 0, True)
            head_max(0, 0, 14, True)
            head_max(0, 0, 15, True)
            values2(1, 1, 1, True)
            ctx_high(2, 0, True)
            x_window(1, 1, prev2=False)
            x_window(2, 0)
            x_window(3, 1)
            with dve.Fori(0, (B - 8) // 2) as i:
                for k in range(2):
                    x_window(2 * i + 4 + k, k)
            x_window(B - 4, 0)
            x_window(B - 3, 1)
            x_window(B - 2, 0, nxt2=False)
            x_window(B - 1, 1, nxt=False, nxt2=False)
            residual2(B - 2)
            norm2(B - 2)
            shift_mix(B - 2)
            attention(B - 1, b_m[1])
            sigmoid_r(B - 2)
            residual3(B - 2)
            residual2(B - 1, b_m[1])
            norm3(B - 2, 0)
            norm2(B - 1)
            shift_mix(B - 1)
            sigmoid_r(B - 1)
            residual3(B - 1)
            norm3(B - 1, 1)


def kernel(**inputs):
    import numpy as np
    import concourse.bacc as bacc
    from concourse.bass_utils import run_bass_kernel_spmd

    a = {k: np.asarray(v_) for k, v_ in inputs.items()}

    def chunks(m):
        return m.reshape(C, P, -1).transpose(1, 0, 2)

    order = np.arange(D).reshape(C, 4, 32).transpose(0, 2, 1).reshape(D)
    wkv = a["L0_xattn_Wkv"].reshape(D, D, 2)
    mats = [a["L0_attn_Wq"].T, a["L0_attn_Wk"].T, a["L0_attn_Wv"].T, a["L0_attn_Wo"].T,
            a["L0_xattn_Wq"][:, order], wkv[:, order, 0], wkv[:, :, 1], a["L0_xattn_Wout"],
            a["L0_ffn_W_r"].T, a["L0_ffn_W_k"].T, a["L0_ffn_W_v"].T]
    wpack = np.stack([chunks(m) for m in mats], axis=1)
    bkv = a["L0_xattn_bkv"].reshape(D, 2)
    cols = [a["L0_attn_bq"], a["L0_attn_bk"], a["L0_xattn_bq"][order], bkv[order, 0],
            a["L0_ffn_mu_r"], a["L0_ffn_mu_k"], a["L0_attn_bgp"], a["L0_attn_bv"]]
    vecs = np.zeros((P, NVEC), np.float32)
    for i, m in enumerate(cols):
        vecs[:, 2 * i:2 * i + 2] = m.reshape(C, P).T
    vecs[:, VEC["bd"]] = np.concatenate([a["L0_attn_bd"]] * (P // GATE))
    vecs[0:GATE, VEC["bg"]] = a["L0_attn_bg"]
    rows = np.concatenate([a["L0_attn_bo"], bkv[:, 1], a["L0_xattn_bout"]]).reshape(1, -1)
    wd = np.zeros((P, P), np.float32)
    for i in range(P // GATE):
        wd[i * GATE:(i + 1) * GATE, i * GATE:(i + 1) * GATE] = a["L0_attn_Wd"].T
    part = np.arange(P)
    consts = np.concatenate([np.eye(P), part[:, None] // DH1 == np.arange(HC1),
                             part[:, None] // (P // 2) == np.arange(2)], axis=1).astype(np.float32)
    xT = a["x"].reshape(B * S, C, P).transpose(2, 1, 0)
    ctxT = np.zeros((B, P, C, SCP), np.float32)
    ctxT[:, :, :, 0:SC] = a["ctx_1024"].reshape(B, SC, C, P).transpose(0, 3, 2, 1)
    arrays = {"x": a["x"], "xT": xT, "ctxT": ctxT, "wpack": wpack, "vecs": vecs, "rows": rows, "wd": wd,
              "wg": chunks(a["L0_attn_Wg"].T), "wgp": a["L0_attn_Wgp"].T, "consts": consts}
    nc = bacc.Bacc("TRN2", target_bir_lowering=False, num_devices=1)
    arrays = {f"in_{k}": np.ascontiguousarray(m) for k, m in arrays.items()}
    args = [nc.dram_tensor(k, m.shape, mybir.dt.from_np(m.dtype), kind="ExternalInput").ap()
            for k, m in arrays.items()]
    out = nc.dram_tensor("out_0", (B, S, D), F32, kind="ExternalOutput").ap()
    decoder_layer(nc, *args, out)
    r = run_bass_kernel_spmd(nc, [arrays], core_ids=[0])
    return r.results[0]["out_0"]
```
